# Optimizing a Trainium2 kernel written in Bass

```python
import numpy as np
import jax
import jax.numpy as jnp

def _softmax(x, axis=-1):
    return jax.nn.softmax(x, axis=axis)

def _gelu(x):
    return jax.nn.gelu(x, approximate=True)

def _silu(x):
    return jax.nn.silu(x)

def _sigmoid(x):
    return jax.nn.sigmoid(x)

def _layernorm(x, axis=-1, eps=1e-05):
    m = jnp.mean(x, axis=axis, keepdims=True)
    v = jnp.var(x, axis=axis, keepdims=True)
    return (x - m) / jnp.sqrt(v + eps)

def _scatter_add(tgt, idx, src, axis=0):
    return tgt.at[idx].add(src)

def _segment_sum(src, seg, n):
    return jax.ops.segment_sum(src, seg, n)
kernel_name = 'mk_xattn_ffn_d4_seqx_r8_0d60da'

def setup_inputs(seed: int=0):
    np.random.seed(seed)
    _w = jnp.asarray

    def _rec_inputs():
        import jax
        import jax.numpy as jnp
        _rk = jax.random.key(seed)
        x = 7.22e-05 + 1 * jax.random.normal(jax.random.fold_in(_rk, 1), (16, 56, 128), jnp.float32)
        _lenS = 56 - jax.random.randint(jax.random.fold_in(_rk, 7), (16,), 0, max(1, 56 // 4) + 1, jnp.int32)
        _lenS2 = 1500 - jax.random.randint(jax.random.fold_in(_rk, 8), (16,), 0, max(1, 1500 // 4) + 1, jnp.int32)
        _ctx_1024P = jax.random.normal(jax.random.fold_in(_rk, 11), (16, 16, 128), jnp.float32)
        _ctx_1024c = jax.random.dirichlet(jax.random.fold_in(_rk, 511), 0.3 * jnp.ones((16,), jnp.float32), (16, 1500))
        _ctx_1024t = jnp.einsum('bsk,bkd->bsd', _ctx_1024c, _ctx_1024P)
        _ctx_1024t = _ctx_1024t * jax.lax.rsqrt(jnp.mean(jnp.square(_ctx_1024t)) + 1e-12) * 0.953939
        ctx_1024 = 4.13588e-05 + 0.999923 * (_ctx_1024t + 0.3 * jax.random.normal(jax.random.fold_in(_rk, 611), (16, 1500, 128), jnp.float32))
        _validS = jnp.arange(56)[None, :] < _lenS[:, None]
        _validS2 = jnp.arange(1500)[None, :] < _lenS2[:, None]
        _causal = jnp.tril(jnp.ones((56, 56), dtype=bool))
        mask_BxS2_bf1 = jnp.ones((16, 1500), dtype=bool)
        mask_BxS2_bk0 = jnp.logical_not(jnp.broadcast_to(_validS2[:, :], (16, 1500)))
        return (x, ctx_1024, mask_BxS2_bf1, mask_BxS2_bk0)
    x, ctx_1024, mask_BxS2_bf1, mask_BxS2_bk0 = _rec_inputs()

    def _L0_xattn_setup():
        import jax, jax.numpy as jnp
        import numpy as np
        D_MODEL = 128
        N_HEADS = 16
        HEAD_DIM = D_MODEL // N_HEADS
        key = jax.random.key(seed)
        ks = jax.random.split(key, 11)
        B, Q, K = (4, 256, 256)
        s = 1.0 / np.sqrt(D_MODEL)
        inp = {'q': jax.random.normal(ks[0], (B, Q, D_MODEL), jnp.float32), 'k': jax.random.normal(ks[1], (B, K, D_MODEL), jnp.float32), 'v': jax.random.normal(ks[2], (B, K, D_MODEL), jnp.float32), 'kv_mask': jnp.ones((B, K), dtype=bool), 'Wq': jax.random.normal(ks[3], (D_MODEL, D_MODEL), jnp.float32) * s, 'bq': jnp.zeros((D_MODEL,), jnp.float32), 'Wk': jax.random.normal(ks[4], (D_MODEL, D_MODEL), jnp.float32) * s, 'bk': jnp.zeros((D_MODEL,), jnp.float32), 'Wv': jax.random.normal(ks[5], (D_MODEL, D_MODEL), jnp.float32) * s, 'bv': jnp.zeros((D_MODEL,), jnp.float32), 'Wo': jax.random.normal(ks[6], (D_MODEL, D_MODEL), jnp.float32) * s, 'bo': jnp.zeros((D_MODEL,), jnp.float32)}
        return inp
    _L0_xattn_all = _L0_xattn_setup()
    _L0_xattn_in = {k: v for k, v in _L0_xattn_all.items() if k in ('Wq', 'bq', 'Wk', 'bk', 'Wv', 'bv', 'Wo', 'bo')}
    del _L0_xattn_all

    def _L0_ffn_setup():
        import jax, jax.numpy as jnp
        import numpy as np
        QB = 127.0
        EPS = 1e-05

        def _ste(x, q):
            return x + jax.lax.stop_gradient(q - x)

        def bitlinear(x, W, b):
            w_scale = jnp.clip(jnp.mean(jnp.abs(W)), EPS, None)
            Wq = _ste(W, jnp.clip(jnp.round(W / w_scale), -1.0, 1.0) * w_scale)
            x_scale = jnp.clip(jnp.max(jnp.abs(x), axis=-1, keepdims=True), EPS, None)
            xq = _ste(x, jnp.clip(jnp.round(x * (QB / x_scale)), -QB - 1.0, QB) * (x_scale / QB))
            return jnp.einsum('bnd,hd->bnh', xq, Wq) + b
        key = jax.random.key(seed)
        k0, k1, k2 = jax.random.split(key, 3)
        B, N, D = (8, 512, 128)
        H = int(D * 4.0)
        x = jax.random.normal(k0, (B, N, D), dtype=jnp.float32)
        W1 = jax.random.normal(k1, (H, D), dtype=jnp.float32) * 0.02
        b1 = jnp.zeros((H,), dtype=jnp.float32)
        W2 = jax.random.normal(k2, (D, H), dtype=jnp.float32) * 0.02
        b2 = jnp.zeros((D,), dtype=jnp.float32)
        return {'x': x, 'W1': W1, 'b1': b1, 'W2': W2, 'b2': b2}
    _L0_ffn_all = _L0_ffn_setup()
    _L0_ffn_in = {k: v for k, v in _L0_ffn_all.items() if k in ('W1', 'b1', 'W2', 'b2')}
    del _L0_ffn_all

    def _L1_xattn_setup():
        import jax, jax.numpy as jnp
        import numpy as np
        DIM = 128
        DIM_LATENT = 128
        DIM_HEAD = 64
        INNER = max(DIM, DIM_LATENT)
        HEADS = INNER // DIM_HEAD
        SCALE = DIM_HEAD ** (-0.5)
        LN_EPS = 1e-05
        RMS_EPS = 1e-08

        def layernorm(x, g, b):
            mu = jnp.mean(x, axis=-1, keepdims=True)
            var = jnp.mean(jnp.square(x - mu), axis=-1, keepdims=True)
            return (x - mu) * jax.lax.rsqrt(var + LN_EPS) * g + b

        def rmsnorm(x, gamma):
            n = jnp.linalg.norm(x, axis=-1, keepdims=True) * x.shape[-1] ** (-0.5)
            return x / jnp.maximum(n, RMS_EPS) * gamma
        key = jax.random.key(seed)
        ks = jax.random.split(key, 8)
        b, n, nl = (8, 256, 64)
        x = jax.random.normal(ks[0], (b, n, DIM), dtype=jnp.float32)
        latents = jax.random.normal(ks[1], (b, nl, DIM_LATENT), dtype=jnp.float32)
        mask = jax.random.randint(ks[2], (b, n), 0, 2).astype(bool)
        init = lambda k, shape, fan_in: jax.random.normal(k, shape, jnp.float32) * fan_in ** (-0.5)
        return {'x': x, 'latents': latents, 'mask': mask, 'ln_x_g': jnp.ones((DIM,), jnp.float32), 'ln_x_b': jnp.zeros((DIM,), jnp.float32), 'ln_l_g': jnp.ones((DIM_LATENT,), jnp.float32), 'ln_l_b': jnp.zeros((DIM_LATENT,), jnp.float32), 'q_gamma': jnp.ones((DIM_HEAD,), jnp.float32), 'k_gamma': jnp.ones((DIM_HEAD,), jnp.float32), 'W_q': init(ks[3], (DIM_LATENT, INNER), DIM_LATENT), 'W_kv': init(ks[4], (DIM, 2 * INNER), DIM), 'W_out': init(ks[5], (INNER, DIM_LATENT), INNER), 'b_out': jnp.zeros((DIM_LATENT,), jnp.float32)}
    _L1_xattn_all = _L1_xattn_setup()
    _L1_xattn_in = {k: v for k, v in _L1_xattn_all.items() if k in ('ln_x_g', 'ln_x_b', 'ln_l_g', 'ln_l_b', 'q_gamma', 'k_gamma', 'W_q', 'W_kv', 'W_out', 'b_out')}
    del _L1_xattn_all

    def _L1_ffn_setup():
        import jax, jax.numpy as jnp
        import numpy as np
        TOP_K = 2
        key = jax.random.key(seed)
        ks = jax.random.split(key, 8)
        B, S, D, E = (2, 256, 128, 8)
        F = 4 * D
        x = jax.random.normal(ks[0], (B, S, D), dtype=jnp.float32)
        Wg = jax.random.normal(ks[1], (D, E), dtype=jnp.float32) / np.sqrt(D)
        bg = jnp.zeros((E,), dtype=jnp.float32)
        W1 = jax.random.normal(ks[2], (E, D, F), dtype=jnp.float32) / np.sqrt(D)
        b1 = jnp.zeros((E, F), dtype=jnp.float32)
        W2 = jax.random.normal(ks[3], (E, F, D), dtype=jnp.float32) / np.sqrt(F)
        b2 = jnp.zeros((E, D), dtype=jnp.float32)
        return {'x': x, 'Wg': Wg, 'bg': bg, 'W1': W1, 'b1': b1, 'W2': W2, 'b2': b2}
    _L1_ffn_all = _L1_ffn_setup()
    _L1_ffn_in = {k: v for k, v in _L1_ffn_all.items() if k in ('Wg', 'bg', 'W1', 'b1', 'W2', 'b2')}
    del _L1_ffn_all

    def _L2_xattn_setup():
        import jax, jax.numpy as jnp
        import numpy as np
        EPS = 1e-06
        NUM_HEADS = 16
        DIM_HEADS = 64

        def _ln(x, scale, bias):
            mu = jnp.mean(x, axis=-1, keepdims=True)
            var = jnp.mean(jnp.square(x - mu), axis=-1, keepdims=True)
            return (x - mu) * jax.lax.rsqrt(var + EPS) * scale + bias
        key = jax.random.key(seed)
        ks = jax.random.split(key, 8)
        b, n, m, dim, ctx_dim = (8, 512, 32, 128, 128)
        inner = NUM_HEADS * DIM_HEADS
        x = jax.random.normal(ks[0], (b, n, dim), dtype=jnp.float32)
        context = jax.random.normal(ks[1], (b, m, ctx_dim), dtype=jnp.float32)
        mask = jnp.ones((b, m), dtype=bool)
        Wq = jax.random.normal(ks[2], (dim, inner), dtype=jnp.float32) / np.sqrt(dim)
        Wkv = jax.random.normal(ks[3], (ctx_dim, 2 * inner), dtype=jnp.float32) / np.sqrt(ctx_dim)
        null_kv = jax.random.normal(ks[4], (2, DIM_HEADS), dtype=jnp.float32)
        Wo = jax.random.normal(ks[5], (inner, dim), dtype=jnp.float32) / np.sqrt(inner)
        return {'x': x, 'context': context, 'mask': mask, 'ln1_s': jnp.ones((dim,), jnp.float32), 'ln1_b': jnp.zeros((dim,), jnp.float32), 'lnc_s': jnp.ones((ctx_dim,), jnp.float32), 'lnc_b': jnp.zeros((ctx_dim,), jnp.float32), 'Wq': Wq, 'Wkv': Wkv, 'null_kv': null_kv, 'Wo': Wo, 'lno_s': jnp.ones((dim,), jnp.float32), 'lno_b': jnp.zeros((dim,), jnp.float32)}
    _L2_xattn_all = _L2_xattn_setup()
    _L2_xattn_in = {k: v for k, v in _L2_xattn_all.items() if k in ('ln1_s', 'ln1_b', 'lnc_s', 'lnc_b', 'Wq', 'Wkv', 'null_kv', 'Wo', 'lno_s', 'lno_b')}
    del _L2_xattn_all

    def _L2_ffn_setup():
        import jax, jax.numpy as jnp
        import numpy as np
        B, S, D, E, K = (4, 512, 128, 8, 2)
        H = 2 * D
        key = jax.random.key(seed)
        ks = jax.random.split(key, 7)
        scale = 0.02
        return {'x': jax.random.normal(ks[0], (B, S, D), dtype=jnp.float32), 'router_w': jax.random.normal(ks[1], (D, E), dtype=jnp.float32) * scale, 'router_b': jnp.zeros((E,), dtype=jnp.float32), 'w1': jax.random.normal(ks[2], (E, D, H), dtype=jnp.float32) * scale, 'b1': jnp.zeros((E, H), dtype=jnp.float32), 'w2': jax.random.normal(ks[3], (E, H, D), dtype=jnp.float32) * scale, 'b2': jnp.zeros((E, D), dtype=jnp.float32)}
    _L2_ffn_all = _L2_ffn_setup()
    _L2_ffn_in = {k: v for k, v in _L2_ffn_all.items() if k in ('router_w', 'router_b', 'w1', 'b1', 'w2', 'b2')}
    del _L2_ffn_all

    def _L3_xattn_setup():
        import jax, jax.numpy as jnp
        import numpy as np
        K_DIM = 128
        HEADS = 16
        key = jax.random.key(seed)
        ks = jax.random.split(key, 8)
        b, t, tc, k = (2, 256, 256, K_DIM)
        scale = 1.0 / np.sqrt(k)
        x = jax.random.normal(ks[0], (b, t, k), dtype=jnp.float32)
        context = jax.random.normal(ks[1], (b, tc, k), dtype=jnp.float32)
        Wq = jax.random.normal(ks[2], (k, k), dtype=jnp.float32) * scale
        Wk = jax.random.normal(ks[3], (k, k), dtype=jnp.float32) * scale
        Wv = jax.random.normal(ks[4], (k, k), dtype=jnp.float32) * scale
        Wo = jax.random.normal(ks[5], (k, k), dtype=jnp.float32) * scale
        bo = jax.random.normal(ks[6], (k,), dtype=jnp.float32) * 0.01
        return {'x': x, 'context': context, 'Wq': Wq, 'Wk': Wk, 'Wv': Wv, 'Wo': Wo, 'bo': bo}
    _L3_xattn_all = _L3_xattn_setup()
    _L3_xattn_in = {k: v for k, v in _L3_xattn_all.items() if k in ('Wq', 'Wk', 'Wv', 'Wo', 'bo')}
    del _L3_xattn_all

    def _L3_ffn_setup():
        import jax, jax.numpy as jnp
        import numpy as np
        EPS = 1e-06
        LN_EPS = 1e-05

        def _absmean_core(W):
            gamma = jnp.mean(jnp.abs(W)) + EPS
            Ws = W / gamma
            Wq = jnp.sign(Ws) * jnp.minimum(jnp.round(jnp.abs(Ws)), 1.0)
            return (Wq, gamma)

        @jax.custom_vjp
        def absmean(W):
            return _absmean_core(W)[0]

        def _absmean_fwd(W):
            Wq, gamma = _absmean_core(W)
            return (Wq, gamma)

        def _absmean_bwd(gamma, g):
            return (g / gamma,)
        absmean.defvjp(_absmean_fwd, _absmean_bwd)

        def layernorm(x, w, b, eps=LN_EPS):
            mu = jnp.mean(x, axis=-1, keepdims=True)
            var = jnp.mean((x - mu) ** 2, axis=-1, keepdims=True)
            return (x - mu) * jax.lax.rsqrt(var + eps) * w + b
        key = jax.random.key(seed)
        k1, k2, k3 = jax.random.split(key, 3)
        d, h = (128, 512)
        B, T = (8, 256)
        return {'x': jax.random.normal(k1, (B, T, d), jnp.float32), 'W_fc': jax.random.normal(k2, (h, d), jnp.float32), 'ln_w': jnp.ones((h,), jnp.float32), 'ln_b': jnp.zeros((h,), jnp.float32), 'W_proj': jax.random.normal(k3, (d, h), jnp.float32)}
    _L3_ffn_all = _L3_ffn_setup()
    _L3_ffn_in = {k: v for k, v in _L3_ffn_all.items() if k in ('W_fc', 'ln_w', 'ln_b', 'W_proj')}
    del _L3_ffn_all
    return {'x': x, 'ctx_1024': ctx_1024, 'mask_BxS2_bf1': mask_BxS2_bf1, 'mask_BxS2_bk0': mask_BxS2_bk0, 'L0_xattn_Wq': _L0_xattn_in['Wq'], 'L0_xattn_bq': _L0_xattn_in['bq'], 'L0_xattn_Wk': _L0_xattn_in['Wk'], 'L0_xattn_bk': _L0_xattn_in['bk'], 'L0_xattn_Wv': _L0_xattn_in['Wv'], 'L0_xattn_bv': _L0_xattn_in['bv'], 'L0_xattn_Wo': _L0_xattn_in['Wo'], 'L0_xattn_bo': _L0_xattn_in['bo'], 'L0_ffn_W1': _L0_ffn_in['W1'], 'L0_ffn_b1': _L0_ffn_in['b1'], 'L0_ffn_W2': _L0_ffn_in['W2'], 'L0_ffn_b2': _L0_ffn_in['b2'], 'L1_xattn_ln_x_g': _L1_xattn_in['ln_x_g'], 'L1_xattn_ln_x_b': _L1_xattn_in['ln_x_b'], 'L1_xattn_ln_l_g': _L1_xattn_in['ln_l_g'], 'L1_xattn_ln_l_b': _L1_xattn_in['ln_l_b'], 'L1_xattn_q_gamma': _L1_xattn_in['q_gamma'], 'L1_xattn_k_gamma': _L1_xattn_in['k_gamma'], 'L1_xattn_W_q': _L1_xattn_in['W_q'], 'L1_xattn_W_kv': _L1_xattn_in['W_kv'], 'L1_xattn_W_out': _L1_xattn_in['W_out'], 'L1_xattn_b_out': _L1_xattn_in['b_out'], 'L1_ffn_Wg': _L1_ffn_in['Wg'], 'L1_ffn_bg': _L1_ffn_in['bg'], 'L1_ffn_W1': _L1_ffn_in['W1'], 'L1_ffn_b1': _L1_ffn_in['b1'], 'L1_ffn_W2': _L1_ffn_in['W2'], 'L1_ffn_b2': _L1_ffn_in['b2'], 'L2_xattn_ln1_s': _L2_xattn_in['ln1_s'], 'L2_xattn_ln1_b': _L2_xattn_in['ln1_b'], 'L2_xattn_lnc_s': _L2_xattn_in['lnc_s'], 'L2_xattn_lnc_b': _L2_xattn_in['lnc_b'], 'L2_xattn_Wq': _L2_xattn_in['Wq'], 'L2_xattn_Wkv': _L2_xattn_in['Wkv'], 'L2_xattn_null_kv': _L2_xattn_in['null_kv'], 'L2_xattn_Wo': _L2_xattn_in['Wo'], 'L2_xattn_lno_s': _L2_xattn_in['lno_s'], 'L2_xattn_lno_b': _L2_xattn_in['lno_b'], 'L2_ffn_router_w': _L2_ffn_in['router_w'], 'L2_ffn_router_b': _L2_ffn_in['router_b'], 'L2_ffn_w1': _L2_ffn_in['w1'], 'L2_ffn_b1': _L2_ffn_in['b1'], 'L2_ffn_w2': _L2_ffn_in['w2'], 'L2_ffn_b2': _L2_ffn_in['b2'], 'L3_xattn_Wq': _L3_xattn_in['Wq'], 'L3_xattn_Wk': _L3_xattn_in['Wk'], 'L3_xattn_Wv': _L3_xattn_in['Wv'], 'L3_xattn_Wo': _L3_xattn_in['Wo'], 'L3_xattn_bo': _L3_xattn_in['bo'], 'L3_ffn_W_fc': _L3_ffn_in['W_fc'], 'L3_ffn_ln_w': _L3_ffn_in['ln_w'], 'L3_ffn_ln_b': _L3_ffn_in['ln_b'], 'L3_ffn_W_proj': _L3_ffn_in['W_proj']}

def reference(x, ctx_1024, mask_BxS2_bf1, mask_BxS2_bk0, L0_xattn_Wq, L0_xattn_bq, L0_xattn_Wk, L0_xattn_bk, L0_xattn_Wv, L0_xattn_bv, L0_xattn_Wo, L0_xattn_bo, L0_ffn_W1, L0_ffn_b1, L0_ffn_W2, L0_ffn_b2, L1_xattn_ln_x_g, L1_xattn_ln_x_b, L1_xattn_ln_l_g, L1_xattn_ln_l_b, L1_xattn_q_gamma, L1_xattn_k_gamma, L1_xattn_W_q, L1_xattn_W_kv, L1_xattn_W_out, L1_xattn_b_out, L1_ffn_Wg, L1_ffn_bg, L1_ffn_W1, L1_ffn_b1, L1_ffn_W2, L1_ffn_b2, L2_xattn_ln1_s, L2_xattn_ln1_b, L2_xattn_lnc_s, L2_xattn_lnc_b, L2_xattn_Wq, L2_xattn_Wkv, L2_xattn_null_kv, L2_xattn_Wo, L2_xattn_lno_s, L2_xattn_lno_b, L2_ffn_router_w, L2_ffn_router_b, L2_ffn_w1, L2_ffn_b1, L2_ffn_w2, L2_ffn_b2, L3_xattn_Wq, L3_xattn_Wk, L3_xattn_Wv, L3_xattn_Wo, L3_xattn_bo, L3_ffn_W_fc, L3_ffn_ln_w, L3_ffn_ln_b, L3_ffn_W_proj):
    import jax
    import jax.numpy as jnp

    def _L0_xattn_ref(q, k, v, kv_mask, Wq, bq, Wk, bk, Wv, bv, Wo, bo):
        import jax, jax.numpy as jnp
        import numpy as np
        D_MODEL = 128
        N_HEADS = 16
        HEAD_DIM = D_MODEL // N_HEADS
        B, Qlen, _ = q.shape
        Klen = k.shape[1]
        qh = (q @ Wq.T + bq).reshape(B, Qlen, N_HEADS, HEAD_DIM).transpose(0, 2, 1, 3)
        kh = (k @ Wk.T + bk).reshape(B, Klen, N_HEADS, HEAD_DIM).transpose(0, 2, 1, 3)
        vh = (v @ Wv.T + bv).reshape(B, Klen, N_HEADS, HEAD_DIM).transpose(0, 2, 1, 3)
        score = jnp.einsum('bhqd,bhkd->bhqk', qh, kh) / np.sqrt(HEAD_DIM).astype(np.float32)
        score = jnp.where(kv_mask[:, None, None, :], score, jnp.float32(-10000.0))
        attn = jax.nn.softmax(score, axis=-1)
        out = jnp.einsum('bhqk,bhkd->bhqd', attn, vh)
        out = out.transpose(0, 2, 1, 3).reshape(B, Qlen, D_MODEL)
        return out @ Wo.T + bo

    def _L0_ffn_ref(x, W1, b1, W2, b2):
        import jax, jax.numpy as jnp
        import numpy as np
        QB = 127.0
        EPS = 1e-05

        def _ste(x, q):
            return x + jax.lax.stop_gradient(q - x)

        def bitlinear(x, W, b):
            w_scale = jnp.clip(jnp.mean(jnp.abs(W)), EPS, None)
            Wq = _ste(W, jnp.clip(jnp.round(W / w_scale), -1.0, 1.0) * w_scale)
            x_scale = jnp.clip(jnp.max(jnp.abs(x), axis=-1, keepdims=True), EPS, None)
            xq = _ste(x, jnp.clip(jnp.round(x * (QB / x_scale)), -QB - 1.0, QB) * (x_scale / QB))
            return jnp.einsum('bnd,hd->bnh', xq, Wq) + b
        h = bitlinear(x, W1, b1)
        h = jax.nn.gelu(h, approximate=False)
        return bitlinear(h, W2, b2)

    def _L1_xattn_ref(x, latents, mask, ln_x_g, ln_x_b, ln_l_g, ln_l_b, q_gamma, k_gamma, W_q, W_kv, W_out, b_out):
        import jax, jax.numpy as jnp
        import numpy as np
        DIM = 128
        DIM_LATENT = 128
        DIM_HEAD = 64
        INNER = max(DIM, DIM_LATENT)
        HEADS = INNER // DIM_HEAD
        SCALE = DIM_HEAD ** (-0.5)
        LN_EPS = 1e-05
        RMS_EPS = 1e-08

        def layernorm(x, g, b):
            mu = jnp.mean(x, axis=-1, keepdims=True)
            var = jnp.mean(jnp.square(x - mu), axis=-1, keepdims=True)
            return (x - mu) * jax.lax.rsqrt(var + LN_EPS) * g + b

        def rmsnorm(x, gamma):
            n = jnp.linalg.norm(x, axis=-1, keepdims=True) * x.shape[-1] ** (-0.5)
            return x / jnp.maximum(n, RMS_EPS) * gamma
        b, n, _ = x.shape
        nl = latents.shape[1]
        xn = layernorm(x, ln_x_g, ln_x_b)
        ln = layernorm(latents, ln_l_g, ln_l_b)
        q = ln @ W_q
        kv = jnp.concatenate([xn @ W_kv, ln @ W_kv], axis=1)
        k, v = (kv[..., :INNER], kv[..., INNER:])
        to_heads = lambda t: t.reshape(t.shape[0], t.shape[1], HEADS, DIM_HEAD).transpose(0, 2, 1, 3)
        q, k, v = (to_heads(q), to_heads(k), to_heads(v))
        qn = rmsnorm(q, q_gamma) * SCALE
        kn = rmsnorm(k, k_gamma)
        sim = jnp.einsum('bhid,bhjd->bhij', qn, kn)
        full_mask = jnp.pad(mask, ((0, 0), (0, nl)), constant_values=True)
        neg = -jnp.finfo(sim.dtype).max
        sim = jnp.where(full_mask[:, None, None, :], sim, neg)
        attn = jax.nn.softmax(sim.astype(jnp.float32), axis=-1).astype(sim.dtype)
        out = jnp.einsum('bhij,bhjd->bhid', attn, v)
        out = out.transpose(0, 2, 1, 3).reshape(b, nl, INNER)
        return out @ W_out + b_out

    def _L1_ffn_ref(x, Wg, bg, W1, b1, W2, b2):
        import jax, jax.numpy as jnp
        import numpy as np
        TOP_K = 2
        B, S, D = x.shape
        T = B * S
        xf = x.reshape(T, D)
        gates = jax.nn.softmax(xf @ Wg + bg, axis=-1)
        topk_vals, topk_idx = jax.lax.top_k(gates, TOP_K)
        rows = jnp.arange(T)[:, None]
        mask = jnp.zeros_like(gates).at[rows, topk_idx].set(topk_vals)
        h = jax.nn.relu(jnp.einsum('td,edf->etf', xf, W1) + b1[:, None, :])
        y = jnp.einsum('etf,efd->etd', h, W2) + b2[:, None, :]
        out = jnp.einsum('te,etd->td', mask, y)
        return out.reshape(B, S, D)

    def _L2_xattn_ref(x, context, mask, ln1_s, ln1_b, lnc_s, lnc_b, Wq, Wkv, null_kv, Wo, lno_s, lno_b):
        import jax, jax.numpy as jnp
        import numpy as np
        EPS = 1e-06
        NUM_HEADS = 16
        DIM_HEADS = 64

        def _ln(x, scale, bias):
            mu = jnp.mean(x, axis=-1, keepdims=True)
            var = jnp.mean(jnp.square(x - mu), axis=-1, keepdims=True)
            return (x - mu) * jax.lax.rsqrt(var + EPS) * scale + bias
        b, n, _ = x.shape
        h, d = (NUM_HEADS, DIM_HEADS)
        scale = h ** (-0.5)
        xn = _ln(x, ln1_s, ln1_b)
        cn = _ln(context, lnc_s, lnc_b)
        q = xn @ Wq
        kv = cn @ Wkv
        k, v = jnp.split(kv, 2, axis=-1)

        def to_heads(t):
            return t.reshape(t.shape[0], t.shape[1], h, d).transpose(0, 2, 1, 3)
        q, k, v = (to_heads(q), to_heads(k), to_heads(v))
        nk = jnp.broadcast_to(null_kv[0], (b, h, 1, d))
        nv = jnp.broadcast_to(null_kv[1], (b, h, 1, d))
        k = jnp.concatenate((nk, k), axis=2)
        v = jnp.concatenate((nv, v), axis=2)
        sim = jnp.einsum('bhid,bhjd->bhij', q * scale, k)
        mfull = jnp.pad(mask, ((0, 0), (1, 0)), constant_values=True)[:, None, None, :]
        max_neg = -jnp.finfo(sim.dtype).max
        sim = jnp.where(mfull, sim, max_neg)
        attn = jax.nn.softmax(sim, axis=-1)
        out = jnp.einsum('bhij,bhjd->bhid', attn, v)
        out = out.transpose(0, 2, 1, 3).reshape(b, n, h * d)
        out = out @ Wo
        return _ln(out, lno_s, lno_b)

    def _L2_ffn_ref(x, router_w, router_b, w1, b1, w2, b2):
        import jax, jax.numpy as jnp
        import numpy as np
        B, S, D, E, K = (4, 512, 128, 8, 2)
        H = 2 * D
        logits = jnp.einsum('bsd,de->bse', x, router_w) + router_b
        probs = jax.nn.softmax(logits, axis=-1)
        top_p, top_i = jax.lax.top_k(probs, K)
        top_p = top_p / jnp.sum(top_p, axis=-1, keepdims=True)
        out = jnp.zeros_like(x)
        for e in range(E):
            gate = jnp.sum(top_p * (top_i == e), axis=-1)
            h = jax.nn.relu(jnp.einsum('bsd,dh->bsh', x, w1[e]) + b1[e])
            y = jnp.einsum('bsh,hd->bsd', h, w2[e]) + b2[e]
            out = out + y * gate[..., None]
        return out

    def _L3_xattn_ref(x, context, Wq, Wk, Wv, Wo, bo):
        import jax, jax.numpy as jnp
        import numpy as np
        K_DIM = 128
        HEADS = 16
        b, t, e = x.shape
        tc = context.shape[1]
        h = HEADS
        s = e // h
        q = (x @ Wq.T).reshape(b, t, h, s)
        k_ = (context @ Wk.T).reshape(b, tc, h, s)
        v = (context @ Wv.T).reshape(b, tc, h, s)
        inv4 = e ** (-0.25)
        q = q * inv4
        k_ = k_ * inv4
        dot = jnp.einsum('bthd,bchd->bhtc', q, k_)
        attn = jax.nn.softmax(dot, axis=-1)
        out = jnp.einsum('bhtc,bchd->bthd', attn, v).reshape(b, t, e)
        return out @ Wo.T + bo

    def _L3_ffn_ref(x, W_fc, ln_w, ln_b, W_proj):
        import jax, jax.numpy as jnp
        import numpy as np
        EPS = 1e-06
        LN_EPS = 1e-05

        def _absmean_core(W):
            gamma = jnp.mean(jnp.abs(W)) + EPS
            Ws = W / gamma
            Wq = jnp.sign(Ws) * jnp.minimum(jnp.round(jnp.abs(Ws)), 1.0)
            return (Wq, gamma)

        @jax.custom_vjp
        def absmean(W):
            return _absmean_core(W)[0]

        def _absmean_fwd(W):
            Wq, gamma = _absmean_core(W)
            return (Wq, gamma)

        def _absmean_bwd(gamma, g):
            return (g / gamma,)
        absmean.defvjp(_absmean_fwd, _absmean_bwd)

        def layernorm(x, w, b, eps=LN_EPS):
            mu = jnp.mean(x, axis=-1, keepdims=True)
            var = jnp.mean((x - mu) ** 2, axis=-1, keepdims=True)
            return (x - mu) * jax.lax.rsqrt(var + eps) * w + b
        h = jnp.einsum('btd,hd->bth', x, absmean(W_fc))
        h = jax.nn.gelu(h, approximate=False)
        h = layernorm(h, ln_w, ln_b)
        return jnp.einsum('bth,dh->btd', h, absmean(W_proj))
    x = x + _L0_xattn_ref(_layernorm(x, axis=-1), ctx_1024, ctx_1024, mask_BxS2_bf1, L0_xattn_Wq, L0_xattn_bq, L0_xattn_Wk, L0_xattn_bk, L0_xattn_Wv, L0_xattn_bv, L0_xattn_Wo, L0_xattn_bo)
    x = x + _L0_ffn_ref(_layernorm(x, axis=-1), L0_ffn_W1, L0_ffn_b1, L0_ffn_W2, L0_ffn_b2)
    x = x + _L1_xattn_ref(ctx_1024, _layernorm(x, axis=-1), mask_BxS2_bk0, L1_xattn_ln_x_g, L1_xattn_ln_x_b, L1_xattn_ln_l_g, L1_xattn_ln_l_b, L1_xattn_q_gamma, L1_xattn_k_gamma, L1_xattn_W_q, L1_xattn_W_kv, L1_xattn_W_out, L1_xattn_b_out)
    x = x + _L1_ffn_ref(_layernorm(x, axis=-1), L1_ffn_Wg, L1_ffn_bg, L1_ffn_W1, L1_ffn_b1, L1_ffn_W2, L1_ffn_b2)
    x = x + _L2_xattn_ref(_layernorm(x, axis=-1), ctx_1024, mask_BxS2_bf1, L2_xattn_ln1_s, L2_xattn_ln1_b, L2_xattn_lnc_s, L2_xattn_lnc_b, L2_xattn_Wq, L2_xattn_Wkv, L2_xattn_null_kv, L2_xattn_Wo, L2_xattn_lno_s, L2_xattn_lno_b)
    x = x + _L2_ffn_ref(_layernorm(x, axis=-1), L2_ffn_router_w, L2_ffn_router_b, L2_ffn_w1, L2_ffn_b1, L2_ffn_w2, L2_ffn_b2)
    x = x + _L3_xattn_ref(_layernorm(x, axis=-1), ctx_1024, L3_xattn_Wq, L3_xattn_Wk, L3_xattn_Wv, L3_xattn_Wo, L3_xattn_bo)
    x = x + _L3_ffn_ref(_layernorm(x, axis=-1), L3_ffn_W_fc, L3_ffn_ln_w, L3_ffn_ln_b, L3_ffn_W_proj)
    return x

_drawn_inputs = setup_inputs


def setup_inputs(seed=0):
    import zlib

    import numpy as np

    out = dict(_drawn_inputs(seed))
    spreads = {'L0_xattn_bq': (0.0, 0.282),
     'L0_xattn_bk': (0.0, 0.8),
     'L0_xattn_bv': (0.0, 0.1),
     'L0_xattn_bo': (0.0, 0.1),
     'L0_ffn_b1': (0.0, 0.305),
     'L0_ffn_b2': (0.0, 0.1),
     'L1_xattn_ln_x_g': (1.0, 0.2),
     'L1_xattn_ln_x_b': (0.0, 0.1),
     'L1_xattn_ln_l_g': (1.0, 0.2),
     'L1_xattn_ln_l_b': (0.0, 0.1),
     'L1_xattn_q_gamma': (1.0, 0.2),
     'L1_xattn_k_gamma': (1.0, 0.2),
     'L1_xattn_b_out': (0.0, 0.1),
     'L1_ffn_bg': (0.0, 0.1),
     'L1_ffn_b1': (0.0, 0.311),
     'L1_ffn_b2': (0.0, 0.1),
     'L2_xattn_ln1_s': (1.0, 0.2),
     'L2_xattn_ln1_b': (0.0, 0.1),
     'L2_xattn_lnc_s': (1.0, 0.2),
     'L2_xattn_lnc_b': (0.0, 0.1),
     'L2_xattn_lno_s': (1.0, 0.2),
     'L2_xattn_lno_b': (0.0, 0.1),
     'L2_ffn_router_b': (0.0, 0.1),
     'L2_ffn_b1': (0.0, 0.785),
     'L2_ffn_b2': (0.0, 0.1),
     'L3_ffn_ln_w': (1.0, 0.2),
     'L3_ffn_ln_b': (0.0, 0.1)}
    factors = {'L2_xattn_null_kv': 3.536, 'L2_ffn_w1': 2.794, 'L3_xattn_bo': 7.679}
    for name, (base, spread) in spreads.items():
        noise = np.random.default_rng([zlib.crc32(name.encode()), seed]).standard_normal(out[name].shape)
        drawn = base * np.exp(spread * noise) if base else spread * noise
        out[name] = jnp.asarray(drawn.astype(out[name].dtype))
    for name, factor in factors.items():
        out[name] = (out[name] * factor).astype(out[name].dtype)
    return out
```

```python
from collections import namedtuple
from contextlib import ExitStack

import concourse.bass as bass
from concourse import mybir
from concourse.alu_op_type import AluOpType as ALU

F32 = mybir.dt.float32
U8 = mybir.dt.uint8
BF16 = mybir.dt.bfloat16
ACT = mybir.ActivationFunctionType
AX = mybir.AxisListType

P = 128
B, Q, S2 = 16, 56, 1500
TOK = B * Q
TT = 2 * Q
NTT = TOK // TT
CH, NCH = 125, 12
HALF = 4 * TT
BANK = 512
FLT_MAX = 3.4028234663852886e38

C_ID, C_HEAD, C_PAIR, C_QSEL, C_J32, C_J2, C_TRI, C_HALF = 0, 128, 144, 146, 202, 234, 236, 300
N_CONST = 302


class Vectors:
    names = ["L0_bq", "L0_bk", "L0_bo", "L0_bv0", "L0_bv1", "L0_b2",
             "L1_xg", "L1_xb", "L1_lg", "L1_lb", "L1_qg", "L1_kg", "L1_bout",
             "L2_1s", "L2_1b", "L2_cs", "L2_cb", "L2_os", "L2_ob",
             "L3_bo", "L3_lnw", "L3_lnb", "L1_b1", "L2_b1"]
    width = {"L3_lnw": 4, "L3_lnb": 4, "L1_b1": 32, "L2_b1": 16}
    at = {}
    total = 0
    for _n in names:
        at[_n] = total
        total += width.get(_n, 1)


class Core:

    def __init__(self, ctx, nc):
        sb = lambda name, shape, dt=F32: ctx.enter_context(nc.sbuf_tensor(name, shape, dt))
        self.nc = nc
        self.xT = sb("xT", [P, TOK])
        self.xnT = sb("xnT", [P, TOK])
        self.xn = sb("xn", [TT, NTT, P])
        self.stats = sb("stats", [TT, NTT, 6])
        self.mv = sb("mv", [TT, NTT, 2])
        self.rstd = sb("rstd", [TT, NTT])
        self.ones = sb("ones", [P, P])
        self.half_neg = sb("half_neg", [P, 32])
        self.const = sb("const", [P, N_CONST])
        self.vec = sb("vec", [P, Vectors.total])
        self.ctx_mv = sb("ctx_mv", [CH, B, NCH, 2])
        self.ident = self.const[:, C_ID:C_ID + P]

    def v(self, name, k=0, rows=P):
        c = Vectors.at[name] + k
        return self.vec[0:rows, c:c + 1]


def semaphores(ctx, nc, prefix, names):
    s = namedtuple("Semaphores", names)(*(nc.alloc_semaphore(name=prefix + n) for n in names.split()))
    ctx.callback(clear_semaphores, nc, list(s))
    return s


def clear_semaphores(nc, sems):
    nc.clear_and_free_semaphores(sems)
    nc.all_engine_barrier()


class Chain:

    def __init__(self, eng, sem):
        self.eng, self.sem, self.n = eng, sem, 0

    def __call__(self, ins):
        self.n += 1
        ins.then_inc(self.sem, 1)
        self.eng.wait_ge(self.sem, self.n)


LN_SEMS = "ln_tok ln_var ln_rstd ln_norm ln_feat ln_done"


def ln_pe(pe, k, s, ps, feature_major=True, stream=None):
    nc = k.nc
    for t in range(NTT):
        last = nc.tensor.transpose(ps[0:TT, t // 4, (t % 4) * P:(t % 4 + 1) * P],
                                   (k.xT if stream is None else stream)[:, t * TT:(t + 1) * TT], k.ident)
    last.then_inc(s.ln_tok, 1)
    if not feature_major:
        return
    pe.wait_ge(s.ln_norm, 1)
    for t in range(NTT):
        last = nc.tensor.transpose(ps[:, 2 + t // 4, (t % 4) * TT:(t % 4 + 1) * TT],
                                   k.xn[:, t, :], k.ident[0:TT, 0:TT])
    last.then_inc(s.ln_feat, 1)


def ln_pool(pool, k, s, eps):
    nc = k.nc
    for n, e in enumerate(eps):
        pool.wait_ge(s.ln_var, n + 1)
        nc.gpsimd.tensor_tensor(k.rstd[:], k.mv[:, :, 1], k.half_neg[0:TT, 0:NTT],
                                ALU.pow).then_inc(s.ln_rstd, 1)


def ln_dve(dve, k, s, ps, link, eps, scale=None, bias=None, feature_major=True):
    nc = k.nc
    dve.wait_ge(s.ln_tok, 1)
    src = lambda t: ps[0:TT, t // 4, (t % 4) * P:(t % 4 + 1) * P]
    for n, e in enumerate(eps):
        for t in range(NTT):
            last = nc.vector.bn_stats(k.stats[:, t, :], src(t))
        link(last)
        for t in range(NTT):
            last = nc.vector.bn_aggr(k.mv[:, t, :], k.stats[:, t, :])
        link(last)
        nc.vector.tensor_scalar(k.mv[:, :, 1], k.mv[:, :, 1], e, None, ALU.add).then_inc(s.ln_var, 1)
        dve.wait_ge(s.ln_rstd, n + 1)
        for t in range(NTT):
            last = nc.vector.tensor_scalar(k.xn[:, t, :], src(t), k.mv[:, t, 0:1], k.rstd[:, t:t + 1],
                                           ALU.subtract, ALU.mult)
        if n < len(eps) - 1:
            link(last)
        src = lambda t: k.xn[:, t, :]
    last.then_inc(s.ln_norm, 1)
    if not feature_major:
        return
    dve.wait_ge(s.ln_feat, 1)
    for h in range(2):
        out, src2 = k.xnT[:, h * HALF:(h + 1) * HALF], ps[:, 2 + h, 0:HALF]
        if scale is None:
            last = nc.vector.tensor_copy(out, src2)
        else:
            last = nc.vector.tensor_scalar(out, src2, scale, bias, ALU.mult, ALU.add)
        last.then_inc(s.ln_done, 1)


class Slots:

    def __init__(self, prep, steps, tail, last_steps, ring=2):
        self.ring = ring
        self.prologue = prep
        self.mid = steps
        self.first = [x for x in steps if x[1] not in tail]
        self.last = [x for x in steps if x[1] not in {p[1] for p in prep}]
        self.tail = last_steps
        for a in (self.prologue, self.first):
            assert [x[3] for x in a[-ring:]] == [x[3] for x in self.mid[-ring:]]

    def of(self, kind):
        return {"prologue": self.prologue, "first": self.first, "mid": self.mid, "last": self.last,
                "tail": self.tail}[kind]

    def before(self, kind, b, eng=None):
        n = lambda xs: sum(1 for x in xs if eng is None or x[3] == eng)
        if kind == "prologue":
            return 0
        if kind == "first":
            return n(self.prologue)
        base = n(self.prologue) + n(self.first)
        if kind == "tail":
            return base + n(self.mid) * (B - 2) + n(self.last)
        return base + n(self.mid) * (b - 1)

    def number(self, kind, b, i, eng=None):
        xs = self.of(kind)
        if i >= 0:
            return self.before(kind, b, eng) + sum(1 for x in xs[:i + 1] if eng is None or x[3] == eng)
        less = self.prev(kind)[i + 1:] if i < -1 else []
        return self.before(kind, b, eng) - sum(1 for x in less if eng is None or x[3] == eng)

    def engine(self, kind, i):
        return self.of(kind)[i][3] if i >= 0 else self.prev(kind)[i][3]

    def prev(self, kind):
        return self.last if kind == "tail" else self.mid

    def bank(self, kind, b_odd, i):
        n = {"prologue": 0, "first": len(self.prologue)}.get(kind)
        if n is None:
            n = len(self.prologue) + len(self.first)
            if kind == "tail":
                n += len(self.mid) * (B - 2) + len(self.last)
            else:
                n += len(self.mid) * (b_odd + 1)
                assert len(self.mid) * 2 % self.ring == 0
        return (n + i) % self.ring

    def find(self, kind, what, num):
        for i, x in enumerate(self.of(kind)):
            if x[1:3] == (what, num):
                return i
        return None


def step_slots(plan, kind, step):
    return [(i, x[1], x[2], x[3]) for i, x in enumerate(plan.of(kind)) if x[0] == step]


def batches(eng, do):
    do(0, 0, "first")
    with eng.Fori(0, (B - 2) // 2) as i:
        do(2 * i + 1, 1, "mid")
        do(2 * i + 2, 0, "mid")
    do(B - 1, 1, "last")


NT = 8


def attention_16_small_heads(nc, k, name, src, scale, masked):
    D, A = "D", "A"
    e = D if masked else A
    prep = [(0, "K", 0, D), (1, "K", 1, e), (2, "K", 2, D)] + \
           [(t + 1, "V", t, A) for t in range(6)]
    steps = []
    for t in range(NT):
        if t == 1:
            steps.append((1, "R", 0, D))
        if t == 2:
            steps.append((2, "Y", 0, D))
        steps += [p for p in prep if p[0] == t]
        steps += [(t, "T", 3 * t + j, [A, D, A][j]) for j in range(3)]
        if t in (3, 7):
            steps.append((t, "O", t // 4, D))
    prologue = prep[:-1] + [(0, "V", 5, D)]
    plan = Slots(prologue, steps, ("R", "Y"), [(0, "R", 0, D), (0, "Y", 0, D)])

    with ExitStack() as ctx:
        sb = lambda n, shape, dt=F32: ctx.enter_context(nc.sbuf_tensor(name + n, shape, dt))
        S = ctx.enter_context(nc.psum_tensor(name + "scores", [P, 2, 3, BANK], F32))
        G = ctx.enter_context(nc.psum_tensor(name + "ring", [P, 2, BANK], F32))
        S6 = S[:].rearrange("p a b n -> p (a b) n")
        s = semaphores(ctx, nc, name, LN_SEMS + " w_loaded ctx_loaded0 ctx_loaded1 filled emptied_a emptied_d scores_ready "
                       "rowmax_ready exp_done mask_ready q_ready tail_r tail_a tail_t setup_pe setup_dve "
                       "dve_chain pool_chain carrier")
        KT = sb("keys", [P, 2, S2])
        V = sb("values", [CH, 2, NCH, 2 * P])
        Qt = sb("queries", [P, 2, 16, Q])
        CT = sb("ctxT", [P, 2, S2])
        PR = sb("probs", [TT, 2, S2])
        PT = sb("probsT", [CH, NCH, 4, TT])
        OS = sb("osum", [P, 2, 2, TT])
        ssum = sb("sums", [TT, 2, NT])
        nmax = sb("negmax", [TT, 2, NT])
        rinv = sb("rinv", [TT, NT])
        Am = sb("rinv_spread", [TT, 8, 32])
        R4 = sb("rinv_rows", [P, 2, 2, Q])
        Tm = sb("heads_out", [P, 2, 2, Q])
        qT = sb("qT", [P, TOK])
        W = sb("w", [P, 6, P])
        bout = sb("bout", [P, 1])
        if masked:
            MR = sb("mask", [P, 2, S2], U8)
            MA = sb("maskadd", [TT, 2, S2])
            SM = sb("masked", [TT, 2, S2])
        head_mask = k.const[:, C_HEAD:C_HEAD + 16]
        pair_mask = k.const[:, C_PAIR:C_PAIR + 2]
        same_query = k.const[0:TT, C_QSEL:C_QSEL + Q]
        row_half = k.const[0:TT, C_J32:C_J32 + 32]
        n_load = 2 if masked else 1
        chunks = lambda ap: ap.rearrange("p (c n) -> p c n", c=3)

        ctx_loaded = (s.ctx_loaded0, s.ctx_loaded1)

        def wait_context(eng, b, u):
            eng.wait_ge(ctx_loaded[u], 8 * n_load * (b + 2 - u))

        def filled(eng, kind, b, i):
            eng.wait_ge(s.filled, plan.number(kind, b, i))

        block = ctx.enter_context(nc.Block())

        @block.sync
        def _(sp):
            sp.dma_start(W[:], src[name + "_attn_w"]).then_inc(s.w_loaded, 16)

            def load(b, u):
                sp.dma_start(CT[:, u, :], src["ctxT"][b]).then_inc(ctx_loaded[u], 16)
                if masked:
                    sp.dma_start(MR[:, u, :], src["mask_full"][b].partition_broadcast(P)).then_inc(ctx_loaded[u], 16)

            def reload(b, u, kind, at):
                sp.wait_ge(s.filled, plan.number(kind, at, plan.find(kind, "V", 5)))
                sp.sem_inc(s.carrier, 1)
                if masked:
                    sp.wait_ge(s.emptied_d, plan.number(kind, at, plan.find(kind, "K", 2), D))
                    sp.sem_inc(s.carrier, 1)
                    sp.wait_ge(s.mask_ready, b - 1)
                sp.sem_inc(s.carrier, 1)
                load(b, u)

            load(0, 0)
            load(1, 1)
            reload(2, 0, "prologue", 0)
            reload(3, 1, "first", 0)
            with sp.Fori(1, (B - 2) // 2) as i:
                reload(2 * i + 2, 0, "mid", 2 * i - 1)
                reload(2 * i + 3, 1, "mid", 2 * i)

        @block.tensor
        def _(pe):
            pe.wait_ge(s.w_loaded, 16)
            ln_pe(pe, k, s, S6)
            pe.wait_ge(s.ln_done, 2)
            for h in range(2):
                last = nc.tensor.matmul(S[:, 0, h, 0:HALF], W[:, 0, :], k.xnT[:, h * HALF:(h + 1) * HALF],
                                        start=True, stop=True)
            if name == "L0":
                for h in range(2):
                    last = nc.tensor.matmul(S[:, 1, 0, 0:1], W[:, 4 + h, :], k.v("L0_bv%d" % h),
                                            start=h == 0, stop=h == 1)
            last.then_inc(s.setup_pe, 1)

            def scores(b, odd, t, early):
                if t == 0:
                    pe.wait_ge(s.q_ready, b + 1)
                if not early:
                    pe.wait_ge(s.rowmax_ready if masked else s.exp_done, 8 * b + t - 1)
                for c in range(3):
                    last = nc.tensor.matmul(S[0:TT, t % 2, c, 0:500],
                                            Qt[:, odd, 2 * t:2 * t + 2, :].rearrange("p h q -> p (h q)"),
                                            KT[:, odd, c * 500:(c + 1) * 500], start=True, stop=True)
                last.then_inc(s.scores_ready, 1)

            def slot(b, odd, kind, i, what, num):
                bank = plan.bank(kind, odd, i)
                if kind != "prologue" or i >= 2:
                    e = plan.engine(kind, i - 2)
                    pe.wait_ge(s.emptied_a if e == A else s.emptied_d, plan.number(kind, b, i - 2, e))
                nu = 0 if kind == "prologue" else 1 - odd
                if what == "K":
                    if num == 0:
                        wait_context(pe, 0 if kind == "prologue" else b + 1, nu)
                    last = nc.tensor.matmul(G[:, bank, 0:500], W[:, 1, :], CT[:, nu, num * 500:(num + 1) * 500],
                                            start=True, stop=True)
                elif what == "V":
                    for j in range(2):
                        c = 2 * num + j
                        last = nc.tensor.matmul(G[0:CH, bank, j * 256:(j + 1) * 256],
                                                CT[:, nu, c * CH:(c + 1) * CH],
                                                W[:, 2:4, :].rearrange("p a b -> p (a b)"), start=True, stop=True)
                elif what == "T":
                    t, j = divmod(num, 3)
                    if j == 0:
                        pe.wait_ge(s.exp_done, 8 * b + t + 1)
                    for c in range(4):
                        cc = 4 * j + c
                        last = nc.tensor.transpose(G[0:CH, bank, c * TT:(c + 1) * TT],
                                                   PR[:, t % 2, cc * CH:(cc + 1) * CH], k.ident[0:TT, 0:TT])
                elif what == "O":
                    pe.wait_ge(s.emptied_a, plan.number(kind, b, i - 1, A))
                    pe.wait_ge(s.emptied_d, plan.number(kind, b, i - 1, D))
                    for c in range(NCH):
                        for g in range(4):
                            last = nc.tensor.matmul(G[32 * g:32 * g + 32, bank, 0:TT],
                                                    V[:, odd, c, num * P + 32 * g:num * P + 32 * g + 32],
                                                    PT[:, c, g, :], start=c == 0, stop=c == NCH - 1,
                                                    tile_position=(0, 32 * g))
                elif what == "R":
                    pe.wait_ge(s.tail_a, b + 1 if kind == "tail" else b)
                    for h in range(2):
                        last = nc.tensor.matmul(G[:, bank, h * Q:(h + 1) * Q],
                                                Am[:, 4 * h:4 * h + 4, :].rearrange("p a b -> p (a b)"),
                                                same_query, start=True, stop=True)
                elif what == "Y":
                    pe.wait_ge(s.tail_t, b + 1 if kind == "tail" else b)
                    for h in range(2):
                        for j in range(2):
                            last = nc.tensor.matmul(G[:, bank, 0:Q], W[:, 4 + h, :], Tm[:, h, j, :],
                                                    start=h + j == 0, stop=h + j == 2)
                last.then_inc(s.filled, 1)

            for i, (_, what, num, e) in enumerate(plan.prologue):
                slot(0, 0, "prologue", i, what, num)

            def keys_ready(b, kind):
                at = plan.find(kind, "K", 2)
                pe.wait_ge(s.emptied_d, plan.number(kind, b, at, D))
                if not masked:
                    pe.wait_ge(s.emptied_a, plan.number(kind, b, at, A))

            def batch(b, odd, kind):
                for t in range(NT):
                    if t == 0 and kind == "first":
                        keys_ready(0, "prologue")
                        scores(b, odd, 0, True)
                    if t < NT - 1:
                        scores(b, odd, t + 1, kind == "first" and t == 0)
                    elif kind != "last":
                        keys_ready(b, kind)
                        scores(b + 1, 1 - odd, 0, False)
                    for i, what, num, e in step_slots(plan, kind, t):
                        slot(b, odd, kind, i, what, num)

            batches(pe, batch)
            for i, x in enumerate(plan.tail):
                slot(B - 1, 0, "tail", i, x[1], x[2])

        @block.gpsimd
        def _(pool):
            ln_pool(pool, k, s, [1e-5])
            pool.wait_ge(s.setup_dve, 1)

            def prep(b, u, again):
                if masked:
                    wait_context(pool, b, u)
                    if again:
                        pool.wait_ge(s.rowmax_ready, 8 * b - 8)
                    pool.sem_inc(s.carrier, 1)
                    nc.gpsimd.tensor_scalar(MA[:, u, :], MR[0:TT, u, :], -10000.0, 10000.0, ALU.mult,
                                            ALU.add).then_inc(s.mask_ready, 1)
                if again:
                    pool.wait_ge(s.scores_ready, 8 * b - 8)
                nc.gpsimd.tensor_tensor(Qt[:, u, :, :],
                                        qT[:, bass.ds(b * Q, Q)].unsqueeze(1).to_broadcast([P, 16, Q]),
                                        head_mask.unsqueeze(2).to_broadcast([P, 16, Q]), ALU.mult
                                        ).then_inc(s.q_ready, 1)

            prep(0, 0, False)
            prep(1, 1, False)
            with pool.Fori(1, B // 2) as i:
                prep(2 * i, 0, True)
                prep(2 * i + 1, 1, True)

        @block.scalar
        def _(act):
            def empty(b, odd, kind, i, what, num):
                bank = plan.bank(kind, odd, i)
                nu = 0 if kind == "prologue" else 1 - odd
                filled(act, kind, b, i)
                if what == "K":
                    ins = nc.scalar.copy(KT[:, nu, num * 500:(num + 1) * 500], G[:, bank, 0:500])
                elif what == "V":
                    ins = nc.scalar.copy(V[:, nu, 2 * num:2 * num + 2, :],
                                         G[0:CH, bank, :].rearrange("p (a b) -> p a b", a=2))
                elif what == "T":
                    t, j = divmod(num, 3)
                    ins = nc.scalar.copy(PT[:, 4 * j:4 * j + 4, t % 4, :],
                                         G[0:CH, bank, 0:HALF].rearrange("p (a b) -> p a b", a=4))
                ins.then_inc(s.emptied_a, 1)

            for i, (_, what, num, e) in enumerate(plan.prologue):
                if e == A:
                    empty(0, 0, "prologue", i, what, num)

            def exp(b, odd, t, kind):
                act.wait_ge(s.rowmax_ready, 8 * b + t + 1)
                if t >= 2:
                    act.wait_ge(s.filled, plan.number(kind, b, plan.find(kind, "T", 3 * t - 4)))
                elif kind != "first":
                    act.wait_ge(s.filled, plan.before("mid", b) - len(plan.mid) + 1 +
                                plan.find("mid", "T", 3 * t + 20))
                nc.scalar.activation(chunks(PR[:, t % 2, :]), chunks(SM[:, t % 2, :]) if masked
                                     else S[0:TT, t % 2, :, 0:500], ACT.Exp,
                                     bias=nmax[:, odd, t:t + 1], scale=-1.0,
                                     accum_out=ssum[:, odd, t:t + 1]).then_inc(s.exp_done, 1)

            def batch(b, odd, kind):
                for t in range(NT):
                    if t == 0 and kind == "first":
                        exp(b, odd, 0, kind)
                    for i, what, num, e in step_slots(plan, kind, t):
                        if e == A:
                            empty(b, odd, kind, i, what, num)
                    if t < NT - 1:
                        exp(b, odd, t + 1, kind)
                    elif kind != "last":
                        exp(b + 1, 1 - odd, 0, "mid")

            batches(act, batch)

        @block.vector
        def _(dve):
            link = Chain(dve, s.dve_chain)
            dve.wait_ge(s.w_loaded, 16)
            ln_dve(dve, k, s, S6, link, [1e-5])
            dve.wait_ge(s.setup_pe, 1)
            for h in range(2):
                o = qT[:, h * HALF:(h + 1) * HALF]
                if name == "L0":
                    nc.vector.tensor_scalar(o, S[:, 0, h, 0:HALF], k.v("L0_bq"), -scale, ALU.add, ALU.mult)
                else:
                    nc.vector.tensor_scalar(o, S[:, 0, h, 0:HALF], -scale, None, ALU.mult)
            if name == "L0":
                last = nc.vector.tensor_tensor(bout[:], S[:, 1, 0, 0:1], k.v("L0_bo"), ALU.add)
            else:
                last = nc.vector.tensor_copy(bout[:], k.v("L3_bo"))
            last.then_inc(s.setup_dve, 1)

            def rowmax(b, odd, t, early):
                dve.wait_ge(s.scores_ready, 8 * b + t + 1)
                if masked:
                    if t == 0:
                        dve.wait_ge(s.mask_ready, b + 1)
                    if not early:
                        dve.wait_ge(s.exp_done, 8 * b + t - 1)
                    dve.sem_inc(s.carrier, 1)
                    nc.vector.tensor_tensor_reduce(
                        chunks(SM[:, t % 2, :]), S[0:TT, t % 2, :, 0:500], chunks(MA[:, odd, :]),
                        1.0, FLT_MAX, ALU.add, ALU.min, nmax[:, odd, t:t + 1]).then_inc(s.rowmax_ready, 1)
                else:
                    nc.vector.tensor_reduce(nmax[:, odd, t:t + 1], S[0:TT, t % 2, :, 0:500], AX.XY,
                                            ALU.min).then_inc(s.rowmax_ready, 1)

            def empty(b, odd, kind, i, what, num):
                bank = plan.bank(kind, odd, i)
                nu = 0 if kind == "prologue" else 1 - odd
                tb = b if kind == "tail" else b - 1
                if what == "R":
                    dve.wait_ge(s.exp_done, 8 * tb + 8)
                    nc.vector.reciprocal(rinv[:], ssum[:, 1 - odd, :]).then_inc(s.tail_r, 1)
                    dve.wait_ge(s.tail_r, tb + 1)
                    nc.vector.tensor_tensor(Am[:], rinv[:].unsqueeze(2).to_broadcast([TT, 8, 32]),
                                            row_half.unsqueeze(1).to_broadcast([TT, 8, 32]),
                                            ALU.mult).then_inc(s.tail_a, 1)
                filled(dve, kind, b, i)
                if what == "K":
                    keys, ps = KT[:, nu, num * 500:(num + 1) * 500], G[:, bank, 0:500]
                    if masked:
                        if num == 0:
                            wait_context(dve, 0 if kind == "prologue" else b + 1, nu)
                        ins = nc.vector.scalar_tensor_tensor(keys, ps, k.v("L0_bk"),
                                                             MR[:, nu, num * 500:(num + 1) * 500],
                                                             ALU.add, ALU.mult)
                    else:
                        ins = nc.vector.tensor_copy(keys, ps)
                elif what == "V":
                    ins = nc.vector.tensor_copy(V[:, nu, 2 * num:2 * num + 2, :],
                                                G[0:CH, bank, :].rearrange("p (a b) -> p a b", a=2))
                elif what == "T":
                    t, j = divmod(num, 3)
                    ins = nc.vector.tensor_copy(PT[:, 4 * j:4 * j + 4, t % 4, :],
                                                G[0:CH, bank, 0:HALF].rearrange("p (a b) -> p a b", a=4))
                elif what == "O":
                    ins = nc.vector.tensor_copy(OS[:, odd, num, :], G[:, bank, 0:TT])
                elif what == "R":
                    ins = nc.vector.tensor_tensor(
                        R4[:], G[:, bank, 0:TT].rearrange("p (h q) -> p h q", h=2).unsqueeze(2).to_broadcast([P, 2, 2, Q]),
                        pair_mask.unsqueeze(1).unsqueeze(3).to_broadcast([P, 2, 2, Q]), ALU.mult)
                elif what == "Y":
                    x = k.xT[:, bass.ds(tb * Q, Q)]
                    ins = nc.vector.scalar_tensor_tensor(x, G[:, bank, 0:Q], bout[:], x, ALU.add, ALU.add)
                ins.then_inc(s.emptied_d, 1)
                if what == "R":
                    dve.wait_ge(s.emptied_d, plan.number(kind, b, i, D))
                    nc.vector.tensor_tensor(Tm[:].rearrange("p h j q -> p (h j q)"),
                                            R4[:].rearrange("p h j q -> p (h j q)"),
                                            OS[:, 1 - odd, :, :].rearrange("p h r -> p (h r)"),
                                            ALU.mult).then_inc(s.tail_t, 1)

            for i, (_, what, num, e) in enumerate(plan.prologue):
                if e == D:
                    empty(0, 0, "prologue", i, what, num)

            def batch(b, odd, kind):
                for t in range(NT):
                    if t == 0 and kind == "first":
                        rowmax(b, odd, 0, True)
                    if t < NT - 1:
                        rowmax(b, odd, t + 1, kind == "first" and t == 0)
                    elif kind != "last":
                        rowmax(b + 1, 1 - odd, 0, False)
                    for i, what, num, e in step_slots(plan, kind, t):
                        if e == D:
                            empty(b, odd, kind, i, what, num)

            batches(dve, batch)
            for i, x in enumerate(plan.tail):
                empty(B - 1, 0, "tail", i, x[1], x[2])


def latent_attention(nc, k, src):
    name, D, A = "L1", "D", "A"
    KEYS, HD = S2 + Q, 64
    KCOL = KEYS // 4
    t1 = [(0, "T1", j, [D, A, D][j]) for j in range(3)]
    kv = [(0, "KV", j, D if j in (2, 5) else A) for j in range(6)]
    t2 = [(0, "T2", j, [D, A, D][j]) for j in range(3)]
    t3 = [(0, "T3", j, [A, D, A, A, D][j]) for j in range(5)]
    tail = [(0, "R", 0, D), (0, "Y", 0, D)]
    plan = Slots(t1 + kv + t2, t1 + kv + t3 + [(0, "O", 0, D)] + tail + t2, ("R", "Y"), tail, ring=4)

    with ExitStack() as ctx:
        sb = lambda n, shape, dt=F32: ctx.enter_context(nc.sbuf_tensor(name + n, shape, dt))
        PS = ctx.enter_context(nc.psum_tensor(name + "ps", [P, 8, BANK], F32))
        G = PS[:, 4:8, :]
        s = semaphores(ctx, nc, name, LN_SEMS + " w_loaded ctx_loaded0 ctx_loaded1 mask_loaded0 mask_loaded1 filled "
                       "emptied_a emptied_d qk_filled qk_squares qk_ss qk_rms qk_scaled qk_turned lat_v lat_done "
                       "stats_ready ctx_rms xh_done mv_kept squares ss_ready k_rms k_normed kl_ready vl_ready q_ready "
                       "mask_ready scores_ready rowmax_ready exp_done tail_r tail_a tail_t dve_chain pool_chain "
                       "zeroed stats_a stats_b ss_a carrier")
        ctx_loaded = (s.ctx_loaded0, s.ctx_loaded1)
        mask_loaded = (s.mask_loaded0, s.mask_loaded1)
        W = sb("w", [P, 4, P])
        RAW = sb("raw", [CH, 2, NCH, P])
        XH = sb("xh", [CH, 2, NCH, P])
        XT = sb("xT1", [P, S2])
        KV = sb("kv", [CH, 2, NCH, 2 * P])
        SQ = sb("sq", [CH, NCH, P])
        KN = sb("kn", [CH, NCH, P])
        KT = sb("keysT", [P, 2, KEYS])
        Qd = sb("queries", [P, 2, 2, Q])
        MR = sb("mask", [TT, 2, S2], U8)
        MA = sb("maskadd", [TT, 2, KEYS])
        SM = sb("masked", [TT, KEYS])
        PR = sb("probs", [TT, KEYS])
        PT = sb("probsT", [CH, NCH + 1, TT])
        VL = sb("v_latent", [Q, 2, P])
        VLall = sb("v_latents", [Q, B, P])
        qT = sb("qT", [P, TOK])
        kT = sb("kT", [P, TOK])
        QK = sb("qk", [TT, 2, NTT, P])
        QK2 = sb("qk2", [TT, 2, NTT, P])
        ssq = sb("ssq", [TT, 32])
        rq = sb("rq", [TT, 32])
        st = sb("st", [CH, NCH, 6])
        mvb = sb("mvb", [CH, 2, NCH, 2])
        ve = sb("ve", [CH, 2, NCH])
        rs = sb("rs", [CH, NCH])
        ss = sb("ss", [CH, 24])
        rk = sb("rk", [CH, 24])
        ssum = sb("sums", [TT, 2])
        nmax = sb("negmax", [TT, 2])
        rinv = sb("rinv", [TT, 1])
        Am = sb("rinv_spread", [TT, 2, HD])
        OS = sb("osum", [P, 2, TT])
        R = sb("r", [P, Q])
        Tm = sb("heads_out", [P, Q])
        head_mask = k.const[:, C_HALF:C_HALF + 2]
        row_half = k.const[0:TT, C_J2:C_J2 + 2]
        same_query = k.const[0:TT, C_QSEL:C_QSEL + Q]
        banks = lambda ap: ap.rearrange("p (c n) -> p c n", c=4)

        def batches(eng, do):
            do(0, 0, "first", True)
            with eng.Fori(0, 6) as i:
                do(2 * i + 1, 1, "mid", True)
                do(2 * i + 2, 0, "mid", True)
            do(13, 1, "mid", True)
            do(14, 0, "mid", False)
            do(15, 1, "last", False)

        loads = lambda b, u: 8 * (b + 2 - u)

        block = ctx.enter_context(nc.Block())

        @block.sync
        def _(sp):
            sp.dma_start(W[:], src["L1_attn_w"]).then_inc(s.w_loaded, 16)

            def load(b, u):
                sp.dma_start(RAW[:, u], src["ctx"][b]).then_inc(ctx_loaded[u], 16)
                sp.dma_start(MR[:, u, :], src["mask_some"][b].partition_broadcast(TT)).then_inc(mask_loaded[u], 16)

            def reload(b, u):
                sp.wait_ge(s.xh_done, b - 1)
                sp.sem_inc(s.carrier, 1)
                sp.wait_ge(s.mask_ready, b - 1)
                sp.sem_inc(s.carrier, 1)
                load(b, u)

            load(0, 0)
            load(1, 1)
            with sp.Fori(1, B // 2) as i:
                reload(2 * i, 0)
                reload(2 * i + 1, 1)

        @block.tensor
        def _(pe):
            pe.wait_ge(s.w_loaded, 16)
            ln_pe(pe, k, s, PS)
            pe.wait_ge(s.ln_done, 2)
            for w in range(2):
                for t in range(NTT):
                    last = nc.tensor.matmul(PS[0:TT, 4 + 2 * w + t // 4, (t % 4) * P:(t % 4 + 1) * P],
                                            k.xnT[:, t * TT:(t + 1) * TT], W[:, w, :], start=True, stop=True)
                last.then_inc(s.qk_filled, 1)
            for b in range(B):
                last = nc.tensor.matmul(PS[0:Q, b // 4, (b % 4) * P:(b % 4 + 1) * P],
                                        k.xnT[:, b * Q:(b + 1) * Q], W[:, 2, :], start=True, stop=True)
            last.then_inc(s.lat_v, 1)
            pe.wait_ge(s.qk_scaled, 1)
            for w in range(2):
                for t in range(NTT):
                    last = nc.tensor.transpose(PS[:, 4 + 2 * w + t // 4, (t % 4) * TT:(t % 4 + 1) * TT],
                                               QK[:, w, t, :], k.ident[0:TT, 0:TT])
                last.then_inc(s.qk_turned, 1)
            pe.wait_ge(s.lat_done, 1)

            def slot(b, odd, kind, i, what, num):
                bank = plan.bank(kind, odd, i)
                if kind != "prologue" or i >= 4:
                    e = plan.engine(kind, i - 4)
                    pe.wait_ge(s.emptied_a if e == A else s.emptied_d, plan.number(kind, b, i - 4, e))
                nb, nu = (0, 0) if kind == "prologue" else (b + 1, 1 - odd)
                if what == "T1":
                    if num == 0:
                        pe.wait_ge(s.xh_done, nb + 1)
                    for c in range(4):
                        last = nc.tensor.transpose(G[:, bank, c * CH:(c + 1) * CH], XH[:, nu, 4 * num + c, :],
                                                   k.ident[0:CH, 0:CH])
                elif what == "KV":
                    if num == 0:
                        pe.wait_ge(s.emptied_a, plan.number(kind, b, i - 1, A))
                        pe.wait_ge(s.emptied_d, plan.number(kind, b, i - 1, D))
                    for j in range(2):
                        c = 2 * num + j
                        last = nc.tensor.matmul(G[0:CH, bank, j * 256:(j + 1) * 256], XT[:, c * CH:(c + 1) * CH],
                                                W[:, 1:3, :].rearrange("p a b -> p (a b)"), start=True, stop=True)
                elif what == "T2":
                    if num == 0:
                        pe.wait_ge(s.k_normed, nb + 1)
                    for c in range(4):
                        last = nc.tensor.transpose(G[:, bank, c * CH:(c + 1) * CH], KN[:, 4 * num + c, :],
                                                   k.ident[0:CH, 0:CH])
                elif what == "T3":
                    if num == 0:
                        pe.wait_ge(s.exp_done, b + 1)
                    if num < 4:
                        for c in range(3):
                            cc = 3 * num + c
                            last = nc.tensor.transpose(G[0:CH, bank, c * TT:(c + 1) * TT],
                                                       PR[:, cc * CH:(cc + 1) * CH], k.ident[0:TT, 0:TT])
                    else:
                        pe.sem_inc(s.carrier, 1)
                        last = nc.tensor.transpose(G[0:Q, bank, 0:TT], PR[:, S2:KEYS], k.ident[0:TT, 0:TT])
                elif what == "O":
                    pe.wait_ge(s.emptied_a, plan.number(kind, b, i - 1, A))
                    pe.wait_ge(s.emptied_d, plan.number(kind, b, i - 1, D))
                    pe.wait_ge(s.vl_ready, b + 1)
                    for c in range(NCH):
                        nc.tensor.matmul(G[:, bank, 0:TT], KV[:, odd, c, P:2 * P], PT[:, c, :],
                                         start=c == 0, stop=False)
                    last = nc.tensor.matmul(G[:, bank, 0:TT], VL[:, odd, :], PT[0:Q, NCH, :], start=False, stop=True)
                elif what == "R":
                    pe.wait_ge(s.tail_a, b + 1 if kind == "tail" else b)
                    last = nc.tensor.matmul(G[:, bank, 0:Q], Am[:].rearrange("p a b -> p (a b)"), same_query,
                                            start=True, stop=True)
                elif what == "Y":
                    pe.wait_ge(s.tail_t, b + 1 if kind == "tail" else b)
                    last = nc.tensor.matmul(G[:, bank, 0:Q], W[:, 3, :], Tm[:], start=True, stop=True)
                last.then_inc(s.filled, 1)

            for i, (_, what, num, e) in enumerate(plan.prologue):
                slot(0, 0, "prologue", i, what, num)

            def batch(b, odd, kind, ahead):
                pe.wait_ge(s.emptied_a, plan.before(kind, b, A))
                pe.wait_ge(s.emptied_d, plan.before(kind, b, D))
                pe.wait_ge(s.kl_ready, b + 1)
                pe.wait_ge(s.q_ready, b + 1)
                if kind != "first":
                    pe.wait_ge(s.rowmax_ready, b)
                for c in range(4):
                    last = nc.tensor.matmul(PS[0:TT, c, 0:KCOL], Qd[:, odd].rearrange("p h q -> p (h q)"),
                                            KT[:, odd, c * KCOL:(c + 1) * KCOL], start=True, stop=True)
                last.then_inc(s.scores_ready, 1)
                for i, what, num, e in step_slots(plan, kind, 0):
                    slot(b, odd, kind, i, what, num)

            batches(pe, batch)
            for i, x in enumerate(plan.tail):
                slot(B - 1, 0, "tail", i, x[1], x[2])

        @block.gpsimd
        def _(pool):
            ln_pool(pool, k, s, [1e-5, 1e-5])
            nc.gpsimd.memset(MA[:, :, S2:KEYS], 0.0).then_inc(s.zeroed, 1)
            pool.wait_ge(s.zeroed, 1)
            pool.wait_ge(s.qk_ss, 1)
            nc.gpsimd.tensor_tensor(rq[:], ssq[:], k.half_neg[0:TT, 0:32], ALU.pow).then_inc(s.qk_rms, 1)

            def normalise(b, u, again):
                pool.wait_ge(s.stats_ready, b + 1)
                pool.wait_ge(s.stats_ready, b + 1)
                if again:
                    pool.wait_ge(s.xh_done, b)
                nc.gpsimd.tensor_tensor(rs[:], ve[:, u, :], k.half_neg[0:CH, 0:NCH], ALU.pow).then_inc(s.pool_chain, 1)
                nc.gpsimd.tensor_copy(k.ctx_mv[:, bass.ds(b, 1)].rearrange("p a c n -> p (a c n)"),
                                      mvb[:, u].rearrange("p c n -> p (c n)"))
                nc.gpsimd.tensor_tensor(XH[:, u], RAW[:, u], mvb[:, u, :, 0:1].to_broadcast([CH, NCH, P]),
                                        ALU.subtract).then_inc(s.pool_chain, 1)
                pool.wait_ge(s.pool_chain, 2 * b + 2)
                nc.gpsimd.tensor_tensor(XH[:, u], XH[:, u], rs[:].unsqueeze(2).to_broadcast([CH, NCH, P]),
                                        ALU.mult).then_inc(s.xh_done, 1)

            def operands(b, u, again):
                if again:
                    pool.wait_ge(s.scores_ready, b - 1)
                nc.gpsimd.tensor_tensor(Qd[:, u], qT[:, bass.ds(b * Q, Q)].unsqueeze(1).to_broadcast([P, 2, Q]),
                                        head_mask.unsqueeze(2).to_broadcast([P, 2, Q]), ALU.mult).then_inc(s.q_ready, 1)
                nc.gpsimd.tensor_copy(KT[:, u, S2:KEYS], kT[:, bass.ds(b * Q, Q)]).then_inc(s.kl_ready, 1)
                pool.wait_ge(mask_loaded[u], loads(b, u))
                if again:
                    pool.wait_ge(s.rowmax_ready, b - 1)
                pool.sem_inc(s.carrier, 1)
                nc.gpsimd.tensor_scalar(MA[:, u, 0:S2], MR[:, u, :], -1.0, -FLT_MAX, ALU.add,
                                        ALU.mult).then_inc(s.mask_ready, 1)

            def key_squares(b, u, kind, at):
                i = plan.find(kind, "KV", 5)
                pool.wait_ge(s.emptied_a, plan.number(kind, at, i, A))
                pool.wait_ge(s.emptied_d, plan.number(kind, at, i, D))
                nc.gpsimd.tensor_tensor(SQ[:], KV[:, u, :, 0:P], KV[:, u, :, 0:P], ALU.mult).then_inc(s.squares, 1)
                pool.wait_ge(s.ss_ready, b + 1)
                nc.gpsimd.tensor_tensor(rk[:], ss[:], k.half_neg[0:CH, 0:24], ALU.pow).then_inc(s.k_rms, 1)

            def latent_values(b, u):
                nc.gpsimd.tensor_copy(VL[:, u, :], VLall[:, bass.ds(b, 1), :].rearrange("p a n -> p (a n)")
                                      ).then_inc(s.vl_ready, 1)

            normalise(0, 0, False)
            normalise(1, 1, True)
            pool.wait_ge(s.lat_done, 1)
            operands(0, 0, False)
            operands(1, 1, False)
            latent_values(0, 0)
            key_squares(0, 0, "prologue", 0)

            def batch(b, odd, kind, ahead):
                if kind != "last":
                    key_squares(b + 1, 1 - odd, kind, b)
                    pool.wait_ge(s.filled, plan.before(kind, b))
                    latent_values(b + 1, 1 - odd)
                if ahead:
                    operands(b + 2, odd, True)
                    normalise(b + 2, odd, True)

            batches(pool, batch)

        @block.scalar
        def _(act):
            def empty(b, odd, kind, i, what, num):
                bank = plan.bank(kind, odd, i)
                nu = 0 if kind == "prologue" else 1 - odd
                act.wait_ge(s.filled, plan.number(kind, b, i))
                if what == "T1":
                    ins = nc.scalar.activation(XT[:, num * 500:(num + 1) * 500], G[:, bank, 0:500], ACT.Identity,
                                               bias=k.v("L1_xb"), scale=k.v("L1_xg"))
                elif what == "KV":
                    ins = nc.scalar.copy(KV[:, nu, 2 * num:2 * num + 2, :],
                                         G[0:CH, bank, :].rearrange("p (a b) -> p a b", a=2))
                elif what == "T2":
                    ins = nc.scalar.mul(KT[:, nu, num * 500:(num + 1) * 500], G[:, bank, 0:500], k.v("L1_kg"))
                elif what == "T3":
                    ins = nc.scalar.copy(PT[:, 3 * num:3 * num + 3, :],
                                         G[0:CH, bank, 0:3 * TT].rearrange("p (a b) -> p a b", a=3))
                ins.then_inc(s.emptied_a, 1)

            for i, (_, what, num, e) in enumerate(plan.prologue):
                if e == A:
                    empty(0, 0, "prologue", i, what, num)

            def batch(b, odd, kind, ahead):
                for i, what, num, e in step_slots(plan, kind, 0):
                    if e == A and what in ("T1", "KV"):
                        empty(b, odd, kind, i, what, num)
                act.wait_ge(s.rowmax_ready, b + 1)
                nc.scalar.activation(PR[:], SM[:], ACT.Exp, bias=nmax[:, odd:odd + 1], scale=-1.0,
                                     accum_out=ssum[:, odd:odd + 1]).then_inc(s.exp_done, 1)
                for i, what, num, e in step_slots(plan, kind, 0):
                    if e == A and what not in ("T1", "KV"):
                        empty(b, odd, kind, i, what, num)

            batches(act, batch)

        @block.vector
        def _(dve):
            link = Chain(dve, s.dve_chain)
            ln_dve(dve, k, s, PS, link, [1e-5, 1e-5], k.v("L1_lg"), k.v("L1_lb"))
            dve.wait_ge(s.qk_filled, 2)
            link(nc.vector.tensor_copy(QK[:].rearrange("p w t n -> p (w t n)"),
                                       G[0:TT].rearrange("p a n -> p (a n)")))
            link(nc.vector.tensor_tensor(QK2[:], QK[:], QK[:], ALU.mult))
            link(nc.vector.tensor_reduce(ssq[:], QK2[:].rearrange("p w t (h d) -> p (w t h) d", h=2), AX.X, ALU.add))
            nc.vector.tensor_scalar(ssq[:], ssq[:], 1.0 / HD, 1e-16, ALU.mult, ALU.max).then_inc(s.qk_ss, 1)
            dve.wait_ge(s.lat_v, 1)
            for n in range(4):
                last = nc.vector.tensor_copy(VLall[:, 4 * n:4 * n + 4, :].rearrange("p a n -> p (a n)"), PS[0:Q, n, :])
            link(last)
            dve.wait_ge(s.qk_rms, 1)
            nc.vector.tensor_tensor(QK[:].rearrange("p w t (h d) -> p (w t h) d", h=2),
                                    QK[:].rearrange("p w t (h d) -> p (w t h) d", h=2),
                                    rq[:].unsqueeze(2).to_broadcast([TT, 32, HD]), ALU.mult).then_inc(s.qk_scaled, 1)
            dve.wait_ge(s.qk_turned, 2)
            for h in range(2):
                o = slice(h * HALF, (h + 1) * HALF)
                nc.vector.tensor_scalar(qT[:, o], PS[:, 4 + h, 0:HALF], k.v("L1_qg"), -HD ** -0.5, ALU.mult, ALU.mult)
                last = nc.vector.tensor_scalar(kT[:, o], PS[:, 6 + h, 0:HALF], k.v("L1_kg"), None, ALU.mult)
            last.then_inc(s.lat_done, 1)

            def stats(b, u, again):
                dve.wait_ge(ctx_loaded[u], loads(b, u))
                if again:
                    dve.wait_ge(s.xh_done, b - 1)
                for c in range(NCH):
                    last = nc.vector.bn_stats(st[:, c, :], RAW[:, u, c, :])
                last.then_inc(s.stats_a, 1)
                dve.wait_ge(s.stats_a, b + 1)
                dve.sem_inc(s.carrier, 1)
                for c in range(NCH):
                    last = nc.vector.bn_aggr(mvb[:, u, c, :], st[:, c, :])
                last.then_inc(s.stats_b, 1)
                dve.wait_ge(s.stats_b, b + 1)
                nc.vector.tensor_scalar(ve[:, u, :], mvb[:, u, :, 1], 1e-5, None, ALU.add).then_inc(s.stats_ready, 1)

            def empty(b, odd, kind, i, what, num):
                bank = plan.bank(kind, odd, i)
                nu = 0 if kind == "prologue" else 1 - odd
                tb = b if kind == "tail" else b - 1
                if what == "R":
                    dve.wait_ge(s.exp_done, tb + 1)
                    nc.vector.reciprocal(rinv[:], ssum[:, 1 - odd:2 - odd]).then_inc(s.tail_r, 1)
                    dve.wait_ge(s.tail_r, tb + 1)
                    nc.vector.tensor_scalar(Am[:], row_half.unsqueeze(2).to_broadcast([TT, 2, HD]), rinv[:], None,
                                            ALU.mult).then_inc(s.tail_a, 1)
                dve.wait_ge(s.filled, plan.number(kind, b, i))
                if what == "T1":
                    ins = nc.vector.tensor_scalar(XT[:, num * 500:(num + 1) * 500], G[:, bank, 0:500],
                                                  k.v("L1_xg"), k.v("L1_xb"), ALU.mult, ALU.add)
                elif what == "KV":
                    ins = nc.vector.tensor_copy(KV[:, nu, 2 * num:2 * num + 2, :],
                                                G[0:CH, bank, :].rearrange("p (a b) -> p a b", a=2))
                elif what == "T2":
                    ins = nc.vector.tensor_scalar(KT[:, nu, num * 500:(num + 1) * 500], G[:, bank, 0:500],
                                                  k.v("L1_kg"), None, ALU.mult)
                elif what == "T3" and num < 4:
                    ins = nc.vector.tensor_copy(PT[:, 3 * num:3 * num + 3, :],
                                                G[0:CH, bank, 0:3 * TT].rearrange("p (a b) -> p a b", a=3))
                elif what == "T3":
                    ins = nc.vector.tensor_copy(PT[0:Q, NCH, :], G[0:Q, bank, 0:TT])
                elif what == "O":
                    ins = nc.vector.tensor_copy(OS[:, odd, :], G[:, bank, 0:TT])
                elif what == "R":
                    ins = nc.vector.tensor_copy(R[:], G[:, bank, 0:Q])
                elif what == "Y":
                    x = k.xT[:, bass.ds(tb * Q, Q)]
                    ins = nc.vector.scalar_tensor_tensor(x, G[:, bank, 0:Q], k.v("L1_bout"), x, ALU.add, ALU.add)
                ins.then_inc(s.emptied_d, 1)
                if what == "R":
                    dve.wait_ge(s.emptied_d, plan.number(kind, b, i, D))
                    for h in range(2):
                        p = slice(h * HD, (h + 1) * HD)
                        last = nc.vector.tensor_tensor(Tm[p, :], OS[p, 1 - odd, h * Q:(h + 1) * Q], R[p, :], ALU.mult)
                    last.then_inc(s.tail_t, 1)

            def key_sums(b, u):
                dve.wait_ge(s.squares, b + 1)
                nc.vector.tensor_reduce(ss[:], SQ[:].rearrange("p c (h d) -> p (c h) d", h=2), AX.X,
                                        ALU.add).then_inc(s.ss_a, 1)
                dve.wait_ge(s.ss_a, b + 1)
                nc.vector.tensor_scalar(ss[:], ss[:], 1.0 / HD, 1e-16, ALU.mult, ALU.max).then_inc(s.ss_ready, 1)

            def key_norm(b, u):
                dve.wait_ge(s.k_rms, b + 1)
                for h in range(2):
                    last = nc.vector.tensor_tensor(KN[:, :, h * HD:(h + 1) * HD], KV[:, u, :, h * HD:(h + 1) * HD],
                                                   rk[:].rearrange("p (c h) -> p c h", h=2)[:, :, h:h + 1].to_broadcast([CH, NCH, HD]),
                                                   ALU.mult)
                last.then_inc(s.k_normed, 1)

            stats(0, 0, False)
            stats(1, 1, False)
            for i, (_, what, num, e) in enumerate(plan.prologue):
                if what == "T2" and num == 0:
                    key_sums(0, 0)
                    key_norm(0, 0)
                if e == D:
                    empty(0, 0, "prologue", i, what, num)

            def batch(b, odd, kind, ahead):
                dve.wait_ge(s.scores_ready, b + 1)
                dve.wait_ge(s.mask_ready, b + 1)
                if kind != "first":
                    dve.wait_ge(s.exp_done, b)
                dve.sem_inc(s.carrier, 1)
                nc.vector.tensor_tensor_reduce(banks(SM[:]), PS[0:TT, 0:4, 0:KCOL], banks(MA[:, odd, :]),
                                               1.0, FLT_MAX, ALU.add, ALU.min,
                                               nmax[:, odd:odd + 1]).then_inc(s.rowmax_ready, 1)
                for i, what, num, e in step_slots(plan, kind, 0):
                    if what == "T3" and num == 0 and kind != "last":
                        key_sums(b + 1, 1 - odd)
                    if what == "T2" and num == 0:
                        key_norm(b + 1, 1 - odd)
                    if e == D:
                        empty(b, odd, kind, i, what, num)
                if ahead:
                    stats(b + 2, odd, True)

            batches(dve, batch)
            for i, x in enumerate(plan.tail):
                empty(B - 1, 0, "tail", i, x[1], x[2])


def wide_heads_setup(nc, k, src, QZ, WVO, NN, NVO):
    name, H, HD = "L2s", 16, 64
    SCALE = H ** -0.5
    with ExitStack() as ctx:
        sb = lambda n, shape, dt=F32: ctx.enter_context(nc.sbuf_tensor(name + n, shape, dt))
        ps = ctx.enter_context(nc.psum_tensor(name + "ps", [P, 8, BANK], F32))
        s = semaphores(ctx, nc, name, LN_SEMS + " w_loaded n_loaded folded_filled folded_ready wn_filled wn_ready "
                       "xd_ready nn_filled nn_done nv_filled nv_ready nvo_stored q_filled q_act q_dve dve_chain")
        W = sb("w", [HD, 4, H, P])
        NKV = sb("nkv", [HD, 2])
        WQK = sb("wqk", [P, H, P])
        WN = sb("wn", [P, H])
        XD = sb("xd", [P, B, 2, Q])
        NM = sb("nm", [TT, B * 8, 2])
        NV = sb("nv", [1, H * P])
        row_half = k.const[0:TT, C_J2:C_J2 + 2]
        block = ctx.enter_context(nc.Block())

        @block.sync
        def _(sp):
            sp.dma_start(W[:], src["L2_attn_w"]).then_inc(s.w_loaded, 16)
            sp.dma_start(NKV[:], src["L2_null"]).then_inc(s.n_loaded, 16)
            sp.wait_ge(s.nv_ready, 4)
            sp.dma_start(NVO[:], NV[:].rearrange("a (t n) -> a t n", t=8)).then_inc(s.nvo_stored, 16)
            sp.wait_ge(s.nvo_stored, 16)

        @block.gpsimd
        def _(pool):
            ln_pool(pool, k, s, [1e-5, 1e-6])
            pool.wait_ge(s.ln_done, 2)
            nc.gpsimd.tensor_copy(XD[:], k.xnT[:].rearrange("p (b q) -> p b q", b=B).unsqueeze(2).to_broadcast([P, B, 2, Q])
                                  ).then_inc(s.xd_ready, 1)

        @block.tensor
        def _(pe):
            ln_pe(pe, k, s, ps)
            pe.wait_ge(s.w_loaded, 16)
            for f in range(2):
                for g in range(4):
                    n = 4 * f + g
                    if n >= 4:
                        pe.wait_ge(s.folded_ready, n - 3)
                    for h in range(4 * g, 4 * g + 4):
                        last = nc.tensor.matmul(ps[:, 4 + n % 4, (h % 4) * P:(h % 4 + 1) * P],
                                                W[:, 2 * f, h, :], W[:, 2 * f + 1, h, :], start=True, stop=True)
                    last.then_inc(s.folded_filled, 1)
            pe.wait_ge(s.n_loaded, 16)
            pe.wait_ge(s.ln_done, 2)
            for h in range(H):
                last = nc.tensor.matmul(ps[:, 0, h:h + 1], W[:, 0, h, :], NKV[:, 0:1], start=True, stop=True)
            last.then_inc(s.wn_filled, 1)
            for g in range(4):
                if g >= 2:
                    pe.wait_ge(s.nv_ready, g - 1)
                nc.tensor.matmul(ps[0:1, 2 + g % 2, :], NKV[:, 1:2], W[:, 3, 4 * g:4 * g + 4, :].rearrange("p h n -> p (h n)"),
                                 start=True, stop=True).then_inc(s.nv_filled, 1)
            pe.wait_ge(s.wn_ready, 1)
            pe.wait_ge(s.xd_ready, 1)
            for b in range(B):
                last = nc.tensor.matmul(ps[0:TT, 1, b * H:(b + 1) * H], XD[:, b].rearrange("p j q -> p (j q)"), WN[:],
                                        start=True, stop=True)
            last.then_inc(s.nn_filled, 1)
            pe.wait_ge(s.folded_ready, 8)
            for h in range(H):
                for x in range(2):
                    n = 2 * h + x
                    if n >= 4:
                        pe.wait_ge(s.q_dve if x else s.q_act, h - 1)
                    nc.tensor.matmul(ps[:, 4 + n % 4, 0:HALF], WQK[:, h, :], k.xnT[:, x * HALF:(x + 1) * HALF],
                                     start=True, stop=True).then_inc(s.q_filled, 1)

        @block.scalar
        def _(act):
            for h in range(H):
                act.wait_ge(s.q_filled, 2 * h + 1)
                nc.scalar.mul(QZ[:, 0:8, h, :], ps[:, 4 + 2 * h % 4, 0:HALF].rearrange("p (b q) -> p b q", b=8),
                              -SCALE).then_inc(s.q_act, 1)

        @block.vector
        def _(dve):
            link = Chain(dve, s.dve_chain)
            ln_dve(dve, k, s, ps, link, [1e-5, 1e-6], k.v("L2_1s"), k.v("L2_1b"))
            for n in range(8):
                dve.wait_ge(s.folded_filled, n + 1)
                to = WQK if n < 4 else WVO
                nc.vector.tensor_copy(to[:, 4 * (n % 4):4 * (n % 4) + 4, :].rearrange("p h n -> p (h n)"),
                                      ps[:, 4 + n % 4, :]).then_inc(s.folded_ready, 1)
            dve.wait_ge(s.wn_filled, 1)
            nc.vector.tensor_scalar(WN[:], ps[:, 0, 0:H], -SCALE, None, ALU.mult).then_inc(s.wn_ready, 1)
            for g in range(4):
                dve.wait_ge(s.nv_filled, g + 1)
                nc.vector.tensor_copy(NV[:, g * BANK:(g + 1) * BANK], ps[0:1, 2 + g % 2, :]).then_inc(s.nv_ready, 1)
            dve.wait_ge(s.nn_filled, 1)
            link(nc.vector.tensor_tensor(NM[:], ps[0:TT, 1, 0:B * H].rearrange("p (a j) -> p a j", j=2),
                                         row_half.unsqueeze(1).to_broadcast([TT, B * 8, 2]), ALU.mult))
            nc.vector.tensor_reduce(NN[:], NM[:], AX.X, ALU.add).then_inc(s.nn_done, 1)
            for h in range(H):
                dve.wait_ge(s.q_filled, 2 * h + 2)
                nc.vector.tensor_scalar(QZ[:, 8:16, h, :], ps[:, 4 + (2 * h + 1) % 4, 0:HALF].rearrange("p (b q) -> p b q", b=8),
                                        -SCALE, None, ALU.mult).then_inc(s.q_dve, 1)


def wide_heads(nc, k, src, QZ, NN, PN):
    name, D, A = "L2", "D", "A"
    prep = [(1, "K", 0, D), (2, "K", 1, A), (3, "K", 2, D)]
    tail = [("R", 0), ("R", 1), ("R", 2), ("R", 3), ("N", 0)]
    steps = []
    for t in range(NT):
        if t == 2:
            steps += [(2, "R", j, D) for j in range(2)]
        if t == 3:
            steps += [(3, "R", 2, D), (3, "R", 3, D)]
        if t == 4:
            steps.append((4, "N", 0, D))
        steps += [p for p in prep if p[0] == t]
        steps += [(t, "T", 3 * t + j, [A, D, A][j]) for j in range(3)]
        if t in (3, 7):
            steps.append((t, "O", t // 4, D))
    plan = Slots([(0, "K", 0, D), (0, "K", 1, A), (0, "K", 2, D)], steps, ("R", "N"),
                 [(0, w, n, D) for w, n in tail])
    with ExitStack() as ctx:
        sb = lambda n, shape, dt=F32: ctx.enter_context(nc.sbuf_tensor(name + n, shape, dt))
        S = ctx.enter_context(nc.psum_tensor(name + "scores", [P, 2, 3, BANK], F32))
        G = ctx.enter_context(nc.psum_tensor(name + "ring", [P, 2, BANK], F32))
        s = semaphores(ctx, nc, name, "ctx_loaded mask_loaded0 mask_loaded1 b_loaded filled emptied_a "
                       "emptied_d scores_ready rowmax_ready exp_done mask_ready nn_ready values_ready rs_ready "
                       "ve_ready null_shift null_exp tail_sums tail_r tail_w tail_pn diag_ready z_scaled z_done "
                       "q_ready pool_chain carrier")
        RAW = sb("raw", [CH, NCH, P])
        V = sb("values", [CH, 2, NCH, P])
        KT = sb("keys", [P, 2, S2])
        Qb = sb("queries", [P, 2, 16, Q])
        PR = sb("probs", [TT, 2, S2])
        PT = sb("probsT", [CH, NCH, 4, TT])
        MR = sb("mask", [TT, 2, S2], U8)
        MA = sb("maskadd", [TT, 2, S2])
        SM = sb("masked", [TT, 2, S2])
        OS = sb("osum", [P, 2, 2, HALF])
        cs = sb("cs", [TT, P])
        cb = sb("cb", [TT, P])
        rs = sb("rs", [CH, B, NCH])
        nneg = sb("nneg", [TT, 2, NT])
        ssum = sb("sums", [TT, 2, NT])
        nmax = sb("negmax", [TT, 2, NT])
        en = sb("en", [TT, NT])
        tot = sb("tot", [TT, NT])
        rinv = sb("rinv", [TT, NT])
        wc = sb("wc", [TT, NT])
        pn = sb("pn", [TT, NT])
        DG = sb("diag", [TT, 2, NT, TT])
        ZS = sb("zs", [P, 2, HALF])
        chunks = lambda ap: ap.rearrange("p (c n) -> p c n", c=3)
        mask_loaded = (s.mask_loaded0, s.mask_loaded1)
        loads = lambda b, u: 8 * (b + 2 - u)
        block = ctx.enter_context(nc.Block())

        @block.sync
        def _(sp):
            sp.dma_start(cs[:], src["L2_cs_row"].partition_broadcast(TT)).then_inc(s.b_loaded, 16)
            sp.dma_start(cb[:], src["L2_cb_row"].partition_broadcast(TT)).then_inc(s.b_loaded, 16)

            def load(b, u):
                sp.dma_start(MR[:, u, :], src["mask_full"][b].partition_broadcast(TT)).then_inc(mask_loaded[u], 16)

            def load_context(b):
                sp.dma_start(RAW[:], src["ctx"][b]).then_inc(s.ctx_loaded, 16)

            def reload(b, u):
                sp.wait_ge(s.values_ready, b)
                sp.sem_inc(s.carrier, 1)
                load_context(b)
                sp.wait_ge(s.mask_ready, b - 1)
                sp.sem_inc(s.carrier, 1)
                load(b, u)

            load_context(0)
            load(0, 0)
            load(1, 1)
            sp.wait_ge(s.values_ready, 1)
            load_context(1)
            with sp.Fori(1, B // 2) as i:
                reload(2 * i, 0)
                reload(2 * i + 1, 1)

        @block.tensor
        def _(pe):
            def scores(b, odd, t, early):
                if t == 0:
                    pe.wait_ge(s.q_ready, b + 1)
                if not early:
                    pe.wait_ge(s.rowmax_ready, 8 * b + t - 1)
                for c in range(3):
                    last = nc.tensor.matmul(S[0:TT, t % 2, c, 0:500],
                                            Qb[:, odd, 2 * t:2 * t + 2, :].rearrange("p h q -> p (h q)"),
                                            KT[:, odd, c * 500:(c + 1) * 500], start=True, stop=True)
                last.then_inc(s.scores_ready, 1)

            def slot(b, odd, kind, i, what, num):
                bank = plan.bank(kind, odd, i)
                if kind != "prologue" or i >= 2:
                    e = plan.engine(kind, i - 2)
                    pe.wait_ge(s.emptied_a if e == A else s.emptied_d, plan.number(kind, b, i - 2, e))
                nb, nu = (0, 0) if kind == "prologue" else (b + 1, 1 - odd)
                after = b + 1 if kind == "tail" else b
                if what == "K":
                    if num == 0:
                        pe.wait_ge(s.values_ready, nb + 1)
                    for c in range(4):
                        last = nc.tensor.transpose(G[:, bank, c * CH:(c + 1) * CH], V[:, nu, 4 * num + c, :],
                                                   k.ident[0:CH, 0:CH])
                elif what == "T":
                    t, j = divmod(num, 3)
                    if j == 0:
                        pe.wait_ge(s.exp_done, 8 * b + t + 1)
                    for c in range(4):
                        cc = 4 * j + c
                        last = nc.tensor.transpose(G[0:CH, bank, c * TT:(c + 1) * TT],
                                                   PR[:, t % 2, cc * CH:(cc + 1) * CH], k.ident[0:TT, 0:TT])
                elif what == "O":
                    pe.wait_ge(s.emptied_a, plan.number(kind, b, i - 1, A))
                    pe.wait_ge(s.emptied_d, plan.number(kind, b, i - 1, D))
                    for c in range(NCH):
                        last = nc.tensor.matmul(G[:, bank, 0:HALF], V[:, odd, c, :],
                                                PT[:, c].rearrange("p a n -> p (a n)"),
                                                start=c == 0, stop=c == NCH - 1)
                elif what == "R":
                    h, w = divmod(num, 2)
                    if num == 0:
                        pe.wait_ge(s.diag_ready, 2 * after)
                        if kind == "mid" or kind == "last" or kind == "tail":
                            pe.wait_ge(s.b_loaded, 32)
                    last = nc.tensor.matmul(G[:, bank, 0:HALF], (cb if w else cs)[:],
                                            DG[:, w, 4 * h:4 * h + 4, :].rearrange("p a n -> p (a n)"),
                                            start=True, stop=True)
                elif what == "N":
                    pe.wait_ge(s.tail_pn, after)
                    last = nc.tensor.transpose(G[0:NT, bank, 0:TT], pn[:], k.ident[0:TT, 0:TT])
                last.then_inc(s.filled, 1)

            for i, (_, what, num, e) in enumerate(plan.prologue):
                slot(0, 0, "prologue", i, what, num)

            def keys_ready(b, kind):
                at = plan.find(kind, "K", 2)
                pe.wait_ge(s.emptied_d, plan.number(kind, b, at, D))
                pe.wait_ge(s.emptied_a, plan.number(kind, b, at, A))

            def batch(b, odd, kind):
                for t in range(NT):
                    if t == 0 and kind == "first":
                        keys_ready(0, "prologue")
                        scores(b, odd, 0, True)
                    if t < NT - 1:
                        scores(b, odd, t + 1, kind == "first" and t == 0)
                    elif kind != "last":
                        keys_ready(b, kind)
                        scores(b + 1, 1 - odd, 0, False)
                    for i, what, num, e in step_slots(plan, kind, t):
                        slot(b, odd, kind, i, what, num)

            batches(pe, batch)
            for i, x in enumerate(plan.tail):
                slot(B - 1, 0, "tail", i, x[1], x[2])

        @block.gpsimd
        def _(pool):
            pool.wait_ge(s.ve_ready, 1)
            for b in range(0, B, 2):
                last = nc.gpsimd.tensor_tensor(rs[:, b:b + 2, :].rearrange("p b c -> p (b c)"),
                                               rs[:, b:b + 2, :].rearrange("p b c -> p (b c)"),
                                               k.half_neg[0:CH, 0:24], ALU.pow)
            last.then_inc(s.rs_ready, 1)
            pool.wait_ge(s.rs_ready, 1)

            def values(b, u):
                pool.wait_ge(s.ctx_loaded, 16 * b + 16)
                nc.gpsimd.tensor_tensor(V[:, u], RAW[:],
                                        k.ctx_mv[:, bass.ds(b, 1), :, 0:1].rearrange("p a c n -> p (a c) n").to_broadcast([CH, NCH, P]),
                                        ALU.subtract).then_inc(s.pool_chain, 1)
                pool.wait_ge(s.pool_chain, b + 1)
                nc.gpsimd.tensor_tensor(V[:, u], V[:, u],
                                        rs[:, bass.ds(b, 1), :].rearrange("p a c -> p (a c)").unsqueeze(2).to_broadcast([CH, NCH, P]),
                                        ALU.mult).then_inc(s.values_ready, 1)

            def rows(b, u, again):
                if again:
                    pool.wait_ge(s.scores_ready, 8 * b - 8)
                nc.gpsimd.tensor_copy(Qb[:, u], QZ[:, bass.ds(b, 1)].rearrange("p a h q -> p (a h) q")).then_inc(s.q_ready, 1)
                if again:
                    pool.wait_ge(s.null_shift, b - 1)
                nc.gpsimd.tensor_copy(nneg[:, u, :], NN[:, bass.ds(b * NT, NT)]).then_inc(s.nn_ready, 1)
                pool.wait_ge(mask_loaded[u], loads(b, u))
                if again:
                    pool.wait_ge(s.rowmax_ready, 8 * b - 8)
                pool.sem_inc(s.carrier, 1)
                nc.gpsimd.tensor_scalar(MA[:, u, :], MR[:, u, :], -1.0, -FLT_MAX, ALU.add,
                                        ALU.mult).then_inc(s.mask_ready, 1)

            def diagonals(tb, again):
                pool.wait_ge(s.tail_w, tb + 1)
                if again:
                    pool.wait_ge(s.z_done, 2 * tb)
                for w, x in enumerate((rinv, wc)):
                    nc.gpsimd.tensor_tensor(DG[:, w], k.ident[0:TT, 0:TT].unsqueeze(1).to_broadcast([TT, NT, TT]),
                                            x[:].unsqueeze(2).to_broadcast([TT, NT, TT]), ALU.mult).then_inc(s.diag_ready, 1)

            values(0, 0)
            rows(0, 0, False)
            rows(1, 1, False)

            def batch(b, odd, kind):
                if kind != "last":
                    pool.wait_ge(s.filled, plan.before(kind, b))
                    values(b + 1, 1 - odd)
                if kind != "first":
                    diagonals(b - 1, not (isinstance(b, int) and b == 1))
                if kind != "last":
                    if not (isinstance(b, int) and b >= 14):
                        rows(b + 2, odd, True)

            batch(0, 0, "first")
            batch(1, 1, "mid")
            batch(2, 0, "mid")
            with pool.Fori(1, 6) as i:
                batch(2 * i + 1, 1, "mid")
                batch(2 * i + 2, 0, "mid")
            batch(13, 1, "mid")
            batch(14, 0, "mid")
            batch(15, 1, "last")
            diagonals(15, True)

        @block.scalar
        def _(act):
            def empty(b, odd, kind, i, what, num):
                bank = plan.bank(kind, odd, i)
                nu = 0 if kind == "prologue" else 1 - odd
                act.wait_ge(s.filled, plan.number(kind, b, i))
                if what == "K":
                    ins = nc.scalar.activation(KT[:, nu, num * 500:(num + 1) * 500], G[:, bank, 0:500], ACT.Identity,
                                               bias=k.v("L2_cb"), scale=k.v("L2_cs"))
                elif what == "T":
                    t, j = divmod(num, 3)
                    ins = nc.scalar.copy(PT[:, 4 * j:4 * j + 4, t % 4, :],
                                         G[0:CH, bank, 0:HALF].rearrange("p (a b) -> p a b", a=4))
                ins.then_inc(s.emptied_a, 1)

            for i, (_, what, num, e) in enumerate(plan.prologue):
                if e == A:
                    empty(0, 0, "prologue", i, what, num)

            def exp(b, odd, t, kind):
                act.wait_ge(s.rowmax_ready, 8 * b + t + 1)
                if t >= 2:
                    act.wait_ge(s.filled, plan.number(kind, b, plan.find(kind, "T", 3 * t - 4)))
                elif kind != "first":
                    act.wait_ge(s.filled, plan.before("mid", b) - len(plan.mid) + 1 +
                                plan.find("mid", "T", 3 * t + 20))
                nc.scalar.activation(PR[:, t % 2, :], SM[:, t % 2, :], ACT.Exp,
                                     bias=nmax[:, odd, t:t + 1], scale=-1.0,
                                     accum_out=ssum[:, odd, t:t + 1]).then_inc(s.exp_done, 1)

            def null_exp(tb):
                act.wait_ge(s.null_shift, tb + 1)
                if not (isinstance(tb, int) and tb == 0):
                    act.wait_ge(s.tail_pn, tb)
                nc.scalar.activation(en[:], tot[:], ACT.Exp, scale=-1.0).then_inc(s.null_exp, 1)

            def batch(b, odd, kind):
                for t in range(NT):
                    if t == 0 and kind == "first":
                        exp(b, odd, 0, kind)
                    if t == 1 and kind != "first":
                        null_exp(b - 1)
                    for i, what, num, e in step_slots(plan, kind, t):
                        if e == A:
                            empty(b, odd, kind, i, what, num)
                    if t < NT - 1:
                        exp(b, odd, t + 1, kind)
                    elif kind != "last":
                        exp(b + 1, 1 - odd, 0, "mid")

            batches(act, batch)
            null_exp(15)

        @block.vector
        def _(dve):
            nc.vector.tensor_scalar(rs[:], k.ctx_mv[:, :, :, 1], 1e-6, None, ALU.add).then_inc(s.ve_ready, 1)

            def rowmax(b, odd, t, early):
                dve.wait_ge(s.scores_ready, 8 * b + t + 1)
                if t == 0:
                    dve.wait_ge(s.mask_ready, b + 1)
                    dve.wait_ge(s.nn_ready, b + 1)
                if not early:
                    dve.wait_ge(s.exp_done, 8 * b + t - 1)
                dve.sem_inc(s.carrier, 1)
                nc.vector.tensor_tensor_reduce(
                    chunks(SM[:, t % 2, :]), S[0:TT, t % 2, :, 0:500], chunks(MA[:, odd, :]),
                    1.0, nneg[:, odd, t:t + 1], ALU.add, ALU.min, nmax[:, odd, t:t + 1]).then_inc(s.rowmax_ready, 1)

            def tail_start(tb, odd):
                if not (isinstance(tb, int) and tb == 0):
                    dve.wait_ge(s.tail_pn, tb)
                nc.vector.tensor_tensor(tot[:], nneg[:, odd, :], nmax[:, odd, :], ALU.subtract).then_inc(s.null_shift, 1)

            def tail_sums(tb, odd):
                dve.wait_ge(s.null_exp, tb + 1)
                dve.wait_ge(s.exp_done, 8 * tb + 8)
                if not (isinstance(tb, int) and tb == 0):
                    dve.wait_ge(s.diag_ready, 2 * tb)
                nc.vector.tensor_tensor(tot[:], ssum[:, odd, :], en[:], ALU.add).then_inc(s.tail_sums, 1)
                dve.wait_ge(s.tail_sums, tb + 1)
                nc.vector.reciprocal(rinv[:], tot[:]).then_inc(s.tail_r, 1)
                dve.wait_ge(s.tail_r, tb + 1)
                nc.vector.tensor_tensor(wc[:], ssum[:, odd, :], rinv[:], ALU.mult).then_inc(s.tail_w, 1)
                nc.vector.tensor_tensor(pn[:], en[:], rinv[:], ALU.mult).then_inc(s.tail_pn, 1)

            def empty(b, odd, kind, i, what, num):
                bank = plan.bank(kind, odd, i)
                nu = 0 if kind == "prologue" else 1 - odd
                tb = b if kind == "tail" else b - 1
                dve.wait_ge(s.filled, plan.number(kind, b, i))
                if what == "K":
                    ins = nc.vector.tensor_scalar(KT[:, nu, num * 500:(num + 1) * 500], G[:, bank, 0:500],
                                                  k.v("L2_cs"), k.v("L2_cb"), ALU.mult, ALU.add)
                elif what == "T":
                    t, j = divmod(num, 3)
                    ins = nc.vector.tensor_copy(PT[:, 4 * j:4 * j + 4, t % 4, :],
                                                G[0:CH, bank, 0:HALF].rearrange("p (a b) -> p a b", a=4))
                elif what == "O":
                    ins = nc.vector.tensor_copy(OS[:, odd, num, :], G[:, bank, 0:HALF])
                elif what == "R":
                    h, w = divmod(num, 2)
                    if w == 0:
                        ins = nc.vector.tensor_tensor(ZS[:, h, :], OS[:, 1 - odd, h, :], G[:, bank, 0:HALF], ALU.mult)
                    else:
                        dve.wait_ge(s.emptied_d, plan.number(kind, b, i - 1, D))
                        z = QZ[:, bass.ds(tb, 1), 8 * h:8 * h + 8, :].rearrange("p a h q -> p (a h q)")
                        ins = nc.vector.tensor_tensor(z, ZS[:, h, :], G[:, bank, 0:HALF], ALU.add)
                elif what == "N":
                    ins = nc.vector.tensor_copy(PN[:, bass.ds(tb, 1), :].rearrange("p a n -> p (a n)"),
                                                G[0:NT, bank, 0:TT])
                ins.then_inc(s.emptied_d, 1)
                if what == "R" and num in (1, 3):
                    dve.sem_inc(s.z_done, 1)

            for i, (_, what, num, e) in enumerate(plan.prologue):
                if e == D:
                    empty(0, 0, "prologue", i, what, num)

            def batch(b, odd, kind):
                for t in range(NT):
                    if t == 0 and kind == "first":
                        rowmax(b, odd, 0, True)
                    if t == 0 and kind != "first":
                        tail_start(b - 1, 1 - odd)
                    if t < NT - 1:
                        rowmax(b, odd, t + 1, kind == "first" and t == 0)
                    elif kind != "last":
                        rowmax(b + 1, 1 - odd, 0, False)
                    if t == 1 and kind != "first":
                        tail_sums(b - 1, 1 - odd)
                    for i, what, num, e in step_slots(plan, kind, t):
                        if e == D:
                            empty(b, odd, kind, i, what, num)

            batches(dve, batch)
            tail_start(15, 1)
            tail_sums(15, 1)
            for i, x in enumerate(plan.tail):
                empty(B - 1, 0, "tail", i, x[1], x[2])


def wide_heads_output(nc, k, src, QZ, WVO, PN, NVO):
    name, H = "L2o", 16
    with ExitStack() as ctx:
        sb = lambda n, shape, dt=F32: ctx.enter_context(nc.sbuf_tensor(name + n, shape, dt))
        ps = ctx.enter_context(nc.psum_tensor(name + "ps", [P, 8, BANK], F32))
        s = semaphores(ctx, nc, name, LN_SEMS + " out_filled out_ready dve_chain")
        OUT = sb("out", [P, TOK])
        block = ctx.enter_context(nc.Block())

        @block.gpsimd
        def _(pool):
            ln_pool(pool, k, s, [1e-6])

        @block.tensor
        def _(pe):
            for x in range(2):
                for h in range(H):
                    nc.tensor.matmul(ps[:, 4 + x, 0:HALF], WVO[:, h, :], QZ[:, 8 * x:8 * x + 8, h, :],
                                     start=h == 0, stop=False)
                for j in range(2):
                    last = nc.tensor.matmul(ps[:, 4 + x, 0:HALF], NVO[:, j * P:(j + 1) * P],
                                            PN[:, 8 * x:8 * x + 8, j * Q:(j + 1) * Q], start=False, stop=j == 1)
                last.then_inc(s.out_filled, 1)
            pe.wait_ge(s.out_ready, 2)
            ln_pe(pe, k, s, ps, stream=OUT)

        @block.vector
        def _(dve):
            link = Chain(dve, s.dve_chain)
            for x in range(2):
                dve.wait_ge(s.out_filled, x + 1)
                nc.vector.tensor_copy(OUT[:, x * HALF:(x + 1) * HALF], ps[:, 4 + x, 0:HALF]).then_inc(s.out_ready, 1)
            ln_dve(dve, k, s, ps, link, [1e-6], k.v("L2_os"), k.v("L2_ob"))
            dve.wait_ge(s.ln_done, 2)
            nc.vector.tensor_tensor(k.xT[:], k.xT[:], k.xnT[:], ALU.add)


def attention_16_wide_heads(nc, k, src):
    with ExitStack() as ctx:
        sb = lambda n, shape, dt=F32: ctx.enter_context(nc.sbuf_tensor("L2x" + n, shape, dt))
        QZ = sb("qz", [P, B, 16, Q])
        WVO = sb("wvo", [P, 16, P])
        NN = sb("nn", [TT, B * NT])
        NVO = sb("nvo", [NT, 2 * P])
        PN = sb("pn", [NT, B, TT])
        wide_heads_setup(nc, k, src, QZ, WVO, NN, NVO)
        wide_heads(nc, k, src, QZ, NN, PN)
        wide_heads_output(nc, k, src, QZ, WVO, PN, NVO)


MAGIC = 1.5 * 2.0 ** 23


def abs_sums(nc, out, w):
    return nc.vector.tensor_reduce(out, w, AX.X, ALU.add, apply_absolute_value=True)


def ternary(nc, link, out, w, inverse_scale):
    link(nc.vector.tensor_scalar(w, w, inverse_scale, MAGIC, ALU.mult, ALU.add))
    link(nc.vector.tensor_scalar(w, w, MAGIC, -1.0, ALU.subtract, ALU.max))
    return nc.vector.tensor_scalar(out, w, 1.0, None, ALU.min)


def bitlinear_ffn(nc, k, src):
    F, NF = 512, 4
    name = "L0f"
    with ExitStack() as ctx:
        sb = lambda n, shape, dt=F32: ctx.enter_context(nc.sbuf_tensor(name + n, shape, dt))
        ps = ctx.enter_context(nc.psum_tensor(name + "ps", [P, 8, BANK], F32))
        s = semaphores(ctx, nc, name, LN_SEMS + " w_loaded b_loaded sums_ready sums_total xq_ready xq_turned xqT_ready "
                       "h_ready pre_ready gelu_done gq_ready gq_turned gqT_ready y_ready y_scaled y_turned "
                       "dve_chain")
        W = sb("w", [P, 2, F])
        Wq = sb("wq", [P, 2, F], BF16)
        b1 = sb("b1", [TT, F])
        wsum = sb("wsum", [P, 2])
        ws = sb("ws", [P, 2])
        rws = sb("rws", [P, 2])
        xs = sb("xs", [TT, 2, NTT])
        rxs = sb("rxs", [TT, 2, NTT])
        so = sb("so", [TT, 2, NTT])
        xqT = sb("xqT", [P, TOK], BF16)
        H = sb("h", [TT, 2, F])
        Gl = sb("gelu", [TT, 2, F])
        GqT = sb("gqT", [P, 2, NF, TT], BF16)
        Y = sb("y", [TT, NTT, P])
        block = ctx.enter_context(nc.Block())

        @block.sync
        def _(sp):
            sp.dma_start(W[:], src["L0_ffn_w"]).then_inc(s.w_loaded, 16)
            sp.dma_start(b1[:], src["L0_ffn_b1"].partition_broadcast(TT)).then_inc(s.b_loaded, 16)

        @block.gpsimd
        def _(pool):
            ln_pool(pool, k, s, [1e-5])

        @block.tensor
        def _(pe):
            ln_pe(pe, k, s, ps, feature_major=False)
            pe.wait_ge(s.sums_ready, 1)
            nc.tensor.matmul(ps[:, 7, 0:2], k.ones[:], wsum[:], start=True, stop=True).then_inc(s.sums_total, 1)
            pe.wait_ge(s.xq_ready, 1)
            for t in range(NTT):
                last = nc.tensor.transpose(ps[:, 2 + t // 4, (t % 4) * TT:(t % 4 + 1) * TT],
                                           k.xn[:, t, :], k.ident[0:TT, 0:TT])
            last.then_inc(s.xq_turned, 1)
            pe.wait_ge(s.xqT_ready, 2)

            def up(t):
                if t >= 2:
                    pe.wait_ge(s.pre_ready, t - 1)
                nc.tensor.matmul(ps[0:TT, 4 + t % 2, :], xqT[:, t * TT:(t + 1) * TT], Wq[:, 0, :],
                                 start=True, stop=True).then_inc(s.h_ready, 1)

            def turn(t):
                pe.wait_ge(s.gq_ready, t + 1)
                if t >= 2:
                    pe.wait_ge(s.gqT_ready, t - 1)
                for c in range(NF):
                    last = nc.tensor.transpose(ps[:, 6 + t % 2, c * TT:(c + 1) * TT],
                                               Gl[:, t % 2, c * P:(c + 1) * P], k.ident[0:TT, 0:TT])
                last.then_inc(s.gq_turned, 1)

            def down(t):
                pe.wait_ge(s.gqT_ready, t + 1)
                for c in range(NF):
                    last = nc.tensor.matmul(ps[0:TT, t // 4, (t % 4) * P:(t % 4 + 1) * P], GqT[:, t % 2, c, :],
                                            Wq[:, 1, c * P:(c + 1) * P], start=c == 0, stop=c == NF - 1)
                last.then_inc(s.y_ready, 1)

            up(0)
            up(1)
            for t in range(NTT):
                turn(t)
                if t + 2 < NTT:
                    up(t + 2)
                down(t)
            pe.wait_ge(s.y_scaled, 2)
            for t in range(NTT):
                last = nc.tensor.transpose(ps[:, 2 + t // 4, (t % 4) * TT:(t % 4 + 1) * TT],
                                           Y[:, t, :], k.ident[0:TT, 0:TT])
            last.then_inc(s.y_turned, 1)

        @block.scalar
        def _(act):
            for t in range(NTT):
                act.wait_ge(s.pre_ready, t + 1)
                if t >= 2:
                    act.wait_ge(s.gq_turned, t - 1)
                nc.scalar.activation(Gl[:, t % 2, :], H[:, t % 2, :], ACT.Gelu).then_inc(s.gelu_done, 1)

        @block.vector
        def _(dve):
            link = Chain(dve, s.dve_chain)
            dve.wait_ge(s.w_loaded, 16)
            abs_sums(nc, wsum[:, 0:1], W[:, 0, :])
            abs_sums(nc, wsum[:, 1:2], W[:, 1, :]).then_inc(s.sums_ready, 1)
            ln_dve(dve, k, s, ps, link, [1e-5], feature_major=False)
            dve.wait_ge(s.ln_norm, 1)
            link(nc.vector.tensor_reduce(xs[:, 0, :], k.xn[:], AX.X, ALU.max, apply_absolute_value=True))
            link(nc.vector.tensor_scalar(xs[:, 0, :], xs[:, 0, :], 1e-5, None, ALU.max))
            link(nc.vector.reciprocal(rxs[:, 0, :], xs[:, 0, :]))
            link(nc.vector.tensor_scalar(rxs[:, 0, :], rxs[:, 0, :], 127.0, None, ALU.mult))
            for t in range(NTT):
                last = nc.vector.tensor_scalar(k.xn[:, t, :], k.xn[:, t, :], rxs[:, 0, t:t + 1], MAGIC,
                                               ALU.mult, ALU.add)
            link(last)
            nc.vector.tensor_scalar(k.xn[:], k.xn[:], MAGIC, -128.0, ALU.subtract, ALU.max).then_inc(s.xq_ready, 1)
            dve.wait_ge(s.sums_total, 1)
            for n in range(2):
                last = nc.vector.tensor_scalar(ws[:, n:n + 1], ps[:, 7, n:n + 1], 1.0 / (F * P), 1e-5,
                                               ALU.mult, ALU.max)
            link(last)
            link(nc.vector.reciprocal(rws[:], ws[:]))
            for n in range(2):
                link(ternary(nc, link, Wq[:, n, :], W[:, n, :], rws[:, n:n + 1]))
            link(nc.vector.tensor_scalar(so[:, 0, :], xs[:, 0, :], ws[0:TT, 0:1], 1.0 / 127, ALU.mult, ALU.mult))
            dve.wait_ge(s.xq_turned, 1)
            for h in range(2):
                nc.vector.tensor_scalar(xqT[:, h * HALF:(h + 1) * HALF], ps[:, 2 + h, 0:HALF], 127.0, None,
                                        ALU.min).then_inc(s.xqT_ready, 1)
            dve.wait_ge(s.b_loaded, 16)

            def pre(t):
                dve.wait_ge(s.h_ready, t + 1)
                if t >= 2:
                    dve.wait_ge(s.gelu_done, t - 1)
                nc.vector.scalar_tensor_tensor(H[:, t % 2, :], ps[0:TT, 4 + t % 2, :], so[:, 0, t:t + 1], b1[:],
                                               ALU.mult, ALU.add).then_inc(s.pre_ready, 1)

            pre(0)
            for t in range(NTT):
                if t + 1 < NTT:
                    pre(t + 1)
                g, u = Gl[:, t % 2, :], slice(t, t + 1)
                dve.wait_ge(s.gelu_done, t + 1)
                link(nc.vector.tensor_reduce(xs[:, 1, u], g, AX.X, ALU.max, apply_absolute_value=True))
                link(nc.vector.tensor_scalar(xs[:, 1, u], xs[:, 1, u], 1e-5, None, ALU.max))
                link(nc.vector.reciprocal(rxs[:, 1, u], xs[:, 1, u]))
                nc.vector.tensor_scalar(so[:, 1, u], xs[:, 1, u], ws[0:TT, 1:2], 1.0 / 127, ALU.mult, ALU.mult)
                link(nc.vector.tensor_scalar(rxs[:, 1, u], rxs[:, 1, u], 127.0, None, ALU.mult))
                link(nc.vector.tensor_scalar(g, g, rxs[:, 1, u], MAGIC, ALU.mult, ALU.add))
                nc.vector.tensor_scalar(g, g, MAGIC, -128.0, ALU.subtract, ALU.max).then_inc(s.gq_ready, 1)
                dve.wait_ge(s.gq_turned, t + 1)
                if t >= 2:
                    dve.wait_ge(s.y_ready, t - 1)
                nc.vector.tensor_scalar(GqT[:, t % 2, :, :].rearrange("p c n -> p (c n)"), ps[:, 6 + t % 2, 0:HALF],
                                        127.0, None, ALU.min).then_inc(s.gqT_ready, 1)
            for h in range(2):
                dve.wait_ge(s.y_ready, 4 * h + 4)
                nc.vector.tensor_tensor(Y[:, 4 * h:4 * h + 4, :],
                                        ps[0:TT, h, :].rearrange("p (t m) -> p t m", t=4),
                                        so[:, 1, 4 * h:4 * h + 4].unsqueeze(2).to_broadcast([TT, 4, P]),
                                        ALU.mult).then_inc(s.y_scaled, 1)
            dve.wait_ge(s.y_turned, 1)
            for h in range(2):
                x = k.xT[:, h * HALF:(h + 1) * HALF]
                nc.vector.scalar_tensor_tensor(x, ps[:, 2 + h, 0:HALF], k.v("L0_b2"), x, ALU.add, ALU.add)


def mixture_ffn(nc, k, src, name, NF, normalise):
    E = 8
    with ExitStack() as ctx:
        sb = lambda n, shape, dt=F32: ctx.enter_context(nc.sbuf_tensor(name + "f" + n, shape, dt))
        ps = ctx.enter_context(nc.psum_tensor(name + "fps", [P, 8, BANK], F32))
        s = semaphores(ctx, nc, name + "f", LN_SEMS + " loaded w_loaded0 w_loaded1 logits_ready shifted exp_done "
                       "gates_ready gates_turned gatesT_ready b2_ready gb_filled gb_act gb_dve b2_filled b2_done h_filled h_act "
                       "h_dve y_filled y_read x_added dve_chain carrier")
        w_loaded = (s.w_loaded0, s.w_loaded1)
        Wg = sb("wg", [P, E])
        bg = sb("bg", [TT, E])
        b2 = sb("b2", [E, P])
        W1 = sb("w1", [P, 2, NF, P])
        W2 = sb("w2", [P, 2, NF, P])
        hT = sb("hT", [P, NF, TOK])
        Gb = sb("gb", [P, E, TOK])
        lg = sb("logits", [TT, NTT, E])
        mx = sb("mx", [TT, NTT])
        sm = sb("sm", [TT, NTT])
        gate = sb("gate", [TT, NTT, E])
        rank = sb("rank", [TT, NTT, E])
        gt = sb("gt", [TT, NTT, E, E])
        eq = sb("eq", [TT, NTT, E, E])
        gT = sb("gT", [E, TOK])
        Yg = sb("yg", [P, 2, HALF])
        block = ctx.enter_context(nc.Block())
        tri = k.const[0:TT, C_TRI:C_TRI + 64]
        bank = lambda h, c: (h * NF + c) % 4

        def experts(eng, do):
            do(0, 0)
            do(1, 1)
            with eng.Fori(1, E // 2) as i:
                do(2 * i, 0)
                do(2 * i + 1, 1)

        bcast = lambda ap: ap.unsqueeze(2).to_broadcast([TT, NTT, E])

        @block.sync
        def _(sp):
            sp.dma_start(Wg[:], src[name + "_wg"]).then_inc(s.loaded, 16)
            sp.dma_start(bg[:], src[name + "_bg"].partition_broadcast(TT)).then_inc(s.loaded, 16)
            sp.dma_start(b2[:], src[name + "_b2"]).then_inc(s.loaded, 16)

            def load(e, u):
                sp.dma_start(W1[:, u], src[name + "_w1"][e]).then_inc(w_loaded[u], 16)
                sp.dma_start(W2[:, u], src[name + "_w2"][e]).then_inc(w_loaded[u], 16)

            load(0, 0)
            load(1, 1)
            with sp.Fori(0, E // 2 - 1) as i:
                for u in range(2):
                    sp.wait_ge(s.y_filled, 4 * i + 2 * u + 2)
                    sp.sem_inc(s.carrier, 1)
                    load(2 * i + 2 + u, u)

        @block.gpsimd
        def _(pool):
            ln_pool(pool, k, s, [1e-5])

        @block.tensor
        def _(pe):
            ln_pe(pe, k, s, ps)
            pe.wait_ge(s.ln_done, 2)
            pe.wait_ge(s.loaded, 48)
            for t in range(NTT):
                last = nc.tensor.matmul(ps[0:TT, 0, t * E:(t + 1) * E], k.xnT[:, t * TT:(t + 1) * TT], Wg[:],
                                        start=True, stop=True)
            last.then_inc(s.logits_ready, 1)

            pe.wait_ge(s.gates_ready, 1)
            for t in range(NTT):
                last = nc.tensor.transpose(ps[0:E, 2 + t // 4, (t % 4) * TT:(t % 4 + 1) * TT], gate[:, t, :],
                                           k.ident[0:TT, 0:TT])
            last.then_inc(s.gates_turned, 1)
            pe.wait_ge(s.gatesT_ready, 2)
            for h in range(2):
                nc.tensor.matmul(ps[:, 4 + h, 0:HALF], b2[:], gT[:, h * HALF:(h + 1) * HALF],
                                 start=True, stop=True).then_inc(s.b2_filled, 1)
            for e in range(E):
                for h in range(2):
                    if e >= 1:
                        pe.wait_ge(s.gb_dve if h else s.gb_act, e)
                    nc.tensor.matmul(ps[:, 6 + h, 0:HALF], k.ident[0:E, e:e + 1].to_broadcast([E, P]),
                                     gT[:, h * HALF:(h + 1) * HALF], start=True, stop=True).then_inc(s.gb_filled, 1)

            def expert(e, u):
                first = isinstance(e, int) and e == 0
                if u == 0 or not first:
                    pe.wait_ge(w_loaded[u], 16 * (e + 2 - u))
                for h in range(2):
                    for c in range(NF):
                        if NF == 4 and h == 1:
                            pe.wait_ge(s.h_act, NF * e + c + 1)
                        elif not first:
                            pe.wait_ge(s.h_dve if NF == 4 or h else s.h_act, NF * e - NF + c + 1)
                        nc.tensor.matmul(ps[:, bank(h, c), 0:HALF], W1[:, u, c, :], k.xnT[:, h * HALF:(h + 1) * HALF],
                                         start=True, stop=True).then_inc(s.h_filled, 1)
                for h in range(2):
                    pe.wait_ge(s.h_dve if h else s.h_act, NF * e + NF)
                    if first:
                        pe.wait_ge(s.b2_done, 2)
                    else:
                        pe.wait_ge(s.y_read, 2 * e + h - 1)
                    for c in range(NF):
                        last = nc.tensor.matmul(ps[:, 4 + h, 0:HALF], W2[:, u, c, :],
                                                hT[:, c, h * HALF:(h + 1) * HALF], start=c == 0, stop=c == NF - 1)
                    last.then_inc(s.y_filled, 1)

            experts(pe, expert)

        @block.scalar
        def _(act):
            act.wait_ge(s.shifted, 1)
            nc.scalar.activation(gate[:], lg[:], ACT.Exp).then_inc(s.exp_done, 1)
            for e in range(E):
                act.wait_ge(s.gb_filled, 2 * e + 1)
                nc.scalar.copy(Gb[:, e, 0:HALF], ps[:, 6, 0:HALF]).then_inc(s.gb_act, 1)

            def expert(e, u):
                for c in range(NF):
                    act.wait_ge(s.h_filled, 2 * NF * e + c + 1)
                    nc.scalar.activation(hT[:, c, 0:HALF], ps[:, bank(0, c), 0:HALF], ACT.Relu,
                                         bias=k.vec[:, bass.ds(Vectors.at[name + "_b1"] + NF * e + c, 1)]
                                         ).then_inc(s.h_act, 1)

            experts(act, expert)

        @block.vector
        def _(dve):
            link = Chain(dve, s.dve_chain)
            ln_dve(dve, k, s, ps, link, [1e-5])
            dve.wait_ge(s.loaded, 48)
            dve.wait_ge(s.logits_ready, 1)
            link(nc.vector.tensor_tensor(lg[:], ps[0:TT, 0, 0:NTT * E].rearrange("p (t e) -> p t e", e=E),
                                         bg[:].unsqueeze(1).to_broadcast([TT, NTT, E]), ALU.add))
            link(nc.vector.tensor_reduce(mx[:], lg[:], AX.X, ALU.max))
            nc.vector.tensor_tensor(lg[:], lg[:], bcast(mx[:]), ALU.subtract).then_inc(s.shifted, 1)
            dve.wait_ge(s.exp_done, 1)
            link(nc.vector.tensor_reduce(sm[:], gate[:], AX.X, ALU.add))
            link(nc.vector.reciprocal(sm[:], sm[:]))
            link(nc.vector.tensor_tensor(gate[:], gate[:], bcast(sm[:]), ALU.mult))
            for t in range(NTT):
                g_j = gate[:, t, :].unsqueeze(1).to_broadcast([TT, E, E])
                g_e = gate[:, t, :].unsqueeze(2).to_broadcast([TT, E, E])
                nc.vector.tensor_tensor(gt[:, t], g_j, g_e, ALU.is_gt)
                last = nc.vector.tensor_tensor(eq[:, t], g_j, g_e, ALU.is_equal)
            link(last)
            link(nc.vector.tensor_tensor(eq[:].rearrange("p t e j -> p t (e j)"),
                                         eq[:].rearrange("p t e j -> p t (e j)"),
                                         tri.unsqueeze(1).to_broadcast([TT, NTT, E * E]), ALU.mult))
            link(nc.vector.tensor_tensor(gt[:].rearrange("p t e j -> p (t e j)"), gt[:].rearrange("p t e j -> p (t e j)"),
                                         eq[:].rearrange("p t e j -> p (t e j)"), ALU.add))
            link(nc.vector.tensor_reduce(rank[:], gt[:], AX.X, ALU.add))
            last = nc.vector.scalar_tensor_tensor(gate[:].rearrange("p t e -> p (t e)"),
                                                  rank[:].rearrange("p t e -> p (t e)"), 2.0,
                                                  gate[:].rearrange("p t e -> p (t e)"), ALU.is_lt, ALU.mult)
            if normalise:
                link(last)
                link(nc.vector.tensor_reduce(sm[:], gate[:], AX.X, ALU.add))
                link(nc.vector.reciprocal(sm[:], sm[:]))
                last = nc.vector.tensor_tensor(gate[:], gate[:], bcast(sm[:]), ALU.mult)
            last.then_inc(s.gates_ready, 1)
            dve.wait_ge(s.gates_turned, 1)
            for h in range(2):
                nc.vector.tensor_copy(gT[:, h * HALF:(h + 1) * HALF], ps[0:E, 2 + h, 0:HALF]).then_inc(s.gatesT_ready, 1)
            for h in range(2):
                dve.wait_ge(s.b2_filled, h + 1)
                x = k.xT[:, h * HALF:(h + 1) * HALF]
                nc.vector.tensor_tensor(x, x, ps[:, 4 + h, 0:HALF], ALU.add).then_inc(s.b2_done, 1)
            for e in range(E):
                dve.wait_ge(s.gb_filled, 2 * e + 2)
                nc.vector.tensor_copy(Gb[:, e, HALF:TOK], ps[:, 7, 0:HALF]).then_inc(s.gb_dve, 1)
            dve.wait_ge(s.gb_act, E)
            dve.wait_ge(s.b2_done, 2)

            def expert(e, u):
                for c in range(NF):
                    dve.wait_ge(s.h_filled, 2 * NF * e + NF + c + 1)
                    nc.vector.tensor_scalar(hT[:, c, HALF:TOK], ps[:, bank(1, c), 0:HALF],
                                            k.vec[:, bass.ds(Vectors.at[name + "_b1"] + NF * e + c, 1)], 0.0,
                                            ALU.add, ALU.max).then_inc(s.h_dve, 1)
                for h in range(2):
                    dve.wait_ge(s.y_filled, 2 * e + h + 1)
                    nc.vector.tensor_tensor(Yg[:, h, :], ps[:, 4 + h, 0:HALF], Gb[:, bass.ds(e, 1), h * HALF:(h + 1) * HALF].rearrange("p a n -> p (a n)"),
                                            ALU.mult).then_inc(s.y_read, 1)
                for h in range(2):
                    dve.wait_ge(s.y_read, 2 * e + h + 1)
                    x = k.xT[:, h * HALF:(h + 1) * HALF]
                    nc.vector.tensor_tensor(x, x, Yg[:, h, :], ALU.add).then_inc(s.x_added, 1)
                dve.wait_ge(s.x_added, 2 * e + 2)

            experts(dve, expert)


def ternary_ffn(nc, k, src):
    F, NF = 512, 4
    name = "L3f"
    with ExitStack() as ctx:
        sb = lambda n, shape, dt=F32: ctx.enter_context(nc.sbuf_tensor(name + n, shape, dt))
        ps = ctx.enter_context(nc.psum_tensor(name + "ps", [P, 8, BANK], F32))
        s = semaphores(ctx, nc, name, LN_SEMS + " w_loaded sums_ready sums_total wq_ready h_ready gelu_done var_ready "
                       "rstd_ready norm_ready turned hT_ready y_ready dve_chain")
        W = sb("w", [P, 2, F])
        wsum = sb("wsum", [P, 2])
        rws = sb("rws", [P, 2])
        G = sb("gelu", [TT, NTT, F])
        st = sb("st", [TT, NTT, 6])
        mv = sb("mv2", [TT, NTT, 2])
        rstd = sb("rstd2", [TT, NTT])
        hT = sb("hT", [P, NF, TOK])
        block = ctx.enter_context(nc.Block())

        @block.sync
        def _(sp):
            sp.dma_start(W[:], src["L3_ffn_w"]).then_inc(s.w_loaded, 16)

        @block.gpsimd
        def _(pool):
            ln_pool(pool, k, s, [1e-5])
            for h in range(2):
                pool.wait_ge(s.var_ready, h + 1)
                nc.gpsimd.tensor_tensor(rstd[:, 4 * h:4 * h + 4], mv[:, 4 * h:4 * h + 4, 1], k.half_neg[0:TT, 0:4],
                                        ALU.pow).then_inc(s.rstd_ready, 1)

        @block.tensor
        def _(pe):
            ln_pe(pe, k, s, ps)
            pe.wait_ge(s.sums_ready, 1)
            nc.tensor.matmul(ps[:, 7, 0:2], k.ones[:], wsum[:], start=True, stop=True).then_inc(s.sums_total, 1)
            pe.wait_ge(s.ln_done, 2)
            pe.wait_ge(s.wq_ready, 1)
            for t in range(NTT):
                if t >= 4:
                    pe.wait_ge(s.gelu_done, t - 3)
                nc.tensor.matmul(ps[0:TT, 4 + t % 4, :], k.xnT[:, t * TT:(t + 1) * TT], W[:, 0, :],
                                 start=True, stop=True).then_inc(s.h_ready, 1)
            for h in range(2):
                pe.wait_ge(s.norm_ready, h + 1)
                for c in range(NF):
                    n = h * NF + c
                    if n >= 2:
                        pe.wait_ge(s.hT_ready, n - 1)
                    for t in range(4):
                        last = nc.tensor.transpose(ps[:, n % 2, t * TT:(t + 1) * TT],
                                                   G[:, 4 * h + t, c * P:(c + 1) * P], k.ident[0:TT, 0:TT])
                    last.then_inc(s.turned, 1)
            for h in range(2):
                pe.wait_ge(s.hT_ready, NF * (h + 1))
                for c in range(NF):
                    last = nc.tensor.matmul(ps[:, 2 + h, 0:HALF], W[:, 1, c * P:(c + 1) * P],
                                            hT[:, c, h * HALF:(h + 1) * HALF], start=c == 0, stop=c == NF - 1)
                last.then_inc(s.y_ready, 1)

        @block.scalar
        def _(act):
            for t in range(NTT):
                act.wait_ge(s.h_ready, t + 1)
                nc.scalar.activation(G[:, t, :], ps[0:TT, 4 + t % 4, :], ACT.Gelu).then_inc(s.gelu_done, 1)

        @block.vector
        def _(dve):
            link = Chain(dve, s.dve_chain)
            dve.wait_ge(s.w_loaded, 16)
            abs_sums(nc, wsum[:, 0:1], W[:, 0, :])
            abs_sums(nc, wsum[:, 1:2], W[:, 1, :]).then_inc(s.sums_ready, 1)
            ln_dve(dve, k, s, ps, link, [1e-5])
            dve.wait_ge(s.sums_total, 1)
            link(nc.vector.tensor_scalar(rws[:], ps[:, 7, 0:2], 1.0 / (F * P), 1e-6, ALU.mult, ALU.add))
            link(nc.vector.reciprocal(rws[:], rws[:]))
            for n in range(2):
                last = ternary(nc, link, W[:, n, :], W[:, n, :], rws[:, n:n + 1])
            last.then_inc(s.wq_ready, 1)
            for h in range(2):
                for t in range(4 * h, 4 * h + 4):
                    dve.wait_ge(s.gelu_done, t + 1)
                    last = nc.vector.bn_stats(st[:, t, :], G[:, t, :])
                link(last)
                for t in range(4 * h, 4 * h + 4):
                    last = nc.vector.bn_aggr(mv[:, t, :], st[:, t, :])
                link(last)
                nc.vector.tensor_scalar(mv[:, 4 * h:4 * h + 4, 1], mv[:, 4 * h:4 * h + 4, 1], 1e-5, None,
                                        ALU.add).then_inc(s.var_ready, 1)
            for h in range(2):
                dve.wait_ge(s.rstd_ready, h + 1)
                for t in range(4 * h, 4 * h + 4):
                    last = nc.vector.tensor_scalar(G[:, t, :], G[:, t, :], mv[:, t, 0:1], rstd[:, t:t + 1],
                                                   ALU.subtract, ALU.mult)
                last.then_inc(s.norm_ready, 1)
            for h in range(2):
                for c in range(NF):
                    n = h * NF + c
                    dve.wait_ge(s.turned, n + 1)
                    nc.vector.tensor_scalar(hT[:, c, h * HALF:(h + 1) * HALF], ps[:, n % 2, 0:HALF],
                                            k.v("L3_lnw", c), k.v("L3_lnb", c), ALU.mult,
                                            ALU.add).then_inc(s.hT_ready, 1)
            for h in range(2):
                dve.wait_ge(s.y_ready, h + 1)
                x = k.xT[:, h * HALF:(h + 1) * HALF]
                nc.vector.tensor_tensor(x, x, ps[:, 2 + h, 0:HALF], ALU.add)



def load(nc, k, src):
    with ExitStack() as ctx:
        loaded = ctx.enter_context(nc.semaphore("loaded"))
        block = ctx.enter_context(nc.Block())

        @block.sync
        def _(sp):
            sp.dma_start(k.xT[:], src["xT"]).then_inc(loaded, 16)
            sp.dma_start(k.const[:], src["const"]).then_inc(loaded, 16)
            sp.dma_start(k.vec[:], src["vec"]).then_inc(loaded, 16)
            sp.wait_ge(loaded, 48)

        @block.gpsimd
        def _(pool):
            nc.gpsimd.memset(k.half_neg[:], -0.5)
            nc.gpsimd.memset(k.ones[:], 1.0)


def store(nc, k, out):
    with ExitStack() as ctx:
        stored = ctx.enter_context(nc.semaphore("stored"))
        block = ctx.enter_context(nc.Block())

        @block.sync
        def _(sp):
            sp.dma_start(out, k.xT[:]).then_inc(stored, 16)
            sp.wait_ge(stored, 16)


def build(nc, src, out, stages):
    with ExitStack() as ctx:
        k = Core(ctx, nc)
        load(nc, k, src)
        for name in stages:
            STAGE[name](nc, k, src)
        store(nc, k, out)


STAGE = {
    "L2a": attention_16_wide_heads,
    "L1a": latent_attention,
    "L0f": bitlinear_ffn,
    "L1f": lambda nc, k, src: mixture_ffn(nc, k, src, "L1", 4, False),
    "L2f": lambda nc, k, src: mixture_ffn(nc, k, src, "L2", 2, True),
    "L3f": ternary_ffn,
    "L0a": lambda nc, k, src: attention_16_small_heads(nc, k, "L0", src, 8 ** -0.5, True),
    "L3a": lambda nc, k, src: attention_16_small_heads(nc, k, "L3", src, P ** -0.5, False),
}
STAGES = ["L0a", "L0f", "L1a", "L1f", "L2a", "L2f", "L3a", "L3f"]


def constant_columns(np):
    c = np.zeros((P, N_CONST), np.float32)
    p = np.arange(P)
    c[:, C_ID:C_ID + P] = np.eye(P)
    c[:, C_HEAD:C_HEAD + 16] = p[:, None] // 8 == np.arange(16)
    c[:, C_PAIR:C_PAIR + 2] = (p[:, None] % 32) // 8 == np.arange(2)
    c[:TT, C_QSEL:C_QSEL + Q] = p[:TT, None] % Q == np.arange(Q)
    c[:TT, C_J32:C_J32 + 32] = p[:TT, None] // Q == np.arange(32) // 8
    c[:TT, C_J2:C_J2 + 2] = p[:TT, None] // Q == np.arange(2)
    c[:, C_TRI:C_TRI + 64] = (np.arange(8)[None, :] < np.arange(8)[:, None]).reshape(1, 64)
    c[:, C_HALF:C_HALF + 2] = p[:, None] // 64 == np.arange(2)
    return c


def lay_out(i, np):
    f = {n: np.asarray(a) for n, a in i.items()}
    keys = np.arange(S2).reshape(CH, NCH).T.reshape(-1)
    a = {"xT": f["x"].reshape(TOK, P).T,
         "ctx": f["ctx_1024"].reshape(B, CH, NCH, P),
         "ctxT": f["ctx_1024"].transpose(0, 2, 1)[:, :, keys],
         "mask_full": f["mask_BxS2_bf1"][:, keys],
         "mask_some": f["mask_BxS2_bk0"][:, keys],
         "const": constant_columns(np)}

    def padded(w):
        o = np.zeros(w.shape[:-1] + (2, 4, 32), np.float32)
        o[..., :16] = w.reshape(w.shape[:-1] + (2, 4, 16))
        return o.reshape(w.shape[:-1] + (2, P))

    for n in ("L0", "L3"):
        wq, wk, wv, wo = (f[n + "_xattn_W" + x] for x in "qkvo")
        a[n + "_attn_w"] = np.stack([wq.T, wk.T, *padded(wv.T).transpose(1, 0, 2),
                                     *padded(wo).transpose(1, 2, 0)], 1)
    heads_first = lambda w: w.reshape(P, 16, 64).transpose(2, 1, 0)
    wkv = f["L2_xattn_Wkv"]
    a["L2_attn_w"] = np.stack([heads_first(f["L2_xattn_Wq"]), heads_first(wkv[:, :1024]), heads_first(wkv[:, 1024:]),
                               f["L2_xattn_Wo"].reshape(16, 64, P).transpose(1, 0, 2)], 1)
    a["L2_null"] = f["L2_xattn_null_kv"].T
    a["L2_cs_row"], a["L2_cb_row"] = f["L2_xattn_lnc_s"], f["L2_xattn_lnc_b"]
    wkv = f["L1_xattn_W_kv"]
    a["L1_attn_w"] = np.stack([f["L1_xattn_W_q"], wkv[:, :P], wkv[:, P:], f["L1_xattn_W_out"]], 1)

    def chunked(w):
        w = w.reshape(w.shape[:-2] + (w.shape[-2] // P, P, w.shape[-1]))
        return np.moveaxis(w, -3, -2)

    for n, up, down in (("L0_ffn_w", "L0_ffn_W1", "L0_ffn_W2"), ("L3_ffn_w", "L3_ffn_W_fc", "L3_ffn_W_proj")):
        a[n] = np.stack([f[up].T, chunked(f[down].T).reshape(P, 512)], 1)
    a["L0_ffn_b1"] = f["L0_ffn_b1"]
    for n, wg, bg, w1, w2, b2 in (("L1", "Wg", "bg", "W1", "W2", "b2"),
                                  ("L2", "router_w", "router_b", "w1", "w2", "b2")):
        a[n + "_wg"], a[n + "_bg"], a[n + "_b2"] = (f[n + "_ffn_" + x] for x in (wg, bg, b2))
        w = f[n + "_ffn_" + w1]
        a[n + "_w1"] = w.reshape(8, P, -1, P)
        a[n + "_w2"] = chunked(f[n + "_ffn_" + w2])

    bv = padded(f["L0_xattn_bv"])
    cols = {"L0_bq": f["L0_xattn_bq"], "L0_bk": f["L0_xattn_bk"], "L0_bo": f["L0_xattn_bo"],
            "L0_bv0": bv[0], "L0_bv1": bv[1], "L0_b2": f["L0_ffn_b2"],
            "L1_xg": f["L1_xattn_ln_x_g"], "L1_xb": f["L1_xattn_ln_x_b"], "L1_lg": f["L1_xattn_ln_l_g"],
            "L1_lb": f["L1_xattn_ln_l_b"], "L1_qg": np.tile(f["L1_xattn_q_gamma"], 2),
            "L1_kg": np.tile(f["L1_xattn_k_gamma"], 2), "L1_bout": f["L1_xattn_b_out"],
            "L2_1s": f["L2_xattn_ln1_s"], "L2_1b": f["L2_xattn_ln1_b"], "L2_cs": f["L2_xattn_lnc_s"],
            "L2_cb": f["L2_xattn_lnc_b"], "L2_os": f["L2_xattn_lno_s"], "L2_ob": f["L2_xattn_lno_b"],
            "L3_bo": f["L3_xattn_bo"], "L3_lnw": f["L3_ffn_ln_w"], "L3_lnb": f["L3_ffn_ln_b"],
            "L1_b1": f["L1_ffn_b1"], "L2_b1": f["L2_ffn_b1"]}
    v = np.zeros((P, Vectors.total), np.float32)
    for n in Vectors.names:
        w = Vectors.width.get(n, 1)
        v[:, Vectors.at[n]:Vectors.at[n] + w] = np.asarray(cols[n]).reshape(w, P).T
    a["vec"] = v
    return {n: np.ascontiguousarray(x) for n, x in a.items()}


def kernel(**inputs):
    import numpy as _np
    import concourse.bacc as _bacc
    from concourse import mybir as _mybir
    from concourse.bass_utils import run_bass_kernel_spmd as _run

    nc = _bacc.Bacc("TRN2", target_bir_lowering=False, num_devices=1)
    arrays, src = {}, {}
    for name, a in lay_out(inputs, _np).items():
        arrays["in_" + name] = a
        src[name] = nc.dram_tensor("in_" + name, a.shape, _mybir.dt.from_np(a.dtype), kind="ExternalInput").ap()
    out = nc.dram_tensor("outT", (P, TOK), F32, kind="ExternalOutput").ap()
    build(nc, src, out, STAGES)
    r = _run(nc, [arrays], core_ids=[0])
    return _np.ascontiguousarray(r.results[0]["outT"].T).reshape(B, Q, P)
```

```python
from collections import namedtuple
from contextlib import ExitStack

import concourse.bass as bass
from concourse import mybir
from concourse.alu_op_type import AluOpType as ALU

F32 = mybir.dt.float32
U8 = mybir.dt.uint8
BF16 = mybir.dt.bfloat16
ACT = mybir.ActivationFunctionType
AX = mybir.AxisListType

P = 128
B, Q, S2 = 16, 56, 1500
TOK = B * Q
TT = 2 * Q
NTT = TOK // TT
CH, NCH = 125, 12
HALF = 4 * TT
BANK = 512
FLT_MAX = 3.4028234663852886e38

C_ID, C_HEAD, C_PAIR, C_QSEL, C_J32, C_J2, C_TRI, C_HALF = 0, 128, 144, 146, 202, 234, 236, 300
C_ROW = 302
N_CONST = 310


class Vectors:
    names = ["L0_bq", "L0_bk", "L0_bo", "L0_bv0", "L0_bv1", "L0_b2",
             "L1_xg", "L1_xb", "L1_lg", "L1_lb", "L1_qg", "L1_kg", "L1_bout",
             "L2_1s", "L2_1b", "L2_cs", "L2_cb", "L2_os", "L2_ob",
             "L3_bo", "L3_lnw", "L3_lnb", "L1_b1", "L2_b1"]
    width = {"L3_lnw": 4, "L3_lnb": 4, "L1_b1": 32, "L2_b1": 16}
    at = {}
    total = 0
    for _n in names:
        at[_n] = total
        total += width.get(_n, 1)


class Core:

    def __init__(self, ctx, nc):
        sb = lambda name, shape, dt=F32: ctx.enter_context(nc.sbuf_tensor(name, shape, dt))
        self.nc = nc
        self.xT = sb("xT", [P, TOK])
        self.xnT = sb("xnT", [P, TOK])
        self.xn = sb("xn", [TT, NTT, P])
        self.stats = sb("stats", [TT, NTT, 6])
        self.mv = sb("mv", [TT, NTT, 2])
        self.rstd = sb("rstd", [TT, NTT])
        self.ones = sb("ones", [P, P])
        self.half_neg = sb("half_neg", [P, 32])
        self.const = sb("const", [P, N_CONST])
        self.vec = sb("vec", [P, Vectors.total])
        self.ctx_mv = sb("ctx_mv", [CH, B, NCH, 2])
        self.ident = self.const[:, C_ID:C_ID + P]

    def v(self, name, k=0, rows=P):
        c = Vectors.at[name] + k
        return self.vec[0:rows, c:c + 1]


def semaphores(ctx, nc, prefix, names):
    s = namedtuple("Semaphores", names)(*(nc.alloc_semaphore(name=prefix + n) for n in names.split()))
    ctx.callback(clear_semaphores, nc, list(s))
    return s


def clear_semaphores(nc, sems):
    nc.clear_and_free_semaphores(sems)
    nc.all_engine_barrier()


class Chain:

    def __init__(self, eng, sem):
        self.eng, self.sem, self.n = eng, sem, 0

    def __call__(self, ins):
        self.n += 1
        ins.then_inc(self.sem, 1)
        self.eng.wait_ge(self.sem, self.n)


LN_SEMS = "ln_tok ln_var ln_rstd ln_norm ln_feat ln_done"


def ln_pe(pe, k, s, ps, feature_major=True, stream=None):
    nc = k.nc
    for t in range(NTT):
        last = nc.tensor.transpose(ps[0:TT, t // 4, (t % 4) * P:(t % 4 + 1) * P],
                                   (k.xT if stream is None else stream)[:, t * TT:(t + 1) * TT], k.ident)
    last.then_inc(s.ln_tok, 1)
    if feature_major:
        ln_turn(pe, k, s, ps)


def ln_turn(pe, k, s, ps):
    nc = k.nc
    pe.wait_ge(s.ln_norm, 1)
    for t in range(NTT):
        last = nc.tensor.transpose(ps[:, 2 + t // 4, (t % 4) * TT:(t % 4 + 1) * TT],
                                   k.xn[:, t, :], k.ident[0:TT, 0:TT])
    last.then_inc(s.ln_feat, 1)


def ln_pool(pool, k, s, eps):
    nc = k.nc
    for n in range(len(eps)):
        pool.wait_ge(s.ln_var, n + 1)
        nc.gpsimd.tensor_tensor(k.rstd[:], k.mv[:, :, 1], k.half_neg[0:TT, 0:NTT],
                                ALU.pow).then_inc(s.ln_rstd, 1)


def ln_dve(dve, k, s, ps, link, eps, scale=None, bias=None, feature_major=True):
    nc = k.nc
    dve.wait_ge(s.ln_tok, 1)
    src = lambda t: ps[0:TT, t // 4, (t % 4) * P:(t % 4 + 1) * P]
    for n, e in enumerate(eps):
        for t in range(NTT):
            last = nc.vector.bn_stats(k.stats[:, t, :], src(t))
        link(last)
        for t in range(NTT):
            last = nc.vector.bn_aggr(k.mv[:, t, :], k.stats[:, t, :])
        link(last)
        nc.vector.tensor_scalar(k.mv[:, :, 1], k.mv[:, :, 1], e, None, ALU.add).then_inc(s.ln_var, 1)
        dve.wait_ge(s.ln_rstd, n + 1)
        for t in range(NTT):
            last = nc.vector.tensor_scalar(k.xn[:, t, :], src(t), k.mv[:, t, 0:1], k.rstd[:, t:t + 1],
                                           ALU.subtract, ALU.mult)
        if n < len(eps) - 1:
            link(last)
        src = lambda t: k.xn[:, t, :]
    last.then_inc(s.ln_norm, 1)
    if not feature_major:
        return
    dve.wait_ge(s.ln_feat, 1)
    for h in range(2):
        out, src2 = k.xnT[:, h * HALF:(h + 1) * HALF], ps[:, 2 + h, 0:HALF]
        if scale is None:
            last = nc.vector.tensor_copy(out, src2)
        else:
            last = nc.vector.tensor_scalar(out, src2, scale, bias, ALU.mult, ALU.add)
        last.then_inc(s.ln_done, 1)


class Slots:

    def __init__(self, prep, steps, tail, last_steps, ring=2):
        self.ring = ring
        self.prologue = prep
        self.mid = steps
        self.first = [x for x in steps if x[1] not in tail]
        self.last = [x for x in steps if x[1] not in {p[1] for p in prep}]
        self.tail = last_steps
        for a in (self.prologue, self.first):
            assert [x[3] for x in a[-ring:]] == [x[3] for x in self.mid[-ring:]]

    def of(self, kind):
        return {"prologue": self.prologue, "first": self.first, "mid": self.mid, "last": self.last,
                "tail": self.tail}[kind]

    def before(self, kind, b, eng=None):
        n = lambda xs: sum(1 for x in xs if eng is None or x[3] == eng)
        if kind == "prologue":
            return 0
        if kind == "first":
            return n(self.prologue)
        base = n(self.prologue) + n(self.first)
        if kind == "tail":
            return base + n(self.mid) * (B - 2) + n(self.last)
        return base + n(self.mid) * (b - 1)

    def number(self, kind, b, i, eng=None):
        xs = self.of(kind)
        if i >= 0:
            return self.before(kind, b, eng) + sum(1 for x in xs[:i + 1] if eng is None or x[3] == eng)
        less = self.prev(kind)[i + 1:] if i < -1 else []
        return self.before(kind, b, eng) - sum(1 for x in less if eng is None or x[3] == eng)

    def engine(self, kind, i):
        return self.of(kind)[i][3] if i >= 0 else self.prev(kind)[i][3]

    def prev(self, kind):
        return self.last if kind == "tail" else self.mid

    def bank(self, kind, b_odd, i):
        n = {"prologue": 0, "first": len(self.prologue)}.get(kind)
        if n is None:
            n = len(self.prologue) + len(self.first)
            if kind == "tail":
                n += len(self.mid) * (B - 2) + len(self.last)
            else:
                n += len(self.mid) * (b_odd + 1)
                assert len(self.mid) * 2 % self.ring == 0
        return (n + i) % self.ring

    def find(self, kind, what, num):
        for i, x in enumerate(self.of(kind)):
            if x[1:3] == (what, num):
                return i
        return None


def step_slots(plan, kind, step):
    return [(i, x[1], x[2], x[3]) for i, x in enumerate(plan.of(kind)) if x[0] == step]


def batches(eng, do):
    do(0, 0, "first")
    with eng.Fori(0, (B - 2) // 2) as i:
        do(2 * i + 1, 1, "mid")
        do(2 * i + 2, 0, "mid")
    do(B - 1, 1, "last")


NT = 8


COMBOS = ((0, 0), (0, 1), (1, 0), (1, 1), (0, 2), (2, 0))


def attention_16_small_heads(nc, k, name, src, scale, masked):
    D, A = "D", "A"
    keys = [(5, "K", 0, A), (6, "K", 1, A), (7, "K", 2, A)]
    values = [(t, "V", t, A) for t in range(6)]
    steps = []
    for t in range(NT):
        steps.append((t, "T", 3 * t, D))
        steps += [p for p in keys if p[0] == t]
        steps += [p for p in values if p[0] == t]
        steps.append((t, "T", 3 * t + 1, A))
        if t == 1:
            steps.append((1, "R", 0, D))
        if t == 2:
            steps.append((2, "Y", 0, D))
        steps.append((t, "T", 3 * t + 2, A))
        if t in (3, 7):
            steps.append((t, "O", t // 4, D))
    prologue = keys + values[:4] + [(0, "K", 3, A), (0, "K", 4, A)] + values[4:] + [(0, "K", 5, D)]
    plan = Slots(prologue, steps, ("R", "Y"), [(0, "R", 0, D), (0, "Y", 0, D)])
    ROWS = 16 * len(COMBOS) + (1 if masked else 0)
    SPLIT = 5 if masked else 4
    N_STACK = len(COMBOS) + (1 if masked else 0)

    with ExitStack() as ctx:
        sb = lambda n, shape, dt=F32: ctx.enter_context(nc.sbuf_tensor(name + n, shape, dt))
        S = ctx.enter_context(nc.psum_tensor(name + "scores", [P, 2, 3, BANK], F32))
        G = ctx.enter_context(nc.psum_tensor(name + "ring", [P, 2, BANK], F32))
        S6 = S[:].rearrange("p a b n -> p (a b) n")
        s = semaphores(ctx, nc, name, LN_SEMS + " w_loaded ctx_loaded0 ctx_loaded1 filled emptied_a emptied_d scores_ready "
                       "rowmax_ready exp_done mask_ready parts_ready stacked0 stacked1 q_split mask_weight q_stacked tail_r tail_a tail_t setup_pe "
                       "dve_chain carrier")
        KF = sb("keys", [P, S2])
        KP = sb("key_parts", [P, 3, S2], BF16)
        KS = sb("key_stack", [ROWS, 2, NT, S2], BF16)
        V = sb("values", [CH, 2, NCH, 2 * P])
        QS = sb("query_stack", [ROWS, NT, B, 2, Q], BF16)
        CT = sb("ctxT", [P, 2, S2])
        PR = sb("probs", [TT, 2, S2])
        with ExitStack() as setup:
            QP = setup.enter_context(nc.sbuf_tensor(name + "query_parts", [P, 3, TOK], BF16))
            QM = setup.enter_context(nc.sbuf_tensor(name + "query_masked", [P, 3, B, 2, Q], BF16))
        PT = sb("probsT", [CH, NCH, 4, TT])
        OS = sb("osum", [P, 2, 2, TT])
        ssum = sb("sums", [TT, 2, NT])
        nmax = sb("negmax", [TT, 2, NT])
        rinv = sb("rinv", [TT, NT])
        Am = sb("rinv_spread", [TT, 8, 32])
        R4 = sb("rinv_rows", [P, 2, 2, Q])
        Tm = sb("heads_out", [P, 2, 2, Q])
        qT = sb("qT", [P, TOK])
        W = sb("w", [P, 6, P])
        bout = sb("bout", [P, 1])
        if masked:
            MR = sb("mask", [P, 2, S2], U8)
            MF = sb("mask_float", [P, S2], BF16)
            MW = sb("mask_weights", [TT, P], BF16)
            MB = sb("mask_row", [1, S2], BF16)
        head_mask = k.const[:, C_HALF:C_HALF + 2]
        pair_mask = k.const[:, C_PAIR:C_PAIR + 2]
        same_query = k.const[0:TT, C_QSEL:C_QSEL + Q]
        row_half = k.const[0:TT, C_J32:C_J32 + 32]
        n_load = 2 if masked else 1
        chunks = lambda ap: ap.rearrange("p (c n) -> p c n", c=3)

        ctx_loaded = (s.ctx_loaded0, s.ctx_loaded1)

        def wait_context(eng, b, u):
            eng.wait_ge(ctx_loaded[u], 8 * n_load * (b + 2 - u))

        stacked = (s.stacked0, s.stacked1)

        def keys_of(b, odd, kind, num):
            return (num // 3, num // 3) if kind == "prologue" else (b + 2, odd)

        def keys_free(eng, b, odd, kind, num):
            nb, u = keys_of(b, odd, kind, num)
            if not (isinstance(nb, int) and nb == 0):
                eng.wait_ge(s.parts_ready, SPLIT * nb)

        def filled(eng, kind, b, i):
            eng.wait_ge(s.filled, plan.number(kind, b, i))

        block = ctx.enter_context(nc.Block())

        @block.sync
        def _(sp):
            sp.dma_start(W[:], src[name + "_attn_w"]).then_inc(s.w_loaded, 16)

            def load(b, u):
                b = min(b, B - 1) if isinstance(b, int) else b
                sp.dma_start(CT[:, u, :], src["ctxT"][b]).then_inc(ctx_loaded[u], 16)
                if masked:
                    sp.dma_start(MR[:, u, :], src["mask_full"][b].partition_broadcast(P)).then_inc(ctx_loaded[u], 16)

            def reload(b, u, kind, at):
                sp.wait_ge(s.filled, plan.number(kind, at, plan.find(kind, "V", 5)))
                sp.sem_inc(s.carrier, 1)
                if masked:
                    sp.wait_ge(s.mask_ready, 2 * b - 2)
                    sp.sem_inc(s.carrier, 1)
                load(b, u)

            def stack(b, u, again):
                sp.wait_ge(s.parts_ready, SPLIT * (b + 1))
                sp.sem_inc(s.carrier, 1)
                if masked:
                    sp.wait_ge(s.mask_ready, 2 * b + 2)
                    sp.sem_inc(s.carrier, 1)
                if again:
                    sp.wait_ge(s.scores_ready, 8 * b - 8)
                    sp.sem_inc(s.carrier, 1)
                for n, (_, part) in enumerate(COMBOS):
                    sp.dma_start(KS[16 * n:16 * n + 16, u], KP[:, part]).then_inc(stacked[u], 16)
                if masked:
                    sp.dma_start(KS[16 * len(COMBOS):ROWS, u], MB[:].unsqueeze(1).to_broadcast([1, NT, S2])
                                 ).then_inc(stacked[u], 16)

            load(0, 0)
            load(1, 1)
            stack(0, 0, False)
            for n in sorted(range(len(COMBOS)), key=lambda n: COMBOS[n][0]):
                part = COMBOS[n][0]
                sp.wait_ge(s.q_split, part + 1)
                sp.dma_start(QS[16 * n:16 * n + 16].rearrange("f g b j q -> f g (b j q)"),
                             QM[:, part].rearrange("p b j q -> p (b j q)")).then_inc(s.q_stacked, 16)
            if masked:
                sp.wait_ge(s.mask_weight, 1)
                sp.dma_start(QS[16 * len(COMBOS):ROWS].rearrange("f g b j q -> f (g b j q)"), MW[:]
                             ).then_inc(s.q_stacked, 16)
            reload(2, 0, "prologue", 0)
            stack(1, 1, False)
            reload(3, 1, "first", 0)
            stack(2, 0, True)
            with sp.Fori(0, (B - 4) // 2) as i:
                reload(2 * i + 4, 0, "mid", 2 * i + 1)
                stack(2 * i + 3, 1, True)
                reload(2 * i + 5, 1, "mid", 2 * i + 2)
                stack(2 * i + 4, 0, True)
            reload(B, 0, "mid", B - 3)
            stack(B - 1, 1, True)

        @block.tensor
        def _(pe):
            def scores(b, odd, t, early):
                if t == 0:
                    pe.wait_ge(stacked[odd], 8 * N_STACK * (b + 2 - odd))
                if not early:
                    pe.wait_ge(s.exp_done, 8 * b + t - 1)
                for c in range(3):
                    last = nc.tensor.matmul(S[0:TT, t % 2, c, 0:500],
                                            QS[:, t, bass.ds(b, 1)].rearrange("p a j q -> p (a j q)"),
                                            KS[:, odd, t, c * 500:(c + 1) * 500], start=True, stop=True)
                last.then_inc(s.scores_ready, 1)

            def slot(b, odd, kind, i, what, num):
                bank = plan.bank(kind, odd, i)
                if kind != "prologue" or i >= 2:
                    e = plan.engine(kind, i - 2)
                    pe.wait_ge(s.emptied_a if e == A else s.emptied_d, plan.number(kind, b, i - 2, e))
                nu = 0 if kind == "prologue" else 1 - odd
                if what == "K":
                    nb, u = keys_of(b, odd, kind, num)
                    if num % 3 == 0:
                        wait_context(pe, nb, u)
                    last = nc.tensor.matmul(G[:, bank, 0:500], W[:, 1, :], CT[:, u, num % 3 * 500:(num % 3 + 1) * 500],
                                            start=True, stop=True)
                elif what == "V":
                    for j in range(2):
                        c = 2 * num + j
                        last = nc.tensor.matmul(G[0:CH, bank, j * 256:(j + 1) * 256],
                                                CT[:, nu, c * CH:(c + 1) * CH],
                                                W[:, 2:4, :].rearrange("p a b -> p (a b)"), start=True, stop=True)
                elif what == "T":
                    t, j = divmod(num, 3)
                    if j == 0:
                        pe.wait_ge(s.exp_done, 8 * b + t + 1)
                    for c in range(4):
                        cc = 4 * j + c
                        last = nc.tensor.transpose(G[0:CH, bank, c * TT:(c + 1) * TT],
                                                   PR[:, t % 2, cc * CH:(cc + 1) * CH], k.ident[0:TT, 0:TT])
                elif what == "O":
                    for c in range(NCH):
                        if c % 4 == 0:
                            at = plan.find(kind, "T", 12 * num + 9 + c // 4)
                            e = plan.engine(kind, at)
                            pe.wait_ge(s.emptied_a if e == A else s.emptied_d, plan.number(kind, b, at, e))
                            if c == 0:
                                e2 = A if e == D else D
                                pe.wait_ge(s.emptied_a if e2 == A else s.emptied_d,
                                           plan.number(kind, b, at, e2))
                        for g in range(4):
                            last = nc.tensor.matmul(G[32 * g:32 * g + 32, bank, 0:TT],
                                                    V[:, odd, c, num * P + 32 * g:num * P + 32 * g + 32],
                                                    PT[:, c, g, :], start=c == 0, stop=c == NCH - 1,
                                                    tile_position=(0, 32 * g))
                elif what == "R":
                    pe.wait_ge(s.tail_a, b + 1 if kind == "tail" else b)
                    for h in range(2):
                        last = nc.tensor.matmul(G[:, bank, h * Q:(h + 1) * Q],
                                                Am[:, 4 * h:4 * h + 4, :].rearrange("p a b -> p (a b)"),
                                                same_query, start=True, stop=True)
                elif what == "Y":
                    pe.wait_ge(s.tail_t, b + 1 if kind == "tail" else b)
                    for h in range(2):
                        for j in range(2):
                            last = nc.tensor.matmul(G[:, bank, 0:Q], W[:, 4 + h, :], Tm[:, h, j, :],
                                                    start=h + j == 0, stop=h + j == 2)
                last.then_inc(s.filled, 1)

            def prologue(slots):
                for i, (_, what, num, e) in slots:
                    slot(0, 0, "prologue", i, what, num)

            pe.wait_ge(s.w_loaded, 16)
            prologue(list(enumerate(plan.prologue))[:3])
            ln_pe(pe, k, s, S6)
            pe.wait_ge(s.ln_done, 2)
            for h in range(2):
                last = nc.tensor.matmul(S[:, 0, h, 0:HALF], W[:, 0, :], k.xnT[:, h * HALF:(h + 1) * HALF],
                                        start=True, stop=True)
            if name == "L0":
                for h in range(2):
                    last = nc.tensor.matmul(S[:, 1, 0, 0:1], W[:, 4 + h, :], k.v("L0_bv%d" % h),
                                            start=h == 0, stop=h == 1)
            last.then_inc(s.setup_pe, 1)
            prologue(list(enumerate(plan.prologue))[3:])

            pe.wait_ge(s.q_stacked, 16 * N_STACK)

            def batch(b, odd, kind):
                if kind == "first":
                    scores(b, odd, 0, True)
                    scores(b, odd, 1, True)
                for t in range(NT):
                    for n, (i, what, num, e) in enumerate(step_slots(plan, kind, t)):
                        slot(b, odd, kind, i, what, num)
                        if n == 0 and t < NT - 2:
                            scores(b, odd, t + 2, False)
                        elif n == 0 and kind != "last":
                            scores(b + 1, 1 - odd, t + 2 - NT, False)

            batches(pe, batch)
            for i, x in enumerate(plan.tail):
                slot(B - 1, 0, "tail", i, x[1], x[2])

        @block.gpsimd
        def _(pool):
            def prepare_mask(b, u):
                wait_context(pool, b, u)
                if not (isinstance(b, int) and b == 0):
                    pool.wait_ge(stacked[1 - u], 8 * N_STACK * (b + u))
                pool.sem_inc(s.carrier, 1)
                nc.gpsimd.tensor_scalar(MB[:], MR[0:1, u, :], -80.0, 80.0, ALU.mult, ALU.add
                                        ).then_inc(s.mask_ready, 1)
                if not (isinstance(b, int) and b == 0):
                    pool.wait_ge(s.parts_ready, SPLIT * b)
                    pool.sem_inc(s.carrier, 1)
                nc.gpsimd.tensor_scalar(MF[:], MR[:, u, :], 1.0, None, ALU.mult).then_inc(s.mask_ready, 1)
                pool.wait_ge(s.mask_ready, 2 * b + 2)

            def split(b, u, kind, at, num):
                if masked and not (isinstance(b, int) and b == 0):
                    prepare_mask(b, u)
                elif not (isinstance(b, int) and b == 0):
                    pool.wait_ge(stacked[1 - u], 8 * N_STACK * (b + u))
                pool.wait_ge(s.emptied_a, plan.number(kind, at, plan.find(kind, "K", num), A))
                if num == 5:
                    pool.wait_ge(s.emptied_d, plan.number(kind, at, plan.find(kind, "K", num), D))
                work = [(KF[:], KF[:], MF[:], ALU.mult)] if masked else []
                work += [(KP[:, 0], KF[:], None, None), (KF[:], KF[:], KP[:, 0], ALU.subtract),
                         (KP[:, 1], KF[:], None, None), (KP[:, 2], KF[:], KP[:, 1], ALU.subtract)]
                for n, (to, x, y, op) in enumerate(work):
                    if n:
                        pool.wait_ge(s.parts_ready, SPLIT * b + n)
                    if y is None and isinstance(b, int) and b == 0:
                        continue
                    if y is None:
                        pool.sem_inc(s.carrier, 1)
                        nc.gpsimd.tensor_scalar(to, x, 1.0, None, ALU.mult).then_inc(s.parts_ready, 1)
                    else:
                        nc.gpsimd.tensor_tensor(to, x, y, op).then_inc(s.parts_ready, 1)

            if masked:
                prepare_mask(0, 0)
            ln_pool(pool, k, s, [1e-5])
            if masked:
                nc.gpsimd.memset(MW[:], 125.0).then_inc(s.mask_weight, 1)
            split(0, 0, "prologue", 0, 2)
            split(1, 1, "prologue", 0, 5)
            split(2, 0, "first", 0, 2)
            with pool.Fori(0, (B - 2) // 2) as i:
                split(2 * i + 3, 1, "mid", 2 * i + 1, 2)
                split(2 * i + 4, 0, "mid", 2 * i + 2, 2)

        @block.scalar
        def _(act):
            def empty(b, odd, kind, i, what, num):
                bank = plan.bank(kind, odd, i)
                nu = 0 if kind == "prologue" else 1 - odd
                filled(act, kind, b, i)
                if what == "K":
                    keys_free(act, b, odd, kind, num)
                    keys, at = KF[:, num % 3 * 500:(num % 3 + 1) * 500], G[:, bank, 0:500]
                    if name == "L0":
                        ins = nc.scalar.activation(keys, at, ACT.Identity, bias=k.v("L0_bk"))
                    else:
                        ins = nc.scalar.copy(keys, at)
                elif what == "V":
                    ins = nc.scalar.copy(V[:, nu, 2 * num:2 * num + 2, :],
                                         G[0:CH, bank, :].rearrange("p (a b) -> p a b", a=2))
                elif what == "T":
                    t, j = divmod(num, 3)
                    ins = nc.scalar.copy(PT[:, 4 * j:4 * j + 4, t % 4, :],
                                         G[0:CH, bank, 0:HALF].rearrange("p (a b) -> p a b", a=4))
                ins.then_inc(s.emptied_a, 1)

            for i, (_, what, num, e) in enumerate(plan.prologue):
                if e == A:
                    empty(0, 0, "prologue", i, what, num)
                if (what, num) == ("K", 2):
                    act.wait_ge(s.emptied_a, plan.number("prologue", 0, i, A))
                    for part in range(2):
                        n = SPLIT - 4 + 2 * part
                        if n:
                            act.wait_ge(s.parts_ready, n)
                        nc.scalar.copy(KP[:, part], KF[:]).then_inc(s.parts_ready, 1)

            def exp(b, odd, t, kind):
                act.wait_ge(s.rowmax_ready, 8 * b + t + 1)
                if t >= 2:
                    act.wait_ge(s.filled, plan.number(kind, b, plan.find(kind, "T", 3 * t - 4)))
                elif kind != "first":
                    act.wait_ge(s.filled, plan.before("mid", b) - len(plan.mid) + 1 +
                                plan.find("mid", "T", 3 * t + 20))
                nc.scalar.activation(chunks(PR[:, t % 2, :]), S[0:TT, t % 2, :, 0:500], ACT.Exp,
                                     bias=nmax[:, odd, t:t + 1], scale=-1.0,
                                     accum_out=ssum[:, odd, t:t + 1]).then_inc(s.exp_done, 1)

            def batch(b, odd, kind):
                if kind == "first":
                    exp(b, odd, 0, kind)
                for t in range(NT):
                    if t < NT - 1:
                        exp(b, odd, t + 1, kind)
                    elif kind != "last":
                        exp(b + 1, 1 - odd, 0, "mid")
                    for i, what, num, e in step_slots(plan, kind, t):
                        if e == A:
                            empty(b, odd, kind, i, what, num)

            batches(act, batch)

        @block.vector
        def _(dve):
            link = Chain(dve, s.dve_chain)
            dve.wait_ge(s.w_loaded, 16)
            ln_dve(dve, k, s, S6, link, [1e-5])
            dve.wait_ge(s.setup_pe, 1)
            for h in range(2):
                o = qT[:, h * HALF:(h + 1) * HALF]
                if name == "L0":
                    nc.vector.tensor_scalar(o, S[:, 0, h, 0:HALF], k.v("L0_bq"), -scale, ALU.add, ALU.mult)
                else:
                    nc.vector.tensor_scalar(o, S[:, 0, h, 0:HALF], -scale, None, ALU.mult)
            if name == "L0":
                last = nc.vector.tensor_tensor(bout[:], S[:, 1, 0, 0:1], k.v("L0_bo"), ALU.add)
            else:
                last = nc.vector.tensor_copy(bout[:], k.v("L3_bo"))
            link(last)
            link(nc.vector.tensor_copy(QP[:, 0], qT[:]))
            link(nc.vector.tensor_tensor(qT[:], qT[:], QP[:, 0], ALU.subtract))
            link(nc.vector.tensor_copy(QP[:, 1], qT[:]))
            link(nc.vector.tensor_tensor(QP[:, 2], qT[:], QP[:, 1], ALU.subtract))
            for n in range(3):
                for j in range(2):
                    last = nc.vector.tensor_tensor(QM[:, n, :, j, :], QP[:, n].rearrange("p (b q) -> p b q", b=B),
                                                   head_mask[:, j:j + 1].unsqueeze(2).to_broadcast([P, B, Q]), ALU.mult)
                last.then_inc(s.q_split, 1)

            def rowmax(b, odd, t):
                dve.wait_ge(s.scores_ready, 8 * b + t + 1)
                nc.vector.tensor_reduce(nmax[:, odd, t:t + 1], S[0:TT, t % 2, :, 0:500], AX.XY,
                                        ALU.min).then_inc(s.rowmax_ready, 1)

            def empty(b, odd, kind, i, what, num):
                bank = plan.bank(kind, odd, i)
                nu = 0 if kind == "prologue" else 1 - odd
                tb = b if kind == "tail" else b - 1
                filled(dve, kind, b, i)
                if what == "K":
                    keys_free(dve, b, odd, kind, num)
                    keys, at = KF[:, num % 3 * 500:(num % 3 + 1) * 500], G[:, bank, 0:500]
                    if name == "L0":
                        ins = nc.vector.tensor_scalar(keys, at, k.v("L0_bk"), None, ALU.add)
                    else:
                        ins = nc.vector.tensor_copy(keys, at)
                elif what == "V":
                    ins = nc.vector.tensor_copy(V[:, nu, 2 * num:2 * num + 2, :],
                                                G[0:CH, bank, :].rearrange("p (a b) -> p a b", a=2))
                elif what == "T":
                    t, j = divmod(num, 3)
                    ins = nc.vector.tensor_copy(PT[:, 4 * j:4 * j + 4, t % 4, :],
                                                G[0:CH, bank, 0:HALF].rearrange("p (a b) -> p a b", a=4))
                elif what == "O":
                    ins = nc.vector.tensor_copy(OS[:, odd, num, :], G[:, bank, 0:TT])
                elif what == "R":
                    ins = nc.vector.tensor_tensor(
                        R4[:], G[:, bank, 0:TT].rearrange("p (h q) -> p h q", h=2).unsqueeze(2).to_broadcast([P, 2, 2, Q]),
                        pair_mask.unsqueeze(1).unsqueeze(3).to_broadcast([P, 2, 2, Q]), ALU.mult)
                elif what == "Y":
                    x = k.xT[:, bass.ds(tb * Q, Q)]
                    ins = nc.vector.scalar_tensor_tensor(x, G[:, bank, 0:Q], bout[:], x, ALU.add, ALU.add)
                ins.then_inc(s.emptied_d, 1)
                if what == "R":
                    dve.wait_ge(s.emptied_d, plan.number(kind, b, i, D))
                    nc.vector.tensor_tensor(Tm[:].rearrange("p h j q -> p (h j q)"),
                                            R4[:].rearrange("p h j q -> p (h j q)"),
                                            OS[:, 1 - odd, :, :].rearrange("p h r -> p (h r)"),
                                            ALU.mult).then_inc(s.tail_t, 1)

            def reciprocals(tb, odd):
                dve.wait_ge(s.exp_done, 8 * tb + 8)
                nc.vector.reciprocal(rinv[:], ssum[:, odd, :]).then_inc(s.tail_r, 1)
                dve.wait_ge(s.tail_r, tb + 1)
                nc.vector.tensor_tensor(Am[:], rinv[:].unsqueeze(2).to_broadcast([TT, 8, 32]),
                                        row_half.unsqueeze(1).to_broadcast([TT, 8, 32]),
                                        ALU.mult).then_inc(s.tail_a, 1)

            for i, (_, what, num, e) in enumerate(plan.prologue):
                if e == D:
                    empty(0, 0, "prologue", i, what, num)

            def batch(b, odd, kind):
                if kind != "first":
                    reciprocals(b - 1, 1 - odd)
                if kind == "first":
                    rowmax(b, odd, 0)
                    rowmax(b, odd, 1)
                for t in range(NT):
                    for n, (i, what, num, e) in enumerate(step_slots(plan, kind, t)):
                        if e == D:
                            empty(b, odd, kind, i, what, num)
                        if n == 0 and t < NT - 2:
                            rowmax(b, odd, t + 2)
                        elif n == 0 and kind != "last":
                            rowmax(b + 1, 1 - odd, t + 2 - NT)

            batches(dve, batch)
            reciprocals(B - 1, 1)
            for i, x in enumerate(plan.tail):
                empty(B - 1, 0, "tail", i, x[1], x[2])


def latent_attention(nc, k, src):
    name, D, A = "L1", "D", "A"
    KEYS, HD = S2 + Q, 64
    KCOL = KEYS // 4
    t1 = [(0, "T1", j, A) for j in range(3)]
    kv = [(0, "KV", j, D if j in (4, 5) else A) for j in range(6)]
    t2 = [(0, "T2", j, [D, A, D][j]) for j in range(3)]
    t3 = [(0, "T3", j, [A, D, A, A, D][j]) for j in range(5)]
    tail = [(0, "R", 0, D), (0, "Y", 0, D)]
    plan = Slots(t1 + kv + t2, t1 + kv + tail[:1] + t3 + tail[1:] + [(0, "O", 0, D)] + t2, ("R", "Y"), tail, ring=4)

    with ExitStack() as ctx:
        sb = lambda n, shape, dt=F32: ctx.enter_context(nc.sbuf_tensor(name + n, shape, dt))
        PS = ctx.enter_context(nc.psum_tensor(name + "ps", [P, 8, BANK], F32))
        G = PS[:, 4:8, :]
        s = semaphores(ctx, nc, name, LN_SEMS + " w_loaded ctx_loaded0 ctx_loaded1 mask_loaded0 mask_loaded1 filled "
                       "emptied_a emptied_d qk_filled qk_ss qk_rms qk_scaled qk_turned lat_v lat_done "
                       "stats_ready ctx_rms xh_done mv_kept squares ss_ready k_rms k_normed kl_ready vl_ready q_ready "
                       "mask_ready scores_ready rowmax_ready exp_done tail_r tail_a tail_t dve_chain "
                       "zeroed stats_a stats_b ss_a carrier")
        ctx_loaded = (s.ctx_loaded0, s.ctx_loaded1)
        mask_loaded = (s.mask_loaded0, s.mask_loaded1)
        W = sb("w", [P, 4, P])
        RAW = sb("raw", [CH, 2, NCH, P])
        XH = sb("xh", [CH, 2, NCH, P])
        XT = sb("xT1", [P, S2])
        KV = sb("kv", [CH, 2, NCH, 2 * P])
        SQ = sb("sq", [CH, NCH, P])
        KN = sb("kn", [CH, NCH, P])
        KT = sb("keysT", [P, 2, KEYS])
        Qd = sb("queries", [P, 2, 2, Q])
        MR = sb("mask", [TT, 2, S2], U8)
        MA = sb("maskadd", [TT, 2, KEYS])
        SM = sb("masked", [TT, KEYS])
        PR = sb("probs", [TT, KEYS])
        PT = sb("probsT", [CH, NCH + 1, TT])
        VL = sb("v_latent", [Q, 2, P])
        VLall = sb("v_latents", [Q, B, P])
        qT = sb("qT", [P, TOK])
        kT = sb("kT", [P, TOK])
        QK = sb("qk", [TT, 2, NTT, P])
        QK2 = sb("qk2", [TT, 2, NTT, P])
        ssq = sb("ssq", [TT, 32])
        rq = sb("rq", [TT, 32])
        st = sb("st", [CH, NCH, 6])
        mvb = sb("mvb", [CH, 2, NCH, 2])
        ve = sb("ve", [CH, 2, NCH])
        rs = sb("rs", [CH, NCH])
        ss = sb("ss", [CH, 24])
        rk = sb("rk", [CH, 24])
        ssum = sb("sums", [TT, 2])
        nmax = sb("negmax", [TT, 2])
        rinv = sb("rinv", [TT, 1])
        Am = sb("rinv_spread", [TT, 2, HD])
        OS = sb("osum", [P, 2, TT])
        R = sb("r", [P, Q])
        Tm = sb("heads_out", [P, Q])
        head_mask = k.const[:, C_HALF:C_HALF + 2]
        row_half = k.const[0:TT, C_J2:C_J2 + 2]
        same_query = k.const[0:TT, C_QSEL:C_QSEL + Q]
        banks = lambda ap: ap.rearrange("p (c n) -> p c n", c=4)

        def batches(eng, do):
            do(0, 0, "first", True)
            with eng.Fori(0, 6) as i:
                do(2 * i + 1, 1, "mid", True)
                do(2 * i + 2, 0, "mid", True)
            do(13, 1, "mid", True)
            do(14, 0, "mid", False)
            do(15, 1, "last", False)

        loads = lambda b, u: 8 * (b + 2 - u)

        block = ctx.enter_context(nc.Block())

        @block.sync
        def _(sp):
            sp.dma_start(W[:], src["L1_attn_w"]).then_inc(s.w_loaded, 16)

            def load(b, u):
                sp.dma_start(RAW[:, u], src["ctx"][b]).then_inc(ctx_loaded[u], 16)
                sp.dma_start(MR[:, u, :], src["mask_some"][b].partition_broadcast(TT)).then_inc(mask_loaded[u], 16)

            def reload(b, u):
                sp.wait_ge(s.xh_done, b - 1)
                sp.sem_inc(s.carrier, 1)
                sp.wait_ge(s.mask_ready, b - 1)
                sp.sem_inc(s.carrier, 1)
                load(b, u)

            load(0, 0)
            load(1, 1)
            with sp.Fori(1, B // 2) as i:
                reload(2 * i, 0)
                reload(2 * i + 1, 1)

        @block.tensor
        def _(pe):
            pe.wait_ge(s.w_loaded, 16)
            ln_pe(pe, k, s, PS)
            pe.wait_ge(s.ln_done, 2)
            for w in range(2):
                for t in range(NTT):
                    last = nc.tensor.matmul(PS[0:TT, 4 + 2 * w + t // 4, (t % 4) * P:(t % 4 + 1) * P],
                                            k.xnT[:, t * TT:(t + 1) * TT], W[:, w, :], start=True, stop=True)
                last.then_inc(s.qk_filled, 1)
            for b in range(B):
                last = nc.tensor.matmul(PS[0:Q, b // 4, (b % 4) * P:(b % 4 + 1) * P],
                                        k.xnT[:, b * Q:(b + 1) * Q], W[:, 2, :], start=True, stop=True)
            last.then_inc(s.lat_v, 1)
            pe.wait_ge(s.qk_scaled, 1)
            for w in range(2):
                for t in range(NTT):
                    last = nc.tensor.transpose(PS[:, 4 + 2 * w + t // 4, (t % 4) * TT:(t % 4 + 1) * TT],
                                               QK[:, w, t, :], k.ident[0:TT, 0:TT])
                last.then_inc(s.qk_turned, 1)
            pe.wait_ge(s.lat_done, 1)

            def slot(b, odd, kind, i, what, num):
                bank = plan.bank(kind, odd, i)
                if kind != "prologue" or i >= 4:
                    e = plan.engine(kind, i - 4)
                    pe.wait_ge(s.emptied_a if e == A else s.emptied_d, plan.number(kind, b, i - 4, e))
                nb, nu = (0, 0) if kind == "prologue" else (b + 1, 1 - odd)
                if what == "T1":
                    if num == 0:
                        pe.wait_ge(s.xh_done, nb + 1)
                    for c in range(4):
                        last = nc.tensor.transpose(G[:, bank, c * CH:(c + 1) * CH], XH[:, nu, 4 * num + c, :],
                                                   k.ident[0:CH, 0:CH])
                elif what == "KV":
                    if num == 0:
                        pe.wait_ge(s.emptied_a, plan.number(kind, b, i - 1, A))
                        pe.wait_ge(s.emptied_d, plan.number(kind, b, i - 1, D))
                    for j in range(2):
                        c = 2 * num + j
                        last = nc.tensor.matmul(G[0:CH, bank, j * 256:(j + 1) * 256], XT[:, c * CH:(c + 1) * CH],
                                                W[:, 1:3, :].rearrange("p a b -> p (a b)"), start=True, stop=True)
                elif what == "T2":
                    if num == 0:
                        pe.wait_ge(s.k_normed, nb + 1)
                    for c in range(4):
                        last = nc.tensor.transpose(G[:, bank, c * CH:(c + 1) * CH], KN[:, 4 * num + c, :],
                                                   k.ident[0:CH, 0:CH])
                elif what == "T3":
                    if num == 0:
                        pe.wait_ge(s.exp_done, b + 1)
                    if num < 4:
                        for c in range(3):
                            cc = 3 * num + c
                            last = nc.tensor.transpose(G[0:CH, bank, c * TT:(c + 1) * TT],
                                                       PR[:, cc * CH:(cc + 1) * CH], k.ident[0:TT, 0:TT])
                    else:
                        pe.sem_inc(s.carrier, 1)
                        last = nc.tensor.transpose(G[0:Q, bank, 0:TT], PR[:, S2:KEYS], k.ident[0:TT, 0:TT])
                elif what == "O":
                    pe.wait_ge(s.emptied_a, plan.number(kind, b, i - 1, A))
                    pe.wait_ge(s.emptied_d, plan.number(kind, b, i - 1, D))
                    pe.wait_ge(s.vl_ready, b + 1)
                    for c in range(NCH):
                        nc.tensor.matmul(G[:, bank, 0:TT], KV[:, odd, c, P:2 * P], PT[:, c, :],
                                         start=c == 0, stop=False)
                    last = nc.tensor.matmul(G[:, bank, 0:TT], VL[:, odd, :], PT[0:Q, NCH, :], start=False, stop=True)
                elif what == "R":
                    pe.wait_ge(s.tail_a, b + 1 if kind == "tail" else b)
                    last = nc.tensor.matmul(G[:, bank, 0:Q], Am[:].rearrange("p a b -> p (a b)"), same_query,
                                            start=True, stop=True)
                elif what == "Y":
                    pe.wait_ge(s.tail_t, b + 1 if kind == "tail" else b)
                    last = nc.tensor.matmul(G[:, bank, 0:Q], W[:, 3, :], Tm[:], start=True, stop=True)
                last.then_inc(s.filled, 1)

            for i, (_, what, num, e) in enumerate(plan.prologue):
                slot(0, 0, "prologue", i, what, num)

            def batch(b, odd, kind, ahead):
                pe.wait_ge(s.emptied_a, plan.before(kind, b, A))
                pe.wait_ge(s.emptied_d, plan.before(kind, b, D))
                pe.wait_ge(s.kl_ready, b + 1)
                pe.wait_ge(s.q_ready, b + 1)
                if kind != "first":
                    pe.wait_ge(s.rowmax_ready, b)
                for c in range(4):
                    last = nc.tensor.matmul(PS[0:TT, c, 0:KCOL], Qd[:, odd].rearrange("p h q -> p (h q)"),
                                            KT[:, odd, c * KCOL:(c + 1) * KCOL], start=True, stop=True)
                last.then_inc(s.scores_ready, 1)
                for i, what, num, e in step_slots(plan, kind, 0):
                    slot(b, odd, kind, i, what, num)

            batches(pe, batch)
            for i, x in enumerate(plan.tail):
                slot(B - 1, 0, "tail", i, x[1], x[2])

        @block.gpsimd
        def _(pool):
            ln_pool(pool, k, s, [1e-5, 1e-5])
            nc.gpsimd.memset(MA[:, :, S2:KEYS], 0.0).then_inc(s.zeroed, 1)
            pool.wait_ge(s.zeroed, 1)

            def deviations(b, u, again):
                pool.wait_ge(s.stats_ready, b + 1)
                if again:
                    pool.wait_ge(s.xh_done, b)
                nc.gpsimd.tensor_tensor(rs[:], ve[:, u, :], k.half_neg[0:CH, 0:NCH], ALU.pow).then_inc(s.ctx_rms, 1)
                nc.gpsimd.tensor_copy(k.ctx_mv[:, bass.ds(b, 1)].rearrange("p a c n -> p (a c n)"),
                                      mvb[:, u].rearrange("p c n -> p (c n)")).then_inc(s.mv_kept, 1)

            def operands(b, u, again):
                if again:
                    pool.wait_ge(s.scores_ready, b - 1)
                nc.gpsimd.tensor_tensor(Qd[:, u], qT[:, bass.ds(b * Q, Q)].unsqueeze(1).to_broadcast([P, 2, Q]),
                                        head_mask.unsqueeze(2).to_broadcast([P, 2, Q]), ALU.mult).then_inc(s.q_ready, 1)
                nc.gpsimd.tensor_copy(KT[:, u, S2:KEYS], kT[:, bass.ds(b * Q, Q)]).then_inc(s.kl_ready, 1)
                pool.wait_ge(mask_loaded[u], loads(b, u))
                if again:
                    pool.wait_ge(s.rowmax_ready, b - 1)
                pool.sem_inc(s.carrier, 1)
                nc.gpsimd.tensor_scalar(MA[:, u, 0:S2], MR[:, u, :], -1.0, -FLT_MAX, ALU.add,
                                        ALU.mult).then_inc(s.mask_ready, 1)

            def key_deviations(b):
                pool.wait_ge(s.ss_ready, b + 1)
                nc.gpsimd.tensor_tensor(rk[:], ss[:], k.half_neg[0:CH, 0:24], ALU.pow).then_inc(s.k_rms, 1)

            def latent_values(b, u):
                nc.gpsimd.tensor_copy(VL[:, u, :], VLall[:, bass.ds(b, 1), :].rearrange("p a n -> p (a n)")
                                      ).then_inc(s.vl_ready, 1)

            deviations(0, 0, False)
            pool.wait_ge(s.qk_ss, 1)
            nc.gpsimd.tensor_tensor(rq[:], ssq[:], k.half_neg[0:TT, 0:32], ALU.pow).then_inc(s.qk_rms, 1)
            deviations(1, 1, True)
            pool.wait_ge(s.lat_done, 1)
            operands(0, 0, False)
            operands(1, 1, False)
            latent_values(0, 0)
            key_deviations(0)

            def batch(b, odd, kind, ahead):
                if kind != "last":
                    pool.wait_ge(s.filled, plan.before(kind, b))
                if ahead:
                    deviations(b + 2, odd, True)
                if kind != "last":
                    key_deviations(b + 1)
                    latent_values(b + 1, 1 - odd)
                if ahead:
                    operands(b + 2, odd, True)

            batches(pool, batch)

        @block.scalar
        def _(act):
            def empty(b, odd, kind, i, what, num):
                bank = plan.bank(kind, odd, i)
                nu = 0 if kind == "prologue" else 1 - odd
                act.wait_ge(s.filled, plan.number(kind, b, i))
                if what == "T1":
                    ins = nc.scalar.activation(XT[:, num * 500:(num + 1) * 500], G[:, bank, 0:500], ACT.Identity,
                                               bias=k.v("L1_xb"), scale=k.v("L1_xg"))
                elif what == "KV":
                    ins = nc.scalar.copy(KV[:, nu, 2 * num:2 * num + 2, :],
                                         G[0:CH, bank, :].rearrange("p (a b) -> p a b", a=2))
                elif what == "T2":
                    ins = nc.scalar.mul(KT[:, nu, num * 500:(num + 1) * 500], G[:, bank, 0:500], k.v("L1_kg"))
                elif what == "T3":
                    ins = nc.scalar.copy(PT[:, 3 * num:3 * num + 3, :],
                                         G[0:CH, bank, 0:3 * TT].rearrange("p (a b) -> p a b", a=3))
                ins.then_inc(s.emptied_a, 1)

            def key_squares(b, u, kind, at):
                i = plan.find(kind, "KV", 5)
                act.wait_ge(s.emptied_a, plan.number(kind, at, i, A))
                act.wait_ge(s.emptied_d, plan.number(kind, at, i, D))
                if not (isinstance(b, int) and b == 0):
                    act.wait_ge(s.ss_a, b)
                nc.scalar.activation(SQ[:], KV[:, u, :, 0:P], ACT.Square).then_inc(s.squares, 1)

            for i, (_, what, num, e) in enumerate(plan.prologue):
                if what == "T2" and num == 0:
                    key_squares(0, 0, "prologue", 0)
                if e == A:
                    empty(0, 0, "prologue", i, what, num)

            def batch(b, odd, kind, ahead):
                for i, what, num, e in step_slots(plan, kind, 0):
                    if e == A and what == "T1":
                        empty(b, odd, kind, i, what, num)
                act.wait_ge(s.rowmax_ready, b + 1)
                nc.scalar.activation(PR[:], SM[:], ACT.Exp, bias=nmax[:, odd:odd + 1], scale=-1.0,
                                     accum_out=ssum[:, odd:odd + 1]).then_inc(s.exp_done, 1)
                for i, what, num, e in step_slots(plan, kind, 0):
                    if e == A and what != "T1":
                        empty(b, odd, kind, i, what, num)
                    if what == "KV" and num == 5:
                        key_squares(b + 1, 1 - odd, kind, b)

            batches(act, batch)

        @block.vector
        def _(dve):
            def stats(b, u, again):
                dve.wait_ge(ctx_loaded[u], loads(b, u))
                if again:
                    dve.wait_ge(s.mv_kept, b - 1)
                for c in range(NCH):
                    last = nc.vector.bn_stats(st[:, c, :], RAW[:, u, c, :])
                last.then_inc(s.stats_a, 1)
                dve.wait_ge(s.stats_a, b + 1)
                dve.sem_inc(s.carrier, 1)
                for c in range(NCH):
                    last = nc.vector.bn_aggr(mvb[:, u, c, :], st[:, c, :])
                last.then_inc(s.stats_b, 1)
                dve.wait_ge(s.stats_b, b + 1)
                nc.vector.tensor_scalar(ve[:, u, :], mvb[:, u, :, 1], 1e-5, None, ALU.add).then_inc(s.stats_ready, 1)

            def normalise(b, u):
                dve.wait_ge(s.ctx_rms, b + 1)
                for c in range(NCH):
                    last = nc.vector.tensor_scalar(XH[:, u, c, :], RAW[:, u, c, :], mvb[:, u, c, 0:1], rs[:, c:c + 1],
                                                   ALU.subtract, ALU.mult)
                last.then_inc(s.xh_done, 1)

            link = Chain(dve, s.dve_chain)
            ln_dve(dve, k, s, PS, link, [1e-5, 1e-5], k.v("L1_lg"), k.v("L1_lb"))
            stats(0, 0, False)
            dve.wait_ge(s.qk_filled, 2)
            link(nc.vector.tensor_copy(QK[:].rearrange("p w t n -> p (w t n)"),
                                       G[0:TT].rearrange("p a n -> p (a n)")))
            link(nc.vector.tensor_tensor(QK2[:], QK[:], QK[:], ALU.mult))
            link(nc.vector.tensor_reduce(ssq[:], QK2[:].rearrange("p w t (h d) -> p (w t h) d", h=2), AX.X, ALU.add))
            nc.vector.tensor_scalar(ssq[:], ssq[:], 1.0 / HD, 1e-16, ALU.mult, ALU.max).then_inc(s.qk_ss, 1)
            dve.wait_ge(s.lat_v, 1)
            for n in range(4):
                last = nc.vector.tensor_copy(VLall[:, 4 * n:4 * n + 4, :].rearrange("p a n -> p (a n)"), PS[0:Q, n, :])
            link(last)
            normalise(0, 0)
            dve.wait_ge(s.qk_rms, 1)
            nc.vector.tensor_tensor(QK[:].rearrange("p w t (h d) -> p (w t h) d", h=2),
                                    QK[:].rearrange("p w t (h d) -> p (w t h) d", h=2),
                                    rq[:].unsqueeze(2).to_broadcast([TT, 32, HD]), ALU.mult).then_inc(s.qk_scaled, 1)
            stats(1, 1, False)
            dve.wait_ge(s.qk_turned, 2)
            for h in range(2):
                o = slice(h * HALF, (h + 1) * HALF)
                nc.vector.tensor_scalar(qT[:, o], PS[:, 4 + h, 0:HALF], k.v("L1_qg"), -HD ** -0.5, ALU.mult, ALU.mult)
                last = nc.vector.tensor_scalar(kT[:, o], PS[:, 6 + h, 0:HALF], k.v("L1_kg"), None, ALU.mult)
            last.then_inc(s.lat_done, 1)

            def empty(b, odd, kind, i, what, num):
                bank = plan.bank(kind, odd, i)
                nu = 0 if kind == "prologue" else 1 - odd
                tb = b if kind == "tail" else b - 1
                dve.wait_ge(s.filled, plan.number(kind, b, i))
                if what == "T1":
                    ins = nc.vector.tensor_scalar(XT[:, num * 500:(num + 1) * 500], G[:, bank, 0:500],
                                                  k.v("L1_xg"), k.v("L1_xb"), ALU.mult, ALU.add)
                elif what == "KV":
                    ins = nc.vector.tensor_copy(KV[:, nu, 2 * num:2 * num + 2, :],
                                                G[0:CH, bank, :].rearrange("p (a b) -> p a b", a=2))
                elif what == "T2":
                    ins = nc.vector.tensor_scalar(KT[:, nu, num * 500:(num + 1) * 500], G[:, bank, 0:500],
                                                  k.v("L1_kg"), None, ALU.mult)
                elif what == "T3" and num < 4:
                    ins = nc.vector.tensor_copy(PT[:, 3 * num:3 * num + 3, :],
                                                G[0:CH, bank, 0:3 * TT].rearrange("p (a b) -> p a b", a=3))
                elif what == "T3":
                    ins = nc.vector.tensor_copy(PT[0:Q, NCH, :], G[0:Q, bank, 0:TT])
                elif what == "O":
                    ins = nc.vector.tensor_copy(OS[:, odd, :], G[:, bank, 0:TT])
                elif what == "R":
                    ins = nc.vector.tensor_copy(R[:], G[:, bank, 0:Q])
                elif what == "Y":
                    x = k.xT[:, bass.ds(tb * Q, Q)]
                    ins = nc.vector.scalar_tensor_tensor(x, G[:, bank, 0:Q], k.v("L1_bout"), x, ALU.add, ALU.add)
                ins.then_inc(s.emptied_d, 1)
                if what == "R":
                    dve.wait_ge(s.emptied_d, plan.number(kind, b, i, D))
                    for h in range(2):
                        p = slice(h * HD, (h + 1) * HD)
                        last = nc.vector.tensor_tensor(Tm[p, :], OS[p, 1 - odd, h * Q:(h + 1) * Q], R[p, :], ALU.mult)
                    last.then_inc(s.tail_t, 1)

            def reciprocals(tb, odd):
                dve.wait_ge(s.exp_done, tb + 1)
                nc.vector.reciprocal(rinv[:], ssum[:, odd:odd + 1]).then_inc(s.tail_r, 1)
                dve.wait_ge(s.tail_r, tb + 1)
                nc.vector.tensor_scalar(Am[:], row_half.unsqueeze(2).to_broadcast([TT, 2, HD]), rinv[:], None,
                                        ALU.mult).then_inc(s.tail_a, 1)

            def key_sums(b, u):
                dve.wait_ge(s.squares, b + 1)
                nc.vector.tensor_reduce(ss[:], SQ[:].rearrange("p c (h d) -> p (c h) d", h=2), AX.X,
                                        ALU.add).then_inc(s.ss_a, 1)
                dve.wait_ge(s.ss_a, b + 1)
                nc.vector.tensor_scalar(ss[:], ss[:], 1.0 / HD, 1e-16, ALU.mult, ALU.max).then_inc(s.ss_ready, 1)

            def key_norm(b, u):
                dve.wait_ge(s.k_rms, b + 1)
                for h in range(2):
                    last = nc.vector.tensor_tensor(KN[:, :, h * HD:(h + 1) * HD], KV[:, u, :, h * HD:(h + 1) * HD],
                                                   rk[:].rearrange("p (c h) -> p c h", h=2)[:, :, h:h + 1].to_broadcast([CH, NCH, HD]),
                                                   ALU.mult)
                last.then_inc(s.k_normed, 1)

            for i, (_, what, num, e) in enumerate(plan.prologue):
                if what == "KV" and num == 4:
                    normalise(1, 1)
                if what == "T2" and num == 0:
                    key_sums(0, 0)
                    key_norm(0, 0)
                if e == D:
                    empty(0, 0, "prologue", i, what, num)

            def batch(b, odd, kind, ahead):
                dve.wait_ge(s.scores_ready, b + 1)
                dve.wait_ge(s.mask_ready, b + 1)
                if kind != "first":
                    dve.wait_ge(s.exp_done, b)
                dve.sem_inc(s.carrier, 1)
                nc.vector.tensor_tensor_reduce(banks(SM[:]), PS[0:TT, 0:4, 0:KCOL], banks(MA[:, odd, :]),
                                               1.0, FLT_MAX, ALU.add, ALU.min,
                                               nmax[:, odd:odd + 1]).then_inc(s.rowmax_ready, 1)
                if kind != "first":
                    reciprocals(b - 1, 1 - odd)
                for i, what, num, e in step_slots(plan, kind, 0):
                    if what == "T3" and num == 0 and kind != "last":
                        key_sums(b + 1, 1 - odd)
                    if what == "O" and ahead:
                        normalise(b + 2, odd)
                    if what == "O" and kind != "last":
                        key_norm(b + 1, 1 - odd)
                    if e == D:
                        empty(b, odd, kind, i, what, num)
                    if what == "T1" and num == 2 and ahead:
                        stats(b + 2, odd, True)

            batches(dve, batch)
            reciprocals(B - 1, 1)
            for i, x in enumerate(plan.tail):
                empty(B - 1, 0, "tail", i, x[1], x[2])


def wide_heads_setup(nc, k, src, QZ, WVO, NN, NVO):
    name, H, HD = "L2s", 16, 64
    SCALE = H ** -0.5
    with ExitStack() as ctx:
        sb = lambda n, shape, dt=F32: ctx.enter_context(nc.sbuf_tensor(name + n, shape, dt))
        ps = ctx.enter_context(nc.psum_tensor(name + "ps", [P, 8, BANK], F32))
        s = semaphores(ctx, nc, name, LN_SEMS + " w_loaded n_loaded folded_filled folded_ready wn_filled wn_ready "
                       "xd_ready nn_filled nn_done nv_filled nv_ready nvo_stored q_filled q_act q_dve dve_chain")
        W = sb("w", [HD, 4, H, P])
        NKV = sb("nkv", [HD, 2])
        WQK = sb("wqk", [P, H, P])
        WN = sb("wn", [P, H])
        XD = sb("xd", [P, B, 2, Q])
        NM = sb("nm", [TT, B * 8, 2])
        NV = sb("nv", [1, H * P])
        row_half = k.const[0:TT, C_J2:C_J2 + 2]
        block = ctx.enter_context(nc.Block())

        @block.sync
        def _(sp):
            sp.dma_start(W[:], src["L2_attn_w"]).then_inc(s.w_loaded, 16)
            sp.dma_start(NKV[:], src["L2_null"]).then_inc(s.n_loaded, 16)
            sp.wait_ge(s.nv_ready, 4)
            sp.dma_start(NVO[:], NV[:].rearrange("a (t n) -> a t n", t=8)).then_inc(s.nvo_stored, 16)
            sp.wait_ge(s.nvo_stored, 16)

        @block.gpsimd
        def _(pool):
            ln_pool(pool, k, s, [1e-5, 1e-6])
            pool.wait_ge(s.ln_done, 2)
            nc.gpsimd.tensor_copy(XD[:], k.xnT[:].rearrange("p (b q) -> p b q", b=B).unsqueeze(2).to_broadcast([P, B, 2, Q])
                                  ).then_inc(s.xd_ready, 1)

        @block.tensor
        def _(pe):
            ln_pe(pe, k, s, ps, feature_major=False)
            pe.wait_ge(s.w_loaded, 16)
            for f in range(2):
                for g in range(4):
                    n = 4 * f + g
                    if n >= 4:
                        pe.wait_ge(s.folded_ready, n - 3)
                    for h in range(4 * g, 4 * g + 4):
                        last = nc.tensor.matmul(ps[:, 4 + n % 4, (h % 4) * P:(h % 4 + 1) * P],
                                                W[:, 2 * f, h, :], W[:, 2 * f + 1, h, :], start=True, stop=True)
                    last.then_inc(s.folded_filled, 1)
            ln_turn(pe, k, s, ps)
            pe.wait_ge(s.n_loaded, 16)
            for h in range(H):
                last = nc.tensor.matmul(ps[:, 0, h:h + 1], W[:, 0, h, :], NKV[:, 0:1], start=True, stop=True)
            last.then_inc(s.wn_filled, 1)
            for g in range(4):
                if g == 1:
                    pe.wait_ge(s.wn_ready, 1)
                if g >= 2:
                    pe.wait_ge(s.nv_ready, g - 1)
                nc.tensor.matmul(ps[0:1, 1 - g % 2, :], NKV[:, 1:2], W[:, 3, 4 * g:4 * g + 4, :].rearrange("p h n -> p (h n)"),
                                 start=True, stop=True).then_inc(s.nv_filled, 1)
            pe.wait_ge(s.folded_ready, 8)
            pe.wait_ge(s.ln_done, 2)
            for h in range(H):
                for x in range(2):
                    n = 2 * h + x
                    if n >= 4:
                        pe.wait_ge(s.q_dve if x else s.q_act, h - 1)
                    nc.tensor.matmul(ps[:, 4 + n % 4, 0:HALF], WQK[:, h, :], k.xnT[:, x * HALF:(x + 1) * HALF],
                                     start=True, stop=True).then_inc(s.q_filled, 1)
            pe.wait_ge(s.xd_ready, 1)
            for b in range(B):
                last = nc.tensor.matmul(ps[0:TT, 2, b * H:(b + 1) * H], XD[:, b].rearrange("p j q -> p (j q)"), WN[:],
                                        start=True, stop=True)
            last.then_inc(s.nn_filled, 1)

        @block.scalar
        def _(act):
            for n in range(8):
                act.wait_ge(s.folded_filled, n + 1)
                to = WQK if n < 4 else WVO
                nc.scalar.copy(to[:, 4 * (n % 4):4 * (n % 4) + 4, :].rearrange("p h n -> p (h n)"),
                               ps[:, 4 + n % 4, :]).then_inc(s.folded_ready, 1)
            act.wait_ge(s.wn_filled, 1)
            nc.scalar.mul(WN[:], ps[:, 0, 0:H], -SCALE).then_inc(s.wn_ready, 1)
            for g in range(4):
                act.wait_ge(s.nv_filled, g + 1)
                nc.scalar.copy(NV[:, g * BANK:(g + 1) * BANK], ps[0:1, 1 - g % 2, :]).then_inc(s.nv_ready, 1)
            for h in range(H):
                act.wait_ge(s.q_filled, 2 * h + 1)
                nc.scalar.mul(QZ[:, 0:8, h, :], ps[:, 4 + 2 * h % 4, 0:HALF].rearrange("p (b q) -> p b q", b=8),
                              -SCALE).then_inc(s.q_act, 1)

        @block.vector
        def _(dve):
            link = Chain(dve, s.dve_chain)
            ln_dve(dve, k, s, ps, link, [1e-5, 1e-6], k.v("L2_1s"), k.v("L2_1b"))
            for h in range(H):
                dve.wait_ge(s.q_filled, 2 * h + 2)
                nc.vector.tensor_scalar(QZ[:, 8:16, h, :], ps[:, 4 + (2 * h + 1) % 4, 0:HALF].rearrange("p (b q) -> p b q", b=8),
                                        -SCALE, None, ALU.mult).then_inc(s.q_dve, 1)
            dve.wait_ge(s.nn_filled, 1)
            link(nc.vector.tensor_tensor(NM[:], ps[0:TT, 2, 0:B * H].rearrange("p (a j) -> p a j", j=2),
                                         row_half.unsqueeze(1).to_broadcast([TT, B * 8, 2]), ALU.mult))
            nc.vector.tensor_reduce(NN[:], NM[:], AX.X, ALU.add).then_inc(s.nn_done, 1)


def wide_heads(nc, k, src, QZ, NN, PN):
    name, D, A = "L2", "D", "A"
    prep = [(3, "K", 0, A), (4, "K", 1, A), (5, "K", 2, A)]
    tail = [("R", 0), ("R", 1), ("R", 2), ("R", 3), ("N", 0)]
    steps = []
    for t in range(NT):
        steps.append((t, "T", 3 * t, D))
        if 3 <= t < 7:
            steps.append((t, "R", t - 3, D))
        if t == 7:
            steps.append((t, "N", 0, D))
        steps.append((t, "T", 3 * t + 1, A))
        steps += [p for p in prep if p[0] == t]
        steps.append((t, "T", 3 * t + 2, A))
        if t in (3, 7):
            steps.append((t, "O", t // 4, D))
    plan = Slots([(0, "K", 0, D), (0, "K", 1, A), (0, "K", 2, D)], steps, ("R", "N"),
                 [(0, w, n, D) for w, n in tail])
    with ExitStack() as ctx:
        sb = lambda n, shape, dt=F32: ctx.enter_context(nc.sbuf_tensor(name + n, shape, dt))
        S = ctx.enter_context(nc.psum_tensor(name + "scores", [P, 2, 3, BANK], F32))
        G = ctx.enter_context(nc.psum_tensor(name + "ring", [P, 2, BANK], F32))
        s = semaphores(ctx, nc, name, "ctx_loaded mask_loaded0 mask_loaded1 b_loaded filled emptied_a "
                       "emptied_d scores_ready rowmax_ready exp_done mask_ready nn_ready values_ready rs_ready "
                       "ve_ready null_shift null_exp tail_sums tail_r tail_w tail_pn diag_ready z_done "
                       "q_ready pool_chain carrier")
        RAW = sb("raw", [CH, NCH, P])
        V = sb("values", [CH, 2, NCH, P])
        KT = sb("keys", [P, 2, S2])
        Qb = sb("queries", [P, 2, 16, Q])
        PR = sb("probs", [TT, 2, S2])
        PT = sb("probsT", [CH, NCH, 4, TT])
        MR = sb("mask", [TT, 2, S2], U8)
        MA = sb("maskadd", [TT, 2, S2])
        SM = sb("masked", [TT, 2, S2])
        OS = sb("osum", [P, 2, 2, HALF])
        cs = sb("cs", [TT, P])
        cb = sb("cb", [TT, P])
        rs = sb("rs", [CH, B, NCH])
        nneg = sb("nneg", [TT, 2, NT])
        ssum = sb("sums", [TT, 2, NT])
        nmax = sb("negmax", [TT, 2, NT])
        en = sb("en", [TT, NT])
        tot = sb("tot", [TT, NT])
        rinv = sb("rinv", [TT, NT])
        wc = sb("wc", [TT, NT])
        pn = sb("pn", [TT, NT])
        DG = sb("diag", [TT, 2, NT, TT])
        ZS = sb("zs", [P, 2, HALF])
        chunks = lambda ap: ap.rearrange("p (c n) -> p c n", c=3)
        mask_loaded = (s.mask_loaded0, s.mask_loaded1)
        loads = lambda b, u: 8 * (b + 2 - u)
        block = ctx.enter_context(nc.Block())

        @block.sync
        def _(sp):
            sp.dma_start(cs[:], src["L2_cs_row"].partition_broadcast(TT)).then_inc(s.b_loaded, 16)
            sp.dma_start(cb[:], src["L2_cb_row"].partition_broadcast(TT)).then_inc(s.b_loaded, 16)

            def load(b, u):
                sp.dma_start(MR[:, u, :], src["mask_full"][b].partition_broadcast(TT)).then_inc(mask_loaded[u], 16)

            def load_context(b):
                sp.dma_start(RAW[:], src["ctx"][b]).then_inc(s.ctx_loaded, 16)

            def reload(b, u):
                sp.wait_ge(s.values_ready, b)
                sp.sem_inc(s.carrier, 1)
                load_context(b)
                sp.wait_ge(s.mask_ready, b - 1)
                sp.sem_inc(s.carrier, 1)
                load(b, u)

            load_context(0)
            load(0, 0)
            load(1, 1)
            sp.wait_ge(s.values_ready, 1)
            load_context(1)
            with sp.Fori(1, B // 2) as i:
                reload(2 * i, 0)
                reload(2 * i + 1, 1)

        @block.tensor
        def _(pe):
            def scores(b, odd, t, early):
                if t == 0:
                    pe.wait_ge(s.q_ready, b + 1)
                if not early:
                    pe.wait_ge(s.rowmax_ready, 8 * b + t - 1)
                for c in range(3):
                    last = nc.tensor.matmul(S[0:TT, t % 2, c, 0:500],
                                            Qb[:, odd, 2 * t:2 * t + 2, :].rearrange("p h q -> p (h q)"),
                                            KT[:, odd, c * 500:(c + 1) * 500], start=True, stop=True)
                last.then_inc(s.scores_ready, 1)

            def slot(b, odd, kind, i, what, num):
                bank = plan.bank(kind, odd, i)
                if kind != "prologue" or i >= 2:
                    e = plan.engine(kind, i - 2)
                    pe.wait_ge(s.emptied_a if e == A else s.emptied_d, plan.number(kind, b, i - 2, e))
                nb, nu = (0, 0) if kind == "prologue" else (b + 1, 1 - odd)
                after = b + 1 if kind == "tail" else b
                if what == "K":
                    if num == 0:
                        pe.wait_ge(s.values_ready, nb + 1)
                    for c in range(4):
                        last = nc.tensor.transpose(G[:, bank, c * CH:(c + 1) * CH], V[:, nu, 4 * num + c, :],
                                                   k.ident[0:CH, 0:CH])
                elif what == "T":
                    t, j = divmod(num, 3)
                    if j == 0:
                        pe.wait_ge(s.exp_done, 8 * b + t + 1)
                    for c in range(4):
                        cc = 4 * j + c
                        last = nc.tensor.transpose(G[0:CH, bank, c * TT:(c + 1) * TT],
                                                   PR[:, t % 2, cc * CH:(cc + 1) * CH], k.ident[0:TT, 0:TT])
                elif what == "O":
                    for c in range(NCH):
                        if c % 4 == 0:
                            at = plan.find(kind, "T", 12 * num + 9 + c // 4)
                            e = plan.engine(kind, at)
                            pe.wait_ge(s.emptied_a if e == A else s.emptied_d, plan.number(kind, b, at, e))
                            if c == 0:
                                e2 = A if e == D else D
                                pe.wait_ge(s.emptied_a if e2 == A else s.emptied_d,
                                           plan.number(kind, b, at, e2))
                        last = nc.tensor.matmul(G[:, bank, 0:HALF], V[:, odd, c, :],
                                                PT[:, c].rearrange("p a n -> p (a n)"),
                                                start=c == 0, stop=c == NCH - 1)
                elif what == "R":
                    h, w = divmod(num, 2)
                    if num < 2:
                        pe.wait_ge(s.diag_ready, 2 * after - 1 + num)
                    if num == 0:
                        if kind == "mid" or kind == "last" or kind == "tail":
                            pe.wait_ge(s.b_loaded, 32)
                    last = nc.tensor.matmul(G[:, bank, 0:HALF], (cb if w else cs)[:],
                                            DG[:, w, 4 * h:4 * h + 4, :].rearrange("p a n -> p (a n)"),
                                            start=True, stop=True)
                elif what == "N":
                    pe.wait_ge(s.tail_pn, after)
                    last = nc.tensor.transpose(G[0:NT, bank, 0:TT], pn[:], k.ident[0:TT, 0:TT])
                last.then_inc(s.filled, 1)

            for i, (_, what, num, e) in enumerate(plan.prologue):
                slot(0, 0, "prologue", i, what, num)

            def keys_ready(b, kind):
                at = plan.find(kind, "K", 2)
                pe.wait_ge(s.emptied_d, plan.number(kind, b, at, D))
                pe.wait_ge(s.emptied_a, plan.number(kind, b, at, A))

            def batch(b, odd, kind):
                if kind == "first":
                    keys_ready(0, "prologue")
                    scores(b, odd, 0, True)
                    scores(b, odd, 1, True)
                for t in range(NT):
                    for i, what, num, e in step_slots(plan, kind, t):
                        second = (what, num) == ("T", 3 * t + 1)
                        if second and t < NT - 2:
                            scores(b, odd, t + 2, False)
                        elif second and kind != "last":
                            if t == NT - 2:
                                keys_ready(b, kind)
                            scores(b + 1, 1 - odd, t + 2 - NT, False)
                        slot(b, odd, kind, i, what, num)

            batches(pe, batch)
            for i, x in enumerate(plan.tail):
                slot(B - 1, 0, "tail", i, x[1], x[2])

        @block.gpsimd
        def _(pool):
            def deviations(pair):
                at = rs[:, 2 * pair:2 * pair + 2, :].rearrange("p b c -> p (b c)")
                nc.gpsimd.tensor_tensor(at, at, k.half_neg[0:CH, 0:24], ALU.pow).then_inc(s.rs_ready, 1)

            pool.wait_ge(s.ve_ready, 1)
            deviations(0)
            pool.wait_ge(s.rs_ready, 1)

            def values(b, u):
                pool.wait_ge(s.ctx_loaded, 16 * b + 16)
                nc.gpsimd.tensor_tensor(V[:, u], RAW[:],
                                        k.ctx_mv[:, bass.ds(b, 1), :, 0:1].rearrange("p a c n -> p (a c) n").to_broadcast([CH, NCH, P]),
                                        ALU.subtract).then_inc(s.pool_chain, 1)
                pool.wait_ge(s.pool_chain, b + 1)
                nc.gpsimd.tensor_tensor(V[:, u], V[:, u],
                                        rs[:, bass.ds(b, 1), :].rearrange("p a c -> p (a c)").unsqueeze(2).to_broadcast([CH, NCH, P]),
                                        ALU.mult).then_inc(s.values_ready, 1)

            def rows(b, u, again):
                if again:
                    pool.wait_ge(s.scores_ready, 8 * b - 8)
                nc.gpsimd.tensor_copy(Qb[:, u], QZ[:, bass.ds(b, 1)].rearrange("p a h q -> p (a h) q")).then_inc(s.q_ready, 1)
                if again:
                    pool.wait_ge(s.null_shift, b - 1)
                nc.gpsimd.tensor_copy(nneg[:, u, :], NN[:, bass.ds(b * NT, NT)]).then_inc(s.nn_ready, 1)
                pool.wait_ge(mask_loaded[u], loads(b, u))
                if again:
                    pool.wait_ge(s.rowmax_ready, 8 * b - 8)
                pool.sem_inc(s.carrier, 1)
                nc.gpsimd.tensor_scalar(MA[:, u, :], MR[:, u, :], -1.0, -FLT_MAX, ALU.add,
                                        ALU.mult).then_inc(s.mask_ready, 1)

            def diagonals(tb, again):
                pool.wait_ge(s.tail_w, tb + 1)
                if again:
                    pool.wait_ge(s.z_done, 2 * tb)
                for w, x in enumerate((rinv, wc)):
                    nc.gpsimd.tensor_tensor(DG[:, w], k.ident[0:TT, 0:TT].unsqueeze(1).to_broadcast([TT, NT, TT]),
                                            x[:].unsqueeze(2).to_broadcast([TT, NT, TT]), ALU.mult).then_inc(s.diag_ready, 1)

            values(0, 0)
            rows(0, 0, False)
            rows(1, 1, False)
            for pair in range(1, B // 2):
                deviations(pair)
            pool.wait_ge(s.rs_ready, B // 2)

            def batch(b, odd, kind):
                if kind != "last":
                    pool.wait_ge(s.filled, plan.before(kind, b))
                    values(b + 1, 1 - odd)
                if kind != "first":
                    diagonals(b - 1, not (isinstance(b, int) and b == 1))
                if kind == "mid":
                    rows(b + 1, 1 - odd, True)

            batches(pool, batch)
            diagonals(15, True)

        @block.scalar
        def _(act):
            def empty(b, odd, kind, i, what, num):
                bank = plan.bank(kind, odd, i)
                nu = 0 if kind == "prologue" else 1 - odd
                act.wait_ge(s.filled, plan.number(kind, b, i))
                if what == "K":
                    ins = nc.scalar.activation(KT[:, nu, num * 500:(num + 1) * 500], G[:, bank, 0:500], ACT.Identity,
                                               bias=k.v("L2_cb"), scale=k.v("L2_cs"))
                elif what == "T":
                    t, j = divmod(num, 3)
                    ins = nc.scalar.copy(PT[:, 4 * j:4 * j + 4, t % 4, :],
                                         G[0:CH, bank, 0:HALF].rearrange("p (a b) -> p a b", a=4))
                ins.then_inc(s.emptied_a, 1)

            for i, (_, what, num, e) in enumerate(plan.prologue):
                if e == A:
                    empty(0, 0, "prologue", i, what, num)

            def exp(b, odd, t, kind):
                act.wait_ge(s.rowmax_ready, 8 * b + t + 1)
                if t >= 2:
                    act.wait_ge(s.filled, plan.number(kind, b, plan.find(kind, "T", 3 * t - 4)))
                elif kind != "first":
                    act.wait_ge(s.filled, plan.before("mid", b) - len(plan.mid) + 1 +
                                plan.find("mid", "T", 3 * t + 20))
                nc.scalar.activation(PR[:, t % 2, :], SM[:, t % 2, :], ACT.Exp,
                                     bias=nmax[:, odd, t:t + 1], scale=-1.0,
                                     accum_out=ssum[:, odd, t:t + 1]).then_inc(s.exp_done, 1)

            def null_exp(tb):
                act.wait_ge(s.null_shift, tb + 1)
                if not (isinstance(tb, int) and tb == 0):
                    act.wait_ge(s.tail_pn, tb)
                nc.scalar.activation(en[:], tot[:], ACT.Exp, scale=-1.0).then_inc(s.null_exp, 1)

            def batch(b, odd, kind):
                if kind == "first":
                    exp(b, odd, 0, kind)
                for t in range(NT):
                    if t == 0 and kind != "first":
                        null_exp(b - 1)
                    if t < NT - 1:
                        exp(b, odd, t + 1, kind)
                    elif kind != "last":
                        exp(b + 1, 1 - odd, 0, "mid")
                    for i, what, num, e in step_slots(plan, kind, t):
                        if e == A:
                            empty(b, odd, kind, i, what, num)

            batches(act, batch)
            null_exp(15)

        @block.vector
        def _(dve):
            nc.vector.tensor_scalar(rs[:], k.ctx_mv[:, :, :, 1], 1e-6, None, ALU.add).then_inc(s.ve_ready, 1)

            def rowmax(b, odd, t, early):
                dve.wait_ge(s.scores_ready, 8 * b + t + 1)
                if t == 0:
                    dve.wait_ge(s.mask_ready, b + 1)
                    dve.wait_ge(s.nn_ready, b + 1)
                if not early:
                    dve.wait_ge(s.exp_done, 8 * b + t - 1)
                dve.sem_inc(s.carrier, 1)
                nc.vector.tensor_tensor_reduce(
                    chunks(SM[:, t % 2, :]), S[0:TT, t % 2, :, 0:500], chunks(MA[:, odd, :]),
                    1.0, nneg[:, odd, t:t + 1], ALU.add, ALU.min, nmax[:, odd, t:t + 1]).then_inc(s.rowmax_ready, 1)

            def tail_start(tb, odd):
                if not (isinstance(tb, int) and tb == 0):
                    dve.wait_ge(s.tail_pn, tb)
                nc.vector.tensor_tensor(tot[:], nneg[:, odd, :], nmax[:, odd, :], ALU.subtract).then_inc(s.null_shift, 1)

            def tail_sums(tb, odd):
                dve.wait_ge(s.null_exp, tb + 1)
                dve.wait_ge(s.exp_done, 8 * tb + 8)
                if not (isinstance(tb, int) and tb == 0):
                    dve.wait_ge(s.diag_ready, 2 * tb)
                nc.vector.tensor_tensor(tot[:], ssum[:, odd, :], en[:], ALU.add).then_inc(s.tail_sums, 1)
                dve.wait_ge(s.tail_sums, tb + 1)
                nc.vector.reciprocal(rinv[:], tot[:]).then_inc(s.tail_r, 1)
                dve.wait_ge(s.tail_r, tb + 1)
                nc.vector.tensor_tensor(wc[:], ssum[:, odd, :], rinv[:], ALU.mult).then_inc(s.tail_w, 1)
                nc.vector.tensor_tensor(pn[:], en[:], rinv[:], ALU.mult).then_inc(s.tail_pn, 1)

            def empty(b, odd, kind, i, what, num):
                bank = plan.bank(kind, odd, i)
                nu = 0 if kind == "prologue" else 1 - odd
                tb = b if kind == "tail" else b - 1
                dve.wait_ge(s.filled, plan.number(kind, b, i))
                if what == "K":
                    ins = nc.vector.tensor_scalar(KT[:, nu, num * 500:(num + 1) * 500], G[:, bank, 0:500],
                                                  k.v("L2_cs"), k.v("L2_cb"), ALU.mult, ALU.add)
                elif what == "T":
                    t, j = divmod(num, 3)
                    ins = nc.vector.tensor_copy(PT[:, 4 * j:4 * j + 4, t % 4, :],
                                                G[0:CH, bank, 0:HALF].rearrange("p (a b) -> p a b", a=4))
                elif what == "O":
                    ins = nc.vector.tensor_copy(OS[:, odd, num, :], G[:, bank, 0:HALF])
                elif what == "R":
                    h, w = divmod(num, 2)
                    if w == 0:
                        ins = nc.vector.tensor_tensor(ZS[:, h, :], OS[:, 1 - odd, h, :], G[:, bank, 0:HALF], ALU.mult)
                    else:
                        dve.wait_ge(s.emptied_d, plan.number(kind, b, i - 1, D))
                        z = QZ[:, bass.ds(tb, 1), 8 * h:8 * h + 8, :].rearrange("p a h q -> p (a h q)")
                        ins = nc.vector.tensor_tensor(z, ZS[:, h, :], G[:, bank, 0:HALF], ALU.add)
                elif what == "N":
                    ins = nc.vector.tensor_copy(PN[:, bass.ds(tb, 1), :].rearrange("p a n -> p (a n)"),
                                                G[0:NT, bank, 0:TT])
                ins.then_inc(s.emptied_d, 1)
                if what == "R" and num in (1, 3):
                    dve.sem_inc(s.z_done, 1)

            for i, (_, what, num, e) in enumerate(plan.prologue):
                if e == D:
                    empty(0, 0, "prologue", i, what, num)

            def batch(b, odd, kind):
                if kind == "first":
                    rowmax(b, odd, 0, True)
                    rowmax(b, odd, 1, True)
                for t in range(NT):
                    if t == 0 and kind != "first":
                        tail_start(b - 1, 1 - odd)
                    if t == 1 and kind != "first":
                        tail_sums(b - 1, 1 - odd)
                    for i, what, num, e in step_slots(plan, kind, t):
                        second = (what, num) == ("T", 3 * t + 1)
                        if second and t < NT - 2:
                            rowmax(b, odd, t + 2, False)
                        elif second and kind != "last":
                            rowmax(b + 1, 1 - odd, t + 2 - NT, False)
                        if e == D:
                            empty(b, odd, kind, i, what, num)

            batches(dve, batch)
            tail_start(15, 1)
            tail_sums(15, 1)
            for i, x in enumerate(plan.tail):
                empty(B - 1, 0, "tail", i, x[1], x[2])


def wide_heads_output(nc, k, src, QZ, WVO, PN, NVO):
    name, H = "L2o", 16
    with ExitStack() as ctx:
        sb = lambda n, shape, dt=F32: ctx.enter_context(nc.sbuf_tensor(name + n, shape, dt))
        ps = ctx.enter_context(nc.psum_tensor(name + "ps", [P, 8, BANK], F32))
        s = semaphores(ctx, nc, name, LN_SEMS + " out_filled out_ready dve_chain")
        OUT = sb("out", [P, TOK])
        block = ctx.enter_context(nc.Block())

        @block.gpsimd
        def _(pool):
            ln_pool(pool, k, s, [1e-6])

        @block.tensor
        def _(pe):
            for x in range(2):
                for h in range(H):
                    nc.tensor.matmul(ps[:, 4 + x, 0:HALF], WVO[:, h, :], QZ[:, 8 * x:8 * x + 8, h, :],
                                     start=h == 0, stop=False)
                for j in range(2):
                    last = nc.tensor.matmul(ps[:, 4 + x, 0:HALF], NVO[:, j * P:(j + 1) * P],
                                            PN[:, 8 * x:8 * x + 8, j * Q:(j + 1) * Q], start=False, stop=j == 1)
                last.then_inc(s.out_filled, 1)
            pe.wait_ge(s.out_ready, 2)
            ln_pe(pe, k, s, ps, stream=OUT)

        @block.vector
        def _(dve):
            link = Chain(dve, s.dve_chain)
            for x in range(2):
                dve.wait_ge(s.out_filled, x + 1)
                nc.vector.tensor_copy(OUT[:, x * HALF:(x + 1) * HALF], ps[:, 4 + x, 0:HALF]).then_inc(s.out_ready, 1)
            ln_dve(dve, k, s, ps, link, [1e-6], k.v("L2_os"), k.v("L2_ob"))
            dve.wait_ge(s.ln_done, 2)
            nc.vector.tensor_tensor(k.xT[:], k.xT[:], k.xnT[:], ALU.add)


def attention_16_wide_heads(nc, k, src):
    with ExitStack() as ctx:
        sb = lambda n, shape, dt=F32: ctx.enter_context(nc.sbuf_tensor("L2x" + n, shape, dt))
        QZ = sb("qz", [P, B, 16, Q])
        WVO = sb("wvo", [P, 16, P])
        NN = sb("nn", [TT, B * NT])
        NVO = sb("nvo", [NT, 2 * P])
        PN = sb("pn", [NT, B, TT])
        wide_heads_setup(nc, k, src, QZ, WVO, NN, NVO)
        wide_heads(nc, k, src, QZ, NN, PN)
        wide_heads_output(nc, k, src, QZ, WVO, PN, NVO)


MAGIC = 1.5 * 2.0 ** 23


def abs_sums(nc, out, w):
    return nc.vector.tensor_reduce(out, w, AX.X, ALU.add, apply_absolute_value=True)


def ternary(nc, link, out, w, inverse_scale):
    link(nc.vector.tensor_scalar(w, w, inverse_scale, MAGIC, ALU.mult, ALU.add))
    link(nc.vector.tensor_scalar(w, w, MAGIC, -1.0, ALU.subtract, ALU.max))
    return nc.vector.tensor_scalar(out, w, 1.0, None, ALU.min)


def bitlinear_ffn(nc, k, src):
    F, NF = 512, 4
    name = "L0f"
    with ExitStack() as ctx:
        sb = lambda n, shape, dt=F32: ctx.enter_context(nc.sbuf_tensor(name + n, shape, dt))
        ps = ctx.enter_context(nc.psum_tensor(name + "ps", [P, 8, BANK], F32))
        s = semaphores(ctx, nc, name, LN_SEMS + " w_loaded b_loaded sums_ready sums_total xq_ready xq_turned xqT_ready "
                       "h_ready pre_ready gelu_done gq_ready gq_turned gqT_ready y_ready y_scaled y_turned "
                       "dve_chain")
        W = sb("w", [P, 2, F])
        Wq = sb("wq", [P, 2, F], BF16)
        b1 = sb("b1", [TT, F])
        wsum = sb("wsum", [P, 2])
        ws = sb("ws", [P, 2])
        rws = sb("rws", [P, 2])
        xs = sb("xs", [TT, 2, NTT])
        rxs = sb("rxs", [TT, 2, NTT])
        so = sb("so", [TT, 2, NTT])
        xqT = sb("xqT", [P, TOK], BF16)
        H = sb("h", [TT, 2, F])
        Gl = sb("gelu", [TT, 2, F])
        GqT = sb("gqT", [P, 2, NF, TT], BF16)
        Y = sb("y", [TT, NTT, P])
        block = ctx.enter_context(nc.Block())

        @block.sync
        def _(sp):
            sp.dma_start(W[:], src["L0_ffn_w"]).then_inc(s.w_loaded, 16)
            sp.dma_start(b1[:], src["L0_ffn_b1"].partition_broadcast(TT)).then_inc(s.b_loaded, 16)

        @block.gpsimd
        def _(pool):
            ln_pool(pool, k, s, [1e-5])

        @block.tensor
        def _(pe):
            ln_pe(pe, k, s, ps, feature_major=False)
            pe.wait_ge(s.sums_ready, 1)
            nc.tensor.matmul(ps[:, 7, 0:2], k.ones[:], wsum[:], start=True, stop=True).then_inc(s.sums_total, 1)
            pe.wait_ge(s.xq_ready, 1)
            for t in range(NTT):
                last = nc.tensor.transpose(ps[:, 2 + t // 4, (t % 4) * TT:(t % 4 + 1) * TT],
                                           k.xn[:, t, :], k.ident[0:TT, 0:TT])
            last.then_inc(s.xq_turned, 1)
            pe.wait_ge(s.xqT_ready, 2)

            def up(t):
                if t >= 2:
                    pe.wait_ge(s.pre_ready, t - 1)
                nc.tensor.matmul(ps[0:TT, 4 + t % 2, :], xqT[:, t * TT:(t + 1) * TT], Wq[:, 0, :],
                                 start=True, stop=True).then_inc(s.h_ready, 1)

            def turn(t):
                pe.wait_ge(s.gq_ready, t + 1)
                if t >= 2:
                    pe.wait_ge(s.gqT_ready, t - 1)
                for c in range(NF):
                    last = nc.tensor.transpose(ps[:, 6 + t % 2, c * TT:(c + 1) * TT],
                                               Gl[:, t % 2, c * P:(c + 1) * P], k.ident[0:TT, 0:TT])
                last.then_inc(s.gq_turned, 1)

            def down(t):
                pe.wait_ge(s.gqT_ready, t + 1)
                for c in range(NF):
                    last = nc.tensor.matmul(ps[0:TT, t // 4, (t % 4) * P:(t % 4 + 1) * P], GqT[:, t % 2, c, :],
                                            Wq[:, 1, c * P:(c + 1) * P], start=c == 0, stop=c == NF - 1)
                last.then_inc(s.y_ready, 1)

            up(0)
            up(1)
            for t in range(NTT):
                turn(t)
                if t + 2 < NTT:
                    up(t + 2)
                down(t)
            pe.wait_ge(s.y_scaled, 2)
            for t in range(NTT):
                last = nc.tensor.transpose(ps[:, 2 + t // 4, (t % 4) * TT:(t % 4 + 1) * TT],
                                           Y[:, t, :], k.ident[0:TT, 0:TT])
            last.then_inc(s.y_turned, 1)

        @block.scalar
        def _(act):
            for t in range(NTT):
                act.wait_ge(s.pre_ready, t + 1)
                if t >= 2:
                    act.wait_ge(s.gq_turned, t - 1)
                nc.scalar.activation(Gl[:, t % 2, :], H[:, t % 2, :], ACT.Gelu).then_inc(s.gelu_done, 1)

        @block.vector
        def _(dve):
            link = Chain(dve, s.dve_chain)
            dve.wait_ge(s.w_loaded, 16)
            abs_sums(nc, wsum[:, 0:1], W[:, 0, :])
            abs_sums(nc, wsum[:, 1:2], W[:, 1, :]).then_inc(s.sums_ready, 1)
            ln_dve(dve, k, s, ps, link, [1e-5], feature_major=False)
            dve.wait_ge(s.ln_norm, 1)
            link(nc.vector.tensor_reduce(xs[:, 0, :], k.xn[:], AX.X, ALU.max, apply_absolute_value=True))
            link(nc.vector.tensor_scalar(xs[:, 0, :], xs[:, 0, :], 1e-5, None, ALU.max))
            link(nc.vector.reciprocal(rxs[:, 0, :], xs[:, 0, :]))
            link(nc.vector.tensor_scalar(rxs[:, 0, :], rxs[:, 0, :], 127.0, None, ALU.mult))
            for t in range(NTT):
                last = nc.vector.tensor_scalar(k.xn[:, t, :], k.xn[:, t, :], rxs[:, 0, t:t + 1], MAGIC,
                                               ALU.mult, ALU.add)
            link(last)
            nc.vector.tensor_scalar(k.xn[:], k.xn[:], MAGIC, -128.0, ALU.subtract, ALU.max).then_inc(s.xq_ready, 1)
            dve.wait_ge(s.sums_total, 1)
            for n in range(2):
                last = nc.vector.tensor_scalar(ws[:, n:n + 1], ps[:, 7, n:n + 1], 1.0 / (F * P), 1e-5,
                                               ALU.mult, ALU.max)
            link(last)
            link(nc.vector.reciprocal(rws[:], ws[:]))
            for n in range(2):
                link(ternary(nc, link, Wq[:, n, :], W[:, n, :], rws[:, n:n + 1]))
            link(nc.vector.tensor_scalar(so[:, 0, :], xs[:, 0, :], ws[0:TT, 0:1], 1.0 / 127, ALU.mult, ALU.mult))
            dve.wait_ge(s.xq_turned, 1)
            for h in range(2):
                nc.vector.tensor_scalar(xqT[:, h * HALF:(h + 1) * HALF], ps[:, 2 + h, 0:HALF], 127.0, None,
                                        ALU.min).then_inc(s.xqT_ready, 1)
            dve.wait_ge(s.b_loaded, 16)

            def pre(t):
                dve.wait_ge(s.h_ready, t + 1)
                if t >= 2:
                    dve.wait_ge(s.gelu_done, t - 1)
                nc.vector.scalar_tensor_tensor(H[:, t % 2, :], ps[0:TT, 4 + t % 2, :], so[:, 0, t:t + 1], b1[:],
                                               ALU.mult, ALU.add).then_inc(s.pre_ready, 1)

            pre(0)
            for t in range(NTT):
                if t + 1 < NTT:
                    pre(t + 1)
                g, u = Gl[:, t % 2, :], slice(t, t + 1)
                dve.wait_ge(s.gelu_done, t + 1)
                link(nc.vector.tensor_reduce(xs[:, 1, u], g, AX.X, ALU.max, apply_absolute_value=True))
                link(nc.vector.tensor_scalar(xs[:, 1, u], xs[:, 1, u], 1e-5, None, ALU.max))
                link(nc.vector.reciprocal(rxs[:, 1, u], xs[:, 1, u]))
                nc.vector.tensor_scalar(so[:, 1, u], xs[:, 1, u], ws[0:TT, 1:2], 1.0 / 127, ALU.mult, ALU.mult)
                link(nc.vector.tensor_scalar(rxs[:, 1, u], rxs[:, 1, u], 127.0, None, ALU.mult))
                link(nc.vector.tensor_scalar(g, g, rxs[:, 1, u], MAGIC, ALU.mult, ALU.add))
                nc.vector.tensor_scalar(g, g, MAGIC, -128.0, ALU.subtract, ALU.max).then_inc(s.gq_ready, 1)
                dve.wait_ge(s.gq_turned, t + 1)
                if t >= 2:
                    dve.wait_ge(s.y_ready, t - 1)
                nc.vector.tensor_scalar(GqT[:, t % 2, :, :].rearrange("p c n -> p (c n)"), ps[:, 6 + t % 2, 0:HALF],
                                        127.0, None, ALU.min).then_inc(s.gqT_ready, 1)
            for h in range(2):
                dve.wait_ge(s.y_ready, 4 * h + 4)
                nc.vector.tensor_tensor(Y[:, 4 * h:4 * h + 4, :],
                                        ps[0:TT, h, :].rearrange("p (t m) -> p t m", t=4),
                                        so[:, 1, 4 * h:4 * h + 4].unsqueeze(2).to_broadcast([TT, 4, P]),
                                        ALU.mult).then_inc(s.y_scaled, 1)
            dve.wait_ge(s.y_turned, 1)
            for h in range(2):
                x = k.xT[:, h * HALF:(h + 1) * HALF]
                nc.vector.scalar_tensor_tensor(x, ps[:, 2 + h, 0:HALF], k.v("L0_b2"), x, ALU.add, ALU.add)


def mixture_ffn(nc, k, src, name, NF, normalise):
    E = 8
    with ExitStack() as ctx:
        sb = lambda n, shape, dt=F32: ctx.enter_context(nc.sbuf_tensor(name + "f" + n, shape, dt))
        ps = ctx.enter_context(nc.psum_tensor(name + "fps", [P, 8, BANK], F32))
        s = semaphores(ctx, nc, name + "f", LN_SEMS + " loaded w_loaded0 w_loaded1 logits_ready shifted exp_done "
                       "gates_ready gates_turned gatesT_ready cleared parts_ready gb_filled gb_act gb_dve b2_filled b2_done h_filled h_act "
                       "h_dve y_filled y_read x_added dve_chain carrier")
        w_loaded = (s.w_loaded0, s.w_loaded1)
        Wg = sb("wg", [P, E])
        bg = sb("bg", [TT, E])
        b2 = sb("b2", [E, P])
        W1 = sb("w1", [P, 2, NF, P])
        W2 = sb("w2", [P, 2, NF, P])
        hT = sb("hT", [P, NF, TOK])
        Gb = sb("gb", [P, E, TOK])
        lg = sb("logits", [TT, NTT, E])
        mx = sb("mx", [TT, NTT])
        sm = sb("sm", [TT, NTT])
        gate = sb("gate", [TT, NTT, E])
        rank = sb("rank", [TT, NTT, E])
        gt = sb("gt", [TT, NTT, E, E])
        eq = sb("eq", [TT, NTT, E, E])
        gT = sb("gT", [E, TOK])
        gr = sb("gates_rest", [E, TOK])
        gP = sb("gate_parts", [72, TOK], BF16)
        sel = sb("select", [72, E], BF16)
        Yg = sb("yg", [P, 2, HALF])
        block = ctx.enter_context(nc.Block())
        tri = k.const[0:TT, C_TRI:C_TRI + 64]
        bank = lambda h, c: (h * NF + c) % 4

        def experts(eng, do):
            do(0, 0)
            do(1, 1)
            with eng.Fori(1, E // 2) as i:
                do(2 * i, 0)
                do(2 * i + 1, 1)

        bcast = lambda ap: ap.unsqueeze(2).to_broadcast([TT, NTT, E])

        @block.sync
        def _(sp):
            sp.dma_start(Wg[:], src[name + "_wg"]).then_inc(s.loaded, 16)
            sp.dma_start(bg[:], src[name + "_bg"].partition_broadcast(TT)).then_inc(s.loaded, 16)
            sp.dma_start(b2[:], src[name + "_b2"]).then_inc(s.loaded, 16)

            def load(e, u):
                sp.dma_start(W1[:, u], src[name + "_w1"][e]).then_inc(w_loaded[u], 16)
                sp.dma_start(W2[:, u], src[name + "_w2"][e]).then_inc(w_loaded[u], 16)

            load(0, 0)
            load(1, 1)
            with sp.Fori(0, E // 2 - 1) as i:
                for u in range(2):
                    sp.wait_ge(s.y_filled, 4 * i + 2 * u + 2)
                    sp.sem_inc(s.carrier, 1)
                    load(2 * i + 2 + u, u)

        @block.gpsimd
        def _(pool):
            ln_pool(pool, k, s, [1e-5])
            pool.wait_ge(s.ln_rstd, 1)
            nc.gpsimd.memset(gP[:], 0.0).then_inc(s.cleared, 1)
            pool.wait_ge(s.cleared, 1)
            nc.gpsimd.tensor_copy(sel[:], k.const[0:72, C_ROW:C_ROW + E]).then_inc(s.cleared, 1)

        @block.tensor
        def _(pe):
            ln_pe(pe, k, s, ps)
            pe.wait_ge(s.ln_done, 2)
            pe.wait_ge(s.loaded, 48)
            for t in range(NTT):
                last = nc.tensor.matmul(ps[0:TT, 6, t * E:(t + 1) * E], k.xnT[:, t * TT:(t + 1) * TT], Wg[:],
                                        start=True, stop=True)
            last.then_inc(s.logits_ready, 1)

            def up(e, u):
                first = isinstance(e, int) and e == 0
                if u == 0 or not first:
                    pe.wait_ge(w_loaded[u], 16 * (e + 2 - u))
                for h in range(2):
                    for c in range(NF):
                        if NF == 4 and h == 1:
                            pe.wait_ge(s.h_act, NF * e + c + 1)
                        elif not first:
                            pe.wait_ge(s.h_dve if NF == 4 or h else s.h_act, NF * e - NF + c + 1)
                        nc.tensor.matmul(ps[:, bank(h, c), 0:HALF], W1[:, u, c, :], k.xnT[:, h * HALF:(h + 1) * HALF],
                                         start=True, stop=True).then_inc(s.h_filled, 1)

            up(0, 0)
            pe.wait_ge(s.gates_ready, 1)
            for t in range(NTT):
                last = nc.tensor.transpose(ps[0:E, 4 + t // 4, (t % 4) * TT:(t % 4 + 1) * TT], gate[:, t, :],
                                           k.ident[0:TT, 0:TT])
            last.then_inc(s.gates_turned, 1)
            pe.wait_ge(s.gatesT_ready, 2)
            for h in range(2):
                nc.tensor.matmul(ps[:, 6 + h, 0:HALF], b2[:], gT[:, h * HALF:(h + 1) * HALF],
                                 start=True, stop=True).then_inc(s.b2_filled, 1)
            pe.wait_ge(s.parts_ready, 1)
            for e in range(E):
                for h in range(2):
                    if e == 1:
                        pe.wait_ge(s.b2_done, 2)
                    if e >= 2:
                        pe.wait_ge(s.gb_dve if h else s.gb_act, e - 1)
                    nc.tensor.matmul(ps[:, (6 if e % 2 else 4) + h, 0:HALF], sel[:, e:e + 1].to_broadcast([72, P]),
                                     gP[:, h * HALF:(h + 1) * HALF], start=True, stop=True).then_inc(s.gb_filled, 1)

            def expert(e, u):
                first = isinstance(e, int) and e == 0
                if not first:
                    up(e, u)
                for h in range(2):
                    pe.wait_ge(s.h_dve if h else s.h_act, NF * e + NF)
                    if first:
                        pe.wait_ge(s.b2_done, 2)
                    else:
                        pe.wait_ge(s.y_read, 2 * e + h - 1)
                    for c in range(NF):
                        last = nc.tensor.matmul(ps[:, 4 + h, 0:HALF], W2[:, u, c, :],
                                                hT[:, c, h * HALF:(h + 1) * HALF], start=c == 0, stop=c == NF - 1)
                    last.then_inc(s.y_filled, 1)

            pe.wait_ge(s.gb_act, E)
            pe.wait_ge(s.gb_dve, E)
            experts(pe, expert)

        @block.scalar
        def _(act):
            act.wait_ge(s.shifted, 1)
            nc.scalar.activation(gate[:], lg[:], ACT.Exp).then_inc(s.exp_done, 1)

            def up(e, u):
                for c in range(NF):
                    act.wait_ge(s.h_filled, 2 * NF * e + c + 1)
                    nc.scalar.activation(hT[:, c, 0:HALF], ps[:, bank(0, c), 0:HALF], ACT.Relu,
                                         bias=k.vec[:, bass.ds(Vectors.at[name + "_b1"] + NF * e + c, 1)]
                                         ).then_inc(s.h_act, 1)

            up(0, 0)
            for e in range(E):
                act.wait_ge(s.gb_filled, 2 * e + 1)
                nc.scalar.copy(Gb[:, e, 0:HALF], ps[:, 6 if e % 2 else 4, 0:HALF]).then_inc(s.gb_act, 1)

            experts(act, lambda e, u: None if isinstance(e, int) and e == 0 else up(e, u))

        @block.vector
        def _(dve):
            link = Chain(dve, s.dve_chain)
            ln_dve(dve, k, s, ps, link, [1e-5])
            dve.wait_ge(s.loaded, 48)
            dve.wait_ge(s.logits_ready, 1)
            link(nc.vector.tensor_tensor(lg[:], ps[0:TT, 6, 0:NTT * E].rearrange("p (t e) -> p t e", e=E),
                                         bg[:].unsqueeze(1).to_broadcast([TT, NTT, E]), ALU.add))
            link(nc.vector.tensor_reduce(mx[:], lg[:], AX.X, ALU.max))
            nc.vector.tensor_tensor(lg[:], lg[:], bcast(mx[:]), ALU.subtract).then_inc(s.shifted, 1)
            dve.wait_ge(s.exp_done, 1)
            link(nc.vector.tensor_reduce(sm[:], gate[:], AX.X, ALU.add))
            link(nc.vector.reciprocal(sm[:], sm[:]))
            link(nc.vector.tensor_tensor(gate[:], gate[:], bcast(sm[:]), ALU.mult))
            for t in range(NTT):
                g_j = gate[:, t, :].unsqueeze(1).to_broadcast([TT, E, E])
                g_e = gate[:, t, :].unsqueeze(2).to_broadcast([TT, E, E])
                nc.vector.tensor_tensor(gt[:, t], g_j, g_e, ALU.is_gt)
                last = nc.vector.tensor_tensor(eq[:, t], g_j, g_e, ALU.is_equal)
            link(last)
            link(nc.vector.tensor_tensor(eq[:].rearrange("p t e j -> p t (e j)"),
                                         eq[:].rearrange("p t e j -> p t (e j)"),
                                         tri.unsqueeze(1).to_broadcast([TT, NTT, E * E]), ALU.mult))
            link(nc.vector.tensor_tensor(gt[:].rearrange("p t e j -> p (t e j)"), gt[:].rearrange("p t e j -> p (t e j)"),
                                         eq[:].rearrange("p t e j -> p (t e j)"), ALU.add))
            link(nc.vector.tensor_reduce(rank[:], gt[:], AX.X, ALU.add))
            last = nc.vector.scalar_tensor_tensor(gate[:].rearrange("p t e -> p (t e)"),
                                                  rank[:].rearrange("p t e -> p (t e)"), 2.0,
                                                  gate[:].rearrange("p t e -> p (t e)"), ALU.is_lt, ALU.mult)
            if normalise:
                link(last)
                link(nc.vector.tensor_reduce(sm[:], gate[:], AX.X, ALU.add))
                link(nc.vector.reciprocal(sm[:], sm[:]))
                last = nc.vector.tensor_tensor(gate[:], gate[:], bcast(sm[:]), ALU.mult)
            last.then_inc(s.gates_ready, 1)
            dve.wait_ge(s.gates_turned, 1)
            for h in range(2):
                nc.vector.tensor_copy(gT[:, h * HALF:(h + 1) * HALF], ps[0:E, 4 + h, 0:HALF]).then_inc(s.gatesT_ready, 1)
            dve.wait_ge(s.gatesT_ready, 2)
            dve.wait_ge(s.cleared, 2)
            link(nc.vector.tensor_copy(gP[0:E, :], gT[:]))
            link(nc.vector.tensor_tensor(gr[:], gT[:], gP[0:E, :], ALU.subtract))
            link(nc.vector.tensor_copy(gP[32:32 + E, :], gr[:]))
            link(nc.vector.tensor_tensor(gr[:], gr[:], gP[32:32 + E, :], ALU.subtract))
            nc.vector.tensor_copy(gP[64:72, :], gr[:]).then_inc(s.parts_ready, 1)

            def up(e, u):
                for c in range(NF):
                    dve.wait_ge(s.h_filled, 2 * NF * e + NF + c + 1)
                    nc.vector.tensor_scalar(hT[:, c, HALF:TOK], ps[:, bank(1, c), 0:HALF],
                                            k.vec[:, bass.ds(Vectors.at[name + "_b1"] + NF * e + c, 1)], 0.0,
                                            ALU.add, ALU.max).then_inc(s.h_dve, 1)

            up(0, 0)
            for h in range(2):
                dve.wait_ge(s.b2_filled, h + 1)
                x = k.xT[:, h * HALF:(h + 1) * HALF]
                nc.vector.tensor_tensor(x, x, ps[:, 6 + h, 0:HALF], ALU.add).then_inc(s.b2_done, 1)
            for e in range(E):
                dve.wait_ge(s.gb_filled, 2 * e + 2)
                nc.vector.tensor_copy(Gb[:, e, HALF:TOK], ps[:, 7 if e % 2 else 5, 0:HALF]).then_inc(s.gb_dve, 1)
            dve.wait_ge(s.gb_act, E)
            dve.wait_ge(s.b2_done, 2)

            def expert(e, u):
                if not (isinstance(e, int) and e == 0):
                    up(e, u)
                for h in range(2):
                    dve.wait_ge(s.y_filled, 2 * e + h + 1)
                    nc.vector.tensor_tensor(Yg[:, h, :], ps[:, 4 + h, 0:HALF], Gb[:, bass.ds(e, 1), h * HALF:(h + 1) * HALF].rearrange("p a n -> p (a n)"),
                                            ALU.mult).then_inc(s.y_read, 1)
                for h in range(2):
                    dve.wait_ge(s.y_read, 2 * e + h + 1)
                    x = k.xT[:, h * HALF:(h + 1) * HALF]
                    nc.vector.tensor_tensor(x, x, Yg[:, h, :], ALU.add).then_inc(s.x_added, 1)
                dve.wait_ge(s.x_added, 2 * e + 2)

            experts(dve, expert)


def ternary_ffn(nc, k, src):
    F, NF = 512, 4
    name = "L3f"
    with ExitStack() as ctx:
        sb = lambda n, shape, dt=F32: ctx.enter_context(nc.sbuf_tensor(name + n, shape, dt))
        ps = ctx.enter_context(nc.psum_tensor(name + "ps", [P, 8, BANK], F32))
        s = semaphores(ctx, nc, name, LN_SEMS + " w_loaded sums_ready sums_total wq_ready h_ready gelu_done var_ready "
                       "rstd_ready norm_ready turned hT_ready y_ready dve_chain")
        W = sb("w", [P, 2, F])
        wsum = sb("wsum", [P, 2])
        rws = sb("rws", [P, 2])
        G = sb("gelu", [TT, NTT, F])
        st = sb("st", [TT, NTT, 6])
        mv = sb("mv2", [TT, NTT, 2])
        rstd = sb("rstd2", [TT, NTT])
        hT = sb("hT", [P, NF, TOK])
        block = ctx.enter_context(nc.Block())

        @block.sync
        def _(sp):
            sp.dma_start(W[:], src["L3_ffn_w"]).then_inc(s.w_loaded, 16)

        @block.gpsimd
        def _(pool):
            ln_pool(pool, k, s, [1e-5])
            for h in range(2):
                pool.wait_ge(s.var_ready, h + 1)
                nc.gpsimd.tensor_tensor(rstd[:, 4 * h:4 * h + 4], mv[:, 4 * h:4 * h + 4, 1], k.half_neg[0:TT, 0:4],
                                        ALU.pow).then_inc(s.rstd_ready, 1)

        @block.tensor
        def _(pe):
            ln_pe(pe, k, s, ps)
            pe.wait_ge(s.sums_ready, 1)
            nc.tensor.matmul(ps[:, 7, 0:2], k.ones[:], wsum[:], start=True, stop=True).then_inc(s.sums_total, 1)
            pe.wait_ge(s.ln_done, 2)
            pe.wait_ge(s.wq_ready, 1)
            for t in range(NTT):
                if t >= 4:
                    pe.wait_ge(s.gelu_done, t - 3)
                nc.tensor.matmul(ps[0:TT, 4 + t % 4, :], k.xnT[:, t * TT:(t + 1) * TT], W[:, 0, :],
                                 start=True, stop=True).then_inc(s.h_ready, 1)
            for h in range(2):
                pe.wait_ge(s.norm_ready, h + 1)
                for c in range(NF):
                    n = h * NF + c
                    if n >= 2:
                        pe.wait_ge(s.hT_ready, n - 1)
                    for t in range(4):
                        last = nc.tensor.transpose(ps[:, n % 2, t * TT:(t + 1) * TT],
                                                   G[:, 4 * h + t, c * P:(c + 1) * P], k.ident[0:TT, 0:TT])
                    last.then_inc(s.turned, 1)
            for h in range(2):
                pe.wait_ge(s.hT_ready, NF * (h + 1))
                for c in range(NF):
                    last = nc.tensor.matmul(ps[:, 2 + h, 0:HALF], W[:, 1, c * P:(c + 1) * P],
                                            hT[:, c, h * HALF:(h + 1) * HALF], start=c == 0, stop=c == NF - 1)
                last.then_inc(s.y_ready, 1)

        @block.scalar
        def _(act):
            for t in range(NTT):
                act.wait_ge(s.h_ready, t + 1)
                nc.scalar.activation(G[:, t, :], ps[0:TT, 4 + t % 4, :], ACT.Gelu).then_inc(s.gelu_done, 1)

        @block.vector
        def _(dve):
            link = Chain(dve, s.dve_chain)
            dve.wait_ge(s.w_loaded, 16)
            abs_sums(nc, wsum[:, 0:1], W[:, 0, :])
            abs_sums(nc, wsum[:, 1:2], W[:, 1, :]).then_inc(s.sums_ready, 1)
            ln_dve(dve, k, s, ps, link, [1e-5])
            dve.wait_ge(s.sums_total, 1)
            link(nc.vector.tensor_scalar(rws[:], ps[:, 7, 0:2], 1.0 / (F * P), 1e-6, ALU.mult, ALU.add))
            link(nc.vector.reciprocal(rws[:], rws[:]))
            for n in range(2):
                last = ternary(nc, link, W[:, n, :], W[:, n, :], rws[:, n:n + 1])
            last.then_inc(s.wq_ready, 1)
            for h in range(2):
                for t in range(4 * h, 4 * h + 4):
                    dve.wait_ge(s.gelu_done, t + 1)
                    last = nc.vector.bn_stats(st[:, t, :], G[:, t, :])
                link(last)
                for t in range(4 * h, 4 * h + 4):
                    last = nc.vector.bn_aggr(mv[:, t, :], st[:, t, :])
                link(last)
                nc.vector.tensor_scalar(mv[:, 4 * h:4 * h + 4, 1], mv[:, 4 * h:4 * h + 4, 1], 1e-5, None,
                                        ALU.add).then_inc(s.var_ready, 1)
            for h in range(2):
                dve.wait_ge(s.rstd_ready, h + 1)
                for t in range(4 * h, 4 * h + 4):
                    last = nc.vector.tensor_scalar(G[:, t, :], G[:, t, :], mv[:, t, 0:1], rstd[:, t:t + 1],
                                                   ALU.subtract, ALU.mult)
                last.then_inc(s.norm_ready, 1)
            for h in range(2):
                for c in range(NF):
                    n = h * NF + c
                    dve.wait_ge(s.turned, n + 1)
                    nc.vector.tensor_scalar(hT[:, c, h * HALF:(h + 1) * HALF], ps[:, n % 2, 0:HALF],
                                            k.v("L3_lnw", c), k.v("L3_lnb", c), ALU.mult,
                                            ALU.add).then_inc(s.hT_ready, 1)
            for h in range(2):
                dve.wait_ge(s.y_ready, h + 1)
                x = k.xT[:, h * HALF:(h + 1) * HALF]
                nc.vector.tensor_tensor(x, x, ps[:, 2 + h, 0:HALF], ALU.add)



def load(nc, k, src):
    with ExitStack() as ctx:
        loaded = ctx.enter_context(nc.semaphore("loaded"))
        block = ctx.enter_context(nc.Block())

        @block.sync
        def _(sp):
            sp.dma_start(k.xT[:], src["xT"]).then_inc(loaded, 16)
            sp.dma_start(k.const[:], src["const"]).then_inc(loaded, 16)
            sp.dma_start(k.vec[:], src["vec"]).then_inc(loaded, 16)
            sp.wait_ge(loaded, 48)

        @block.gpsimd
        def _(pool):
            nc.gpsimd.memset(k.half_neg[:], -0.5)
            nc.gpsimd.memset(k.ones[:], 1.0)


def store(nc, k, out):
    with ExitStack() as ctx:
        stored = ctx.enter_context(nc.semaphore("stored"))
        block = ctx.enter_context(nc.Block())

        @block.sync
        def _(sp):
            sp.dma_start(out, k.xT[:]).then_inc(stored, 16)
            sp.wait_ge(stored, 16)


def build(nc, src, out, stages):
    with ExitStack() as ctx:
        k = Core(ctx, nc)
        load(nc, k, src)
        for name in stages:
            STAGE[name](nc, k, src)
        store(nc, k, out)


STAGE = {
    "L2a": attention_16_wide_heads,
    "L1a": latent_attention,
    "L0f": bitlinear_ffn,
    "L1f": lambda nc, k, src: mixture_ffn(nc, k, src, "L1", 4, False),
    "L2f": lambda nc, k, src: mixture_ffn(nc, k, src, "L2", 2, True),
    "L3f": ternary_ffn,
    "L0a": lambda nc, k, src: attention_16_small_heads(nc, k, "L0", src, 8 ** -0.5, True),
    "L3a": lambda nc, k, src: attention_16_small_heads(nc, k, "L3", src, P ** -0.5, False),
}
STAGES = ["L0a", "L0f", "L1a", "L1f", "L2a", "L2f", "L3a", "L3f"]


def constant_columns(np):
    c = np.zeros((P, N_CONST), np.float32)
    p = np.arange(P)
    c[:, C_ID:C_ID + P] = np.eye(P)
    c[:, C_HEAD:C_HEAD + 16] = p[:, None] // 8 == np.arange(16)
    c[:, C_PAIR:C_PAIR + 2] = (p[:, None] % 32) // 8 == np.arange(2)
    c[:TT, C_QSEL:C_QSEL + Q] = p[:TT, None] % Q == np.arange(Q)
    c[:TT, C_J32:C_J32 + 32] = p[:TT, None] // Q == np.arange(32) // 8
    c[:TT, C_J2:C_J2 + 2] = p[:TT, None] // Q == np.arange(2)
    c[:, C_TRI:C_TRI + 64] = (np.arange(8)[None, :] < np.arange(8)[:, None]).reshape(1, 64)
    c[:, C_ROW:C_ROW + 8] = p[:, None] % 32 == np.arange(8)
    c[:, C_HALF:C_HALF + 2] = p[:, None] // 64 == np.arange(2)
    return c


def lay_out(i, np):
    f = {n: np.asarray(a) for n, a in i.items()}
    keys = np.arange(S2).reshape(CH, NCH).T.reshape(-1)
    a = {"xT": f["x"].reshape(TOK, P).T,
         "ctx": f["ctx_1024"].reshape(B, CH, NCH, P),
         "ctxT": f["ctx_1024"].transpose(0, 2, 1)[:, :, keys],
         "mask_full": f["mask_BxS2_bf1"][:, keys],
         "mask_some": f["mask_BxS2_bk0"][:, keys],
         "const": constant_columns(np)}

    def padded(w):
        o = np.zeros(w.shape[:-1] + (2, 4, 32), np.float32)
        o[..., :16] = w.reshape(w.shape[:-1] + (2, 4, 16))
        return o.reshape(w.shape[:-1] + (2, P))

    feature_first = lambda w: w.reshape(w.shape[:-1] + (8, 16)).swapaxes(-1, -2).reshape(w.shape)

    for n in ("L0", "L3"):
        wq, wk, wv, wo = (f[n + "_xattn_W" + x] for x in "qkvo")
        a[n + "_attn_w"] = np.stack([feature_first(wq.T), feature_first(wk.T), *padded(wv.T).transpose(1, 0, 2),
                                     *padded(wo).transpose(1, 2, 0)], 1)
    heads_first = lambda w: w.reshape(P, 16, 64).transpose(2, 1, 0)
    wkv = f["L2_xattn_Wkv"]
    a["L2_attn_w"] = np.stack([heads_first(f["L2_xattn_Wq"]), heads_first(wkv[:, :1024]), heads_first(wkv[:, 1024:]),
                               f["L2_xattn_Wo"].reshape(16, 64, P).transpose(1, 0, 2)], 1)
    a["L2_null"] = f["L2_xattn_null_kv"].T
    a["L2_cs_row"], a["L2_cb_row"] = f["L2_xattn_lnc_s"], f["L2_xattn_lnc_b"]
    wkv = f["L1_xattn_W_kv"]
    a["L1_attn_w"] = np.stack([f["L1_xattn_W_q"], wkv[:, :P], wkv[:, P:], f["L1_xattn_W_out"]], 1)

    def chunked(w):
        w = w.reshape(w.shape[:-2] + (w.shape[-2] // P, P, w.shape[-1]))
        return np.moveaxis(w, -3, -2)

    for n, up, down in (("L0_ffn_w", "L0_ffn_W1", "L0_ffn_W2"), ("L3_ffn_w", "L3_ffn_W_fc", "L3_ffn_W_proj")):
        a[n] = np.stack([f[up].T, chunked(f[down].T).reshape(P, 512)], 1)
    a["L0_ffn_b1"] = f["L0_ffn_b1"]
    for n, wg, bg, w1, w2, b2 in (("L1", "Wg", "bg", "W1", "W2", "b2"),
                                  ("L2", "router_w", "router_b", "w1", "w2", "b2")):
        a[n + "_wg"], a[n + "_bg"], a[n + "_b2"] = (f[n + "_ffn_" + x] for x in (wg, bg, b2))
        w = f[n + "_ffn_" + w1]
        a[n + "_w1"] = w.reshape(8, P, -1, P)
        a[n + "_w2"] = chunked(f[n + "_ffn_" + w2])

    bv = padded(f["L0_xattn_bv"])
    cols = {"L0_bq": feature_first(f["L0_xattn_bq"]), "L0_bk": feature_first(f["L0_xattn_bk"]), "L0_bo": f["L0_xattn_bo"],
            "L0_bv0": bv[0], "L0_bv1": bv[1], "L0_b2": f["L0_ffn_b2"],
            "L1_xg": f["L1_xattn_ln_x_g"], "L1_xb": f["L1_xattn_ln_x_b"], "L1_lg": f["L1_xattn_ln_l_g"],
            "L1_lb": f["L1_xattn_ln_l_b"], "L1_qg": np.tile(f["L1_xattn_q_gamma"], 2),
            "L1_kg": np.tile(f["L1_xattn_k_gamma"], 2), "L1_bout": f["L1_xattn_b_out"],
            "L2_1s": f["L2_xattn_ln1_s"], "L2_1b": f["L2_xattn_ln1_b"], "L2_cs": f["L2_xattn_lnc_s"],
            "L2_cb": f["L2_xattn_lnc_b"], "L2_os": f["L2_xattn_lno_s"], "L2_ob": f["L2_xattn_lno_b"],
            "L3_bo": f["L3_xattn_bo"], "L3_lnw": f["L3_ffn_ln_w"], "L3_lnb": f["L3_ffn_ln_b"],
            "L1_b1": f["L1_ffn_b1"], "L2_b1": f["L2_ffn_b1"]}
    v = np.zeros((P, Vectors.total), np.float32)
    for n in Vectors.names:
        w = Vectors.width.get(n, 1)
        v[:, Vectors.at[n]:Vectors.at[n] + w] = np.asarray(cols[n]).reshape(w, P).T
    a["vec"] = v
    return {n: np.ascontiguousarray(x) for n, x in a.items()}


def kernel(**inputs):
    import numpy as _np
    import concourse.bacc as _bacc
    from concourse import mybir as _mybir
    from concourse.bass_utils import run_bass_kernel_spmd as _run

    nc = _bacc.Bacc("TRN2", target_bir_lowering=False, num_devices=1)
    arrays, src = {}, {}
    for name, a in lay_out(inputs, _np).items():
        arrays["in_" + name] = a
        src[name] = nc.dram_tensor("in_" + name, a.shape, _mybir.dt.from_np(a.dtype), kind="ExternalInput").ap()
    out = nc.dram_tensor("outT", (P, TOK), F32, kind="ExternalOutput").ap()
    build(nc, src, out, STAGES)
    r = _run(nc, [arrays], core_ids=[0])
    return _np.ascontiguousarray(r.results[0]["outT"].T).reshape(B, Q, P)
```
